# Optimizing a Trainium2 kernel written in Bass

```python
import numpy as np
import jax
import jax.numpy as jnp

def _softmax(x, axis=-1):
    return jax.nn.softmax(x, axis=axis)

def _gelu(x):
    return jax.nn.gelu(x, approximate=True)

def _silu(x):
    return jax.nn.silu(x)

def _sigmoid(x):
    return jax.nn.sigmoid(x)

def _layernorm(x, axis=-1, eps=1e-05):
    m = jnp.mean(x, axis=axis, keepdims=True)
    v = jnp.var(x, axis=axis, keepdims=True)
    return (x - m) / jnp.sqrt(v + eps)

def _scatter_add(tgt, idx, src, axis=0):
    return tgt.at[idx].add(src)

def _segment_sum(src, seg, n):
    return jax.ops.segment_sum(src, seg, n)
kernel_name = 'mk_adj_resnorm_d4_adj_r2_83c81e'

def setup_inputs(seed: int=0):
    np.random.seed(seed)
    _w = jnp.asarray

    def _rec_inputs():
        import jax
        import jax.numpy as jnp
        _gk = jax.random.key(seed)
        x = -0.0005207 + 1.001 * jax.random.normal(jax.random.fold_in(_gk, 1), (4096, 128), jnp.float32)
        _a = jax.random.bernoulli(jax.random.fold_in(_gk, 2), 0.00390625, (4096, 4096))
        _a = jnp.logical_or(_a, jnp.swapaxes(_a, -1, -2))
        _af = _a.astype(jnp.float32)
        adj = _af
        return (x, adj)
    x, adj = _rec_inputs()

    def _L0_gnn_setup():
        import jax, jax.numpy as jnp
        import numpy as np
        N = 4096
        IN = 128
        OUT = 128
        EDGE_P = 0.004
        key = jax.random.key(seed)
        k1, k2, k3, k4 = jax.random.split(key, 4)
        node_feats = jax.random.normal(k1, (N, IN), dtype=jnp.float32)
        a = (jax.random.uniform(k2, (N, N)) < EDGE_P).astype(jnp.float32)
        adj_matrix = jnp.maximum(a, a.T)
        W = jax.random.normal(k3, (OUT, IN), dtype=jnp.float32) / np.float32(np.sqrt(IN))
        b = jax.random.normal(k4, (OUT,), dtype=jnp.float32) * 0.01
        return {'node_feats': node_feats, 'adj_matrix': adj_matrix, 'W': W, 'b': b}
    _L0_gnn_all = _L0_gnn_setup()
    _L0_gnn_in = {k: v for k, v in _L0_gnn_all.items() if k in ('W', 'b')}
    del _L0_gnn_all

    def _L1_gnn_setup():
        import jax, jax.numpy as jnp
        import numpy as np
        N = 4096
        D = 128
        DENSITY = 0.02
        key = jax.random.key(seed)
        k1, k2, k3, k4 = jax.random.split(key, 4)
        inputs = jax.random.normal(k1, (N, D), dtype=jnp.float32)
        vals = jax.random.uniform(k2, (N, N), dtype=jnp.float32, minval=0.1, maxval=1.0)
        mask = jax.random.uniform(k3, (N, N), dtype=jnp.float32) < DENSITY
        adj = jnp.where(mask, vals, 0.0)
        H_v = 0.1 * jax.random.normal(k4, (D, 1), dtype=jnp.float32)
        return {'inputs': inputs, 'adj': adj, 'H_v': H_v}
    _L1_gnn_all = _L1_gnn_setup()
    _L1_gnn_in = {k: v for k, v in _L1_gnn_all.items() if k in ('H_v',)}
    del _L1_gnn_all

    def _L2_gnn_setup():
        import jax, jax.numpy as jnp
        import numpy as np
        N = 4096
        D = 128
        CUTOFF = 1.0
        MU = 1.0
        SIGMA = 0.5

        def sensitivity(r, mu, sigma):
            return jnp.exp(-(1.0 / r - 1.0 / mu) ** 2 / (2.0 * sigma * sigma))
        key = jax.random.key(seed)
        k_z, k_d, k_w = jax.random.split(key, 3)
        z = jax.random.normal(k_z, (N, D), dtype=jnp.float32)
        dist_matrix = jax.random.uniform(k_d, (N, N), dtype=jnp.float32) * 2.0 + 0.05
        W = jax.random.normal(k_w, (D, D), dtype=jnp.float32)
        B = jnp.zeros((D,), dtype=jnp.float32)
        return {'z': z, 'dist_matrix': dist_matrix, 'W': W, 'B': B}
    _L2_gnn_all = _L2_gnn_setup()
    _L2_gnn_in = {k: v for k, v in _L2_gnn_all.items() if k in ('W', 'B')}
    del _L2_gnn_all

    def _L3_gnn_setup():
        import jax, jax.numpy as jnp
        import numpy as np
        from jax import lax
        D_MODEL = 128
        D_STATE = 16
        D_CONV = 4
        EXPAND = 2
        D_INNER = EXPAND * D_MODEL
        DT_RANK = (D_MODEL + 15) // 16
        N = 2048
        EPS = 1e-05

        def _mamba(h, w_in, conv_w, conv_b, w_xp, w_dt, b_dt, A_log, D_skip, w_out):
            L = h.shape[0]
            xz = h @ w_in
            xc, z = (xz[:, :D_INNER], xz[:, D_INNER:])
            xpad = jnp.pad(xc, ((D_CONV - 1, 0), (0, 0)))
            xconv = sum((xpad[k:k + L] * conv_w[:, k] for k in range(D_CONV))) + conv_b
            u = jax.nn.silu(xconv)
            dbc = u @ w_xp
            dt = jax.nn.softplus(dbc[:, :DT_RANK] @ w_dt + b_dt)
            B = dbc[:, DT_RANK:DT_RANK + D_STATE]
            C = dbc[:, DT_RANK + D_STATE:]
            A = -jnp.exp(A_log)
            dA = jnp.exp(dt[:, :, None] * A[None])
            dBu = dt[:, :, None] * B[:, None, :] * u[:, :, None]

            def step(hst, inp):
                dAt, dBut, Ct = inp
                hst = dAt * hst + dBut
                return (hst, hst @ Ct)
            _, ys = lax.scan(step, jnp.zeros((D_INNER, D_STATE), h.dtype), (dA, dBu, C))
            y = ys + u * D_skip
            y = y * jax.nn.silu(z)
            return y @ w_out
        key = jax.random.key(seed)
        ks = jax.random.split(key, 16)
        x = jax.random.normal(ks[0], (N, D_MODEL), dtype=jnp.float32)
        a = jax.random.uniform(ks[1], (N, N), dtype=jnp.float32)
        adj = a / a.sum(axis=1, keepdims=True)
        s = lambda fi, fo: 1.0 / np.sqrt(fi)
        gcn_w = jax.random.uniform(ks[2], (D_MODEL, D_MODEL), jnp.float32, -s(D_MODEL, 0), s(D_MODEL, 0))
        gcn_b = jnp.zeros((D_MODEL,), jnp.float32)
        ln_g = jnp.ones((D_MODEL,), jnp.float32)
        ln_b = jnp.zeros((D_MODEL,), jnp.float32)
        w_in = jax.random.normal(ks[3], (D_MODEL, 2 * D_INNER), jnp.float32) * s(D_MODEL, 0)
        conv_w = jax.random.normal(ks[4], (D_INNER, D_CONV), jnp.float32) * s(D_CONV, 0)
        conv_b = jnp.zeros((D_INNER,), jnp.float32)
        w_xp = jax.random.normal(ks[5], (D_INNER, DT_RANK + 2 * D_STATE), jnp.float32) * s(D_INNER, 0)
        w_dt = jax.random.normal(ks[6], (DT_RANK, D_INNER), jnp.float32) * s(DT_RANK, 0)
        b_dt = jnp.log(jnp.expm1(jnp.exp(jax.random.uniform(ks[7], (D_INNER,), jnp.float32, np.log(0.001), np.log(0.1)))))
        A_log = jnp.log(jnp.broadcast_to(jnp.arange(1, D_STATE + 1, dtype=jnp.float32), (D_INNER, D_STATE)))
        D_skip = jnp.ones((D_INNER,), jnp.float32)
        w_out = jax.random.normal(ks[8], (D_INNER, D_MODEL), jnp.float32) * s(D_INNER, 0)
        return dict(x=x, adj=adj, gcn_w=gcn_w, gcn_b=gcn_b, ln_g=ln_g, ln_b=ln_b, w_in=w_in, conv_w=conv_w, conv_b=conv_b, w_xp=w_xp, w_dt=w_dt, b_dt=b_dt, A_log=A_log, D_skip=D_skip, w_out=w_out)
    _L3_gnn_all = _L3_gnn_setup()
    _L3_gnn_in = {k: v for k, v in _L3_gnn_all.items() if k in ('gcn_w', 'gcn_b', 'ln_g', 'ln_b', 'w_in', 'conv_w', 'conv_b', 'w_xp', 'w_dt', 'b_dt', 'A_log', 'D_skip', 'w_out')}
    del _L3_gnn_all
    return {'x': x, 'adj': adj, 'L0_gnn_W': _L0_gnn_in['W'], 'L0_gnn_b': _L0_gnn_in['b'], 'L1_gnn_H_v': _L1_gnn_in['H_v'], 'L2_gnn_W': _L2_gnn_in['W'], 'L2_gnn_B': _L2_gnn_in['B'], 'L3_gnn_gcn_w': _L3_gnn_in['gcn_w'], 'L3_gnn_gcn_b': _L3_gnn_in['gcn_b'], 'L3_gnn_ln_g': _L3_gnn_in['ln_g'], 'L3_gnn_ln_b': _L3_gnn_in['ln_b'], 'L3_gnn_w_in': _L3_gnn_in['w_in'], 'L3_gnn_conv_w': _L3_gnn_in['conv_w'], 'L3_gnn_conv_b': _L3_gnn_in['conv_b'], 'L3_gnn_w_xp': _L3_gnn_in['w_xp'], 'L3_gnn_w_dt': _L3_gnn_in['w_dt'], 'L3_gnn_b_dt': _L3_gnn_in['b_dt'], 'L3_gnn_A_log': _L3_gnn_in['A_log'], 'L3_gnn_D_skip': _L3_gnn_in['D_skip'], 'L3_gnn_w_out': _L3_gnn_in['w_out']}

def reference(x, adj, L0_gnn_W, L0_gnn_b, L1_gnn_H_v, L2_gnn_W, L2_gnn_B, L3_gnn_gcn_w, L3_gnn_gcn_b, L3_gnn_ln_g, L3_gnn_ln_b, L3_gnn_w_in, L3_gnn_conv_w, L3_gnn_conv_b, L3_gnn_w_xp, L3_gnn_w_dt, L3_gnn_b_dt, L3_gnn_A_log, L3_gnn_D_skip, L3_gnn_w_out):
    import jax
    import jax.numpy as jnp

    def _L0_gnn_ref(node_feats, adj_matrix, W, b):
        import jax, jax.numpy as jnp
        import numpy as np
        N = 4096
        IN = 128
        OUT = 128
        EDGE_P = 0.004
        n = adj_matrix.shape[0]
        adj = adj_matrix + jnp.eye(n, dtype=adj_matrix.dtype)
        deg = jnp.sum(adj, axis=1)
        dinv = jnp.where(deg > 0, deg ** (-0.5), 0.0)
        adj_norm = dinv[:, None] * adj * dinv[None, :]
        x = node_feats @ W.T + b
        mean = jnp.mean(x, axis=0, keepdims=True)
        std = jnp.std(x, axis=0, ddof=1, keepdims=True)
        x = (x - mean) / (std + 1e-06)
        return adj_norm @ x

    def _L1_gnn_ref(inputs, adj, H_v):
        import jax, jax.numpy as jnp
        import numpy as np
        N = 4096
        D = 128
        DENSITY = 0.02
        scores = jnp.squeeze(inputs @ H_v, -1)
        mask = adj != 0.0
        logits = adj * scores[None, :]
        neg = jnp.asarray(jnp.finfo(logits.dtype).min, logits.dtype)
        logits = jnp.where(mask, logits, neg)
        m = jnp.max(logits, axis=1, keepdims=True)
        e = jnp.where(mask, jnp.exp(logits - m), 0.0)
        s = jnp.sum(e, axis=1, keepdims=True)
        weights = e / jnp.where(s > 0, s, 1.0)
        return weights @ inputs

    def _L2_gnn_ref(z, dist_matrix, W, B):
        import jax, jax.numpy as jnp
        import numpy as np
        N = 4096
        D = 128
        CUTOFF = 1.0
        MU = 1.0
        SIGMA = 0.5

        def sensitivity(r, mu, sigma):
            return jnp.exp(-(1.0 / r - 1.0 / mu) ** 2 / (2.0 * sigma * sigma))
        msg = z @ W + B
        sens = sensitivity(dist_matrix, MU, SIGMA)
        weights = jnp.where(dist_matrix < CUTOFF, sens, 0.0)
        return weights @ msg

    def _L3_gnn_ref(x, adj, gcn_w, gcn_b, ln_g, ln_b, w_in, conv_w, conv_b, w_xp, w_dt, b_dt, A_log, D_skip, w_out):
        import jax, jax.numpy as jnp
        import numpy as np
        from jax import lax
        D_MODEL = 128
        D_STATE = 16
        D_CONV = 4
        EXPAND = 2
        D_INNER = EXPAND * D_MODEL
        DT_RANK = (D_MODEL + 15) // 16
        N = 2048
        EPS = 1e-05

        def _mamba(h, w_in, conv_w, conv_b, w_xp, w_dt, b_dt, A_log, D_skip, w_out):
            L = h.shape[0]
            xz = h @ w_in
            xc, z = (xz[:, :D_INNER], xz[:, D_INNER:])
            xpad = jnp.pad(xc, ((D_CONV - 1, 0), (0, 0)))
            xconv = sum((xpad[k:k + L] * conv_w[:, k] for k in range(D_CONV))) + conv_b
            u = jax.nn.silu(xconv)
            dbc = u @ w_xp
            dt = jax.nn.softplus(dbc[:, :DT_RANK] @ w_dt + b_dt)
            B = dbc[:, DT_RANK:DT_RANK + D_STATE]
            C = dbc[:, DT_RANK + D_STATE:]
            A = -jnp.exp(A_log)
            dA = jnp.exp(dt[:, :, None] * A[None])
            dBu = dt[:, :, None] * B[:, None, :] * u[:, :, None]

            def step(hst, inp):
                dAt, dBut, Ct = inp
                hst = dAt * hst + dBut
                return (hst, hst @ Ct)
            _, ys = lax.scan(step, jnp.zeros((D_INNER, D_STATE), h.dtype), (dA, dBu, C))
            y = ys + u * D_skip
            y = y * jax.nn.silu(z)
            return y @ w_out
        h = jax.nn.relu(adj @ x @ gcn_w + gcn_b)
        mu = h.mean(-1, keepdims=True)
        var = h.var(-1, keepdims=True)
        h = (h - mu) * lax.rsqrt(var + EPS) * ln_g + ln_b
        return _mamba(h, w_in, conv_w, conv_b, w_xp, w_dt, b_dt, A_log, D_skip, w_out)
    x = _layernorm(x + _L0_gnn_ref(x, adj, L0_gnn_W, L0_gnn_b), axis=-1)
    x = _layernorm(x + _L1_gnn_ref(x, adj, L1_gnn_H_v), axis=-1)
    x = _layernorm(x + _L2_gnn_ref(x, adj, L2_gnn_W, L2_gnn_B), axis=-1)
    x = _layernorm(x + _L3_gnn_ref(x, adj, L3_gnn_gcn_w, L3_gnn_gcn_b, L3_gnn_ln_g, L3_gnn_ln_b, L3_gnn_w_in, L3_gnn_conv_w, L3_gnn_conv_b, L3_gnn_w_xp, L3_gnn_w_dt, L3_gnn_b_dt, L3_gnn_A_log, L3_gnn_D_skip, L3_gnn_w_out), axis=-1)
    return x

_drawn_inputs = setup_inputs


def setup_inputs(seed=0):
    import zlib

    import numpy as np

    out = dict(_drawn_inputs(seed))
    spreads = {'L2_gnn_B': (0.0, 0.1),
     'L3_gnn_gcn_b': (0.0, 0.34),
     'L3_gnn_ln_g': (1.0, 0.2),
     'L3_gnn_ln_b': (0.0, 0.1),
     'L3_gnn_conv_b': (0.0, 0.1),
     'L3_gnn_D_skip': (1.0, 0.2)}
    factors = {'L0_gnn_b': 8.0}
    for name, (base, spread) in spreads.items():
        noise = np.random.default_rng([zlib.crc32(name.encode()), seed]).standard_normal(out[name].shape)
        drawn = base * np.exp(spread * noise) if base else spread * noise
        out[name] = jnp.asarray(drawn.astype(out[name].dtype))
    for name, factor in factors.items():
        out[name] = (out[name] * factor).astype(out[name].dtype)
    return out
```

```python
from contextlib import ExitStack

import concourse.bass as bass
from concourse import mybir

ALU = mybir.AluOpType
ACT = mybir.ActivationFunctionType
AX_X = mybir.AxisListType.X
F32 = mybir.dt.float32
BF16 = mybir.dt.bfloat16

P = 128
N = 4096
D = 128
T = N // P
CH = 512
NC = N // CH
DI = 2 * D
NH = DI // P
S = 16
R = 8
K = 4
EPS = 1e-5
FMAX = 3.4028234663852886e38
AT_SLOTS = 4


class Chain:

    def __init__(self, eng, sem):
        self.eng, self.sem, self.base, self.n, self.total = eng, sem, 0, 0, 0

    def __call__(self, ins):
        ins.then_inc(self.sem, 1)
        self.n += 1
        self.eng.wait_ge(self.sem, self.base + self.n)

    def enter(self, i, per_turn):
        self.total += self.n
        self.n, self.per_turn = 0, per_turn
        self.base = i * per_turn + self.total

    def leave(self, turns):
        assert self.n == self.per_turn, (self.n, self.per_turn)
        self.total += turns * self.n
        self.base, self.n = self.total, 0


def build(nc, x, adj, W0, b0, Hv, W2, B2, gcn_w, gcn_b, ln_g, ln_b, w_in, conv_w, conv_b, w_xp,
          w_dt, b_dt, A_log, D_skip, w_out, out):
    with ExitStack() as ctx:
        def sb(name, shape, dt=F32):
            return ctx.enter_context(nc.sbuf_tensor(name, shape, dt))

        def sem(name):
            return ctx.enter_context(nc.semaphore(name))

        bank = [ctx.enter_context(nc.psum_tensor(f"bank{i}", [P, CH], F32)) for i in range(8)]

        xs = sb("xs", [P, T, D])
        xT = sb("xT", [P, N])
        zs = sb("zs", [P, T, D])
        ys = sb("ys", [P, T, D])
        ident = sb("ident", [P, P])
        w0T = sb("w0T", [P, P])
        w0n = sb("w0n", [P, P])
        b0c = sb("b0c", [P, 1])
        hvc = sb("hvc", [P, 1])
        hv_rep = sb("hv_rep", [P, P])
        w2 = sb("w2", [P, P])
        b2bc = sb("b2bc", [P, P])
        neg_half = sb("neg_half", [P, T])
        half = sb("half", [P, 1])
        deg = sb("deg", [P, T])
        dinv = sb("dinv", [P, T])
        den = sb("den", [P, T])
        st_a = sb("st_a", [P, T])
        st_b = sb("st_b", [P, T])
        bn = sb("bn", [P, NC, 6])
        mv = sb("mv", [P, 2])
        cs = sb("cs", [P, 4])
        nmax = sb("nmax", [P, 2])
        den1 = sb("den1", [P, 1])

        gw = sb("gw", [P, P])
        gbbc = sb("gbbc", [P, P])
        lng = sb("lng", [P, 1])
        lnb = sb("lnb", [P, 1])
        win = sb("win", [P, 2 * DI])
        cw = sb("cw", [P, NH, K])
        cb = sb("cb", [P, NH])
        wxp = sb("wxp", [P, NH, R + 2 * S])
        wxp3 = sb("wxp3", [P, NH, 3, 2 * S])
        wdt = sb("wdt", [R, DI])
        bdt = sb("bdt", [P, NH])
        alog = sb("alog", [P, NH, S])
        Aneg = sb("Aneg", [P, NH, S])
        dsk = sb("dsk", [P, NH])
        wout = sb("wout", [P, NH, D])
        sel = sb("sel", [96, 2 * S, P], BF16)
        state = sb("state", [P, NH, S])
        xcp = sb("xcp", [P, NH, CH + K - 1])

        arena = sb("arena", [P, 22528])
        a_row = [arena[:, i * N:(i + 1) * N] for i in range(2)]
        w_row = arena[:, 2 * N:3 * N]
        tmp_row = arena[:, 3 * N:4 * N]
        s_bc = arena[:, 4 * N:5 * N]
        at_sb = sb("at_sb", [P, AT_SLOTS, CH])

        zs2 = zs[:, :, :].rearrange("p t d -> p (t d)")
        xs2 = xs[:, :, :].rearrange("p t d -> p (t d)")
        ys2 = ys[:, :, :].rearrange("p t d -> p (t d)")

        def bc(stat, n=T):
            return stat.unsqueeze(2).broadcast_to([P, n, D])

        s_in = sem("s_in")
        s_const = sem("s_const")
        s_fill = sem("s_fill")
        dve_seq = sem("dve_seq")
        act_seq = sem("act_seq")
        x_tp = sem("x_tp")
        x_ev = sem("x_ev")
        lin_ps = sem("lin_ps")
        lin_sb = sem("lin_sb")
        var_rdy = sem("var_rdy")
        pow_rdy = sem("pow_rdy")
        xh_rdy = sem("xh_rdy")
        a_loaded = [sem(f"a_loaded{i}") for i in range(2)]
        deg_used = sem("deg_used")
        tp_done = sem("tp_done")
        at_ready = sem("at_ready")
        mm_done = sem("mm_done")
        y_read = sem("y_read")
        nmax_rdy = sem("nmax_rdy")
        exp_rdy = sem("exp_rdy")
        rec_rdy = sem("rec_rdy")
        sens_rdy = sem("sens_rdy")
        w_rdy = sem("w_rdy")
        hv_rdy = sem("hv_rdy")
        s_out = sem("s_out")

        LOADS = [
            (xs[:, :, :], x.rearrange("(t p) d -> p t d", p=P)),
            (w0n[:, :], W0), (b0c[:, :], b0.rearrange("(p a) -> p a", a=1)), (hvc[:, :], Hv),
            (w2[:, :], W2), (b2bc[:, :], B2.partition_broadcast(P)),
            (gw[:, :], gcn_w), (gbbc[:, :], gcn_b.partition_broadcast(P)),
            (lng[:, :], ln_g.rearrange("(p a) -> p a", a=1)), (lnb[:, :], ln_b.rearrange("(p a) -> p a", a=1)),
            (win[:, :], w_in),
            (cw[:, :, :], conv_w.rearrange("(h p) k -> p h k", p=P)),
            (cb[:, :], conv_b.rearrange("(h p) -> p h", p=P)),
            (wxp[:, :, :], w_xp.rearrange("(h p) k -> p h k", p=P)),
            (wdt[:, :], w_dt), (bdt[:, :], b_dt.rearrange("(h p) -> p h", p=P)),
            (alog[:, :, :], A_log.rearrange("(h p) k -> p h k", p=P)),
            (dsk[:, :], D_skip.rearrange("(h p) -> p h", p=P)),
            (wout[:, :, :], w_out.rearrange("(h p) k -> p h k", p=P)),
        ]
        ALL_IN = 16 * len(LOADS)
        adj_t = adj.rearrange("(t p) j -> t p j", p=P)

        class Count:
            dve = act = xtp = xev = var = 0

        with nc.Block() as block:
            @block.sync
            def _(sp):
                for dst, src in LOADS:
                    sp.dma_start(dst, src, allow_slow_non_contiguous=True).then_inc(s_in, 16)
                for r in range(2):
                    sp.dma_start(a_row[r], adj_t[r]).then_inc(a_loaded[r], 16)
                with sp.Fori(1, T // 2) as i:
                    for par in range(2):
                        sp.wait_ge(deg_used, i * 2 + (par - 1))
                        sp.dma_start(a_row[par], adj_t[bass.ds(i * 2 + par, 1)]
                                     .rearrange("a p j -> (a p) j")).then_inc(a_loaded[par], 16)

            @block.gpsimd
            def _(pool):
                fills = 0
                for ap, value in ((ident[:, :], 0.0), (sel[:, :, :], 0.0), (neg_half[:, :], -0.5),
                                  (half[:, :], 0.5), (state[:, :, :], 0.0), (xcp[:, :, 0:K - 1], 0.0)):
                    nc.gpsimd.memset(ap, value).then_inc(s_fill, 1)
                    fills += 1
                pool.wait_ge(s_fill, fills)
                nc.gpsimd.affine_select(out=ident[:, :], in_=ident[:, :], compare_op=ALU.not_equal, fill=1.0,
                                        base=0, pattern=[[-1, P]], channel_multiplier=1).then_inc(s_const, 1)
                for k in range(3):
                    nc.gpsimd.affine_select(out=sel[:, :, :], in_=sel[:, :, :], compare_op=ALU.not_equal,
                                            fill=1.0, base=-2 * S * k, pattern=[[-1, 2 * S], [0, P]],
                                            channel_multiplier=1).then_inc(s_fill, 1)
                    fills += 1
                    pool.wait_ge(s_fill, fills)
                pool.wait_ge(var_rdy, 1)
                nc.gpsimd.tensor_tensor(cs[:, 1:2], cs[:, 0:1], half[:, :], ALU.pow).then_inc(pow_rdy, 1)
                pool.wait_ge(var_rdy, 2)
                nc.gpsimd.tensor_tensor(st_b[:, :], st_a[:, :], neg_half[:, :], ALU.pow).then_inc(pow_rdy, 1)

            @block.tensor
            def _(pe):
                pe.wait_ge(s_in, ALL_IN)
                pe.wait_ge(s_const, 1)
                nc.tensor.transpose(bank[4][:, 0:P], w0n[:, :], ident[:, :]).then_inc(x_tp, 1)
                for g in range(NC):
                    if g >= 2:
                        pe.wait_ge(x_ev, g)
                    for q in range(4):
                        last = nc.tensor.transpose(bank[g % 2][:, q * P:(q + 1) * P], xs[:, 4 * g + q, :], ident[:, :])
                    last.then_inc(x_tp, 1)
                for c in range(NC):
                    pe.wait_ge(x_ev, c + 2)
                    if c >= 2:
                        pe.wait_ge(lin_sb, c - 1)
                    nc.tensor.matmul(bank[2 + c % 2][:, :], w0T[:, :], xT[:, c * CH:(c + 1) * CH],
                                     start=True, stop=True).then_inc(lin_ps, 1)
                for g in range(NC):
                    pe.wait_ge(xh_rdy, 1)
                    if g >= 2:
                        pe.wait_ge(x_ev, 1 + NC + g - 1)
                    for q in range(4):
                        last = nc.tensor.transpose(bank[g % 2][:, q * P:(q + 1) * P],
                                                   w_row[:, (4 * g + q) * P:(4 * g + q + 1) * P], ident[:, :])
                    last.then_inc(x_tp, 1)

            @block.scalar
            def _(act):
                for c in range(NC):
                    act.wait_ge(lin_ps, c + 1)
                    nc.scalar.activation(w_row[:, c * CH:(c + 1) * CH], bank[2 + c % 2][:, :], ACT.Identity,
                                         bias=b0c[:, :]).then_inc(lin_sb, 1)
                for h in range(1):
                    nc.scalar.activation(Aneg[:, :, :], alog[:, :, :], ACT.Exp).then_inc(act_seq, 1)

            @block.vector
            def _(dve):
                seq = Chain(dve, dve_seq)
                dve.wait_ge(x_tp, 1)
                nc.vector.tensor_copy(w0T[:, :], bank[4][:, 0:P]).then_inc(x_ev, 1)
                for g in range(NC):
                    dve.wait_ge(x_tp, g + 2)
                    nc.vector.tensor_copy(xT[:, g * CH:(g + 1) * CH], bank[g % 2][:, :]).then_inc(x_ev, 1)
                nc.vector.tensor_copy(hv_rep[:, :], hvc[:, :].broadcast_to([P, P])).then_inc(hv_rdy, 1)
                for k in range(3):
                    nc.vector.tensor_copy(wxp3[:, :, k, :], wxp[:, :, R:R + 2 * S]).then_inc(hv_rdy, 1)
                for c in range(NC):
                    dve.wait_ge(lin_sb, c + 1)
                    seq(nc.vector.bn_stats(bn[:, c, :], w_row[:, c * CH:(c + 1) * CH]))
                seq(nc.vector.bn_aggr(mv[:, :], bn[:, :, :]))
                nc.vector.tensor_scalar(cs[:, 0:1], mv[:, 1:2], N / (N - 1.0), None, ALU.mult).then_inc(var_rdy, 1)
                dve.wait_ge(pow_rdy, 1)
                seq(nc.vector.tensor_scalar(cs[:, 2:3], cs[:, 1:2], 1e-6, None, ALU.add))
                seq(nc.vector.reciprocal(cs[:, 3:4], cs[:, 2:3]))
                nc.vector.tensor_scalar(w_row, w_row, mv[:, 0:1], cs[:, 3:4], ALU.subtract, ALU.mult).then_inc(xh_rdy, 1)
                for g in range(NC):
                    dve.wait_ge(x_tp, 1 + NC + g + 1)
                    nc.vector.tensor_copy(zs2[:, g * CH:(g + 1) * CH], bank[g % 2][:, :]).then_inc(x_ev, 1)
                dve.wait_ge(act_seq, 1)
                seq(nc.vector.tensor_scalar(Aneg[:, :, :], Aneg[:, :, :], -1.0, None, ALU.mult))
                with dve.Fori(0, T // 2) as i:
                    for par in range(2):
                        dve.wait_ge(a_loaded[par], i * 16 + 16)
                        nc.vector.tensor_reduce(deg[:, bass.ds(i * 2 + par, 1)], a_row[par], AX_X, ALU.add)\
                            .then_inc(deg_used, 1)
                dve.wait_ge(deg_used, T)
                seq(nc.vector.tensor_scalar(deg[:, :], deg[:, :], 1.0, None, ALU.add))
                nc.vector.tensor_scalar(st_a[:, :], deg[:, :], 1e-37, None, ALU.max).then_inc(var_rdy, 1)
                dve.wait_ge(pow_rdy, 2)
                nc.vector.scalar_tensor_tensor(out=dinv[:, :], in0=deg[:, :], scalar=0.0, in1=st_b[:, :],
                                               op0=ALU.is_gt, op1=ALU.mult).then_inc(dve_seq, 1)
                dve.wait_ge(dve_seq, seq.total + seq.n + 1)
                nc.vector.tensor_tensor(zs[:, :, :], zs[:, :, :], bc(dinv[:, :]), ALU.mult).then_inc(dve_seq, 1)
                Count.dve = seq.total + seq.n + 2
        Count.xtp, Count.xev, Count.var, Count.loaded = 1 + 2 * NC, 1 + 2 * NC, 2, 8 * T

        def a_pass(layer, kind, rhs):
            base = layer * T
            loaded0 = Count.loaded
            src = (lambda par: a_row[par]) if kind == "plain" else (lambda par: w_row)

            def tiles(eng, body):
                for r in range(2):
                    body(r, r, True)
                with eng.Fori(1, T // 2) as i:
                    for par in range(2):
                        body(i * 2 + par, par, False)

            with nc.Block() as block:
                @block.sync
                def _(sp):
                    def load(r, par, first):
                        if not first:
                            if kind == "plain":
                                sp.wait_ge(tp_done, (r + (base - 1)) * 8)
                            else:
                                sp.wait_ge(w_rdy, r + (w_base - 1))
                        if first:
                            sp.dma_start(a_row[par], adj_t[r]).then_inc(a_loaded[par], 16)
                        else:
                            sp.dma_start(a_row[par], adj_t[bass.ds(r, 1)].rearrange("a p j -> (a p) j"))\
                                .then_inc(a_loaded[par], 16)
                    w_base = (layer - 1) * T
                    tiles(sp, load)

                @block.tensor
                def _(pe):
                    def tile(r, par, first):
                        t = r + base

                        def products(g):
                            pe.wait_ge(at_ready, t * 8 + (g + 1))
                            if g == 0 and not (first and base == 0):
                                pe.wait_ge(y_read, t + (-1))
                            for q in range(4):
                                jb = 4 * g + q
                                last = nc.tensor.matmul(bank[2 + par][:, 0:D],
                                                        at_sb[:, g % AT_SLOTS, q * P:(q + 1) * P], rhs[:, jb, :],
                                                        start=(jb == 0), stop=(jb == T - 1))
                            last.then_inc(mm_done, 1)

                        if kind == "plain":
                            pe.wait_ge(a_loaded[par], (r - par) * 8 + (16 + loaded0))
                        else:
                            pe.wait_ge(w_rdy, r + ((layer - 1) * T + 1))
                        for g in range(8):
                            if not (first and base == 0 and r == 0 and g < 2):
                                pe.wait_ge(at_ready, t * 8 + (g - 1))
                            for q in range(4):
                                jb = 4 * g + q
                                last = nc.tensor.transpose(bank[g % 2][:, q * P:(q + 1) * P],
                                                           src(par)[:, jb * P:(jb + 1) * P], ident[:, :])
                            last.then_inc(tp_done, 1)
                            if g >= 1:
                                products(g - 1)
                        products(7)
                    tiles(pe, tile)

                @block.scalar
                def _(act):
                    def tile(r, par, first):
                        t = r + base
                        if kind == "soft":
                            act.wait_ge(nmax_rdy, r + 1)
                            nc.scalar.activation(w_row, w_row, ACT.Exp, bias=nmax[:, 1:2]).then_inc(exp_rdy, 1)
                        if kind == "sens":
                            act.wait_ge(rec_rdy, r + 1)
                            nc.scalar.activation(w_row, w_row, ACT.Square, bias=cs[:, 0:1]).then_inc(sens_rdy, 1)
                            act.wait_ge(sens_rdy, r * 2 + 1)
                            nc.scalar.activation(w_row, w_row, ACT.Exp, scale=-2.0).then_inc(sens_rdy, 1)
                        for g in range(8):
                            act.wait_ge(tp_done, t * 8 + (g + 1))
                            if not (first and base == 0 and r == 0 and g < AT_SLOTS):
                                act.wait_ge(mm_done, t * 8 + (g + 1 - AT_SLOTS))
                            nc.scalar.copy(at_sb[:, g % AT_SLOTS, :], bank[g % 2][:, :]).then_inc(at_ready, 1)
                    tiles(act, tile)

                @block.vector
                def _(dve):
                    seq = Chain(dve, dve_seq)
                    seq.total = seq.base = Count.dve

                    def weights(r, par):
                        t = r + base
                        a = a_row[par]
                        dve.wait_ge(a_loaded[par], (r - par) * 8 + (16 + loaded0))
                        dve.wait_ge(tp_done, t * 8)
                        if kind == "soft":
                            seq(nc.vector.tensor_tensor(w_row, a, s_bc, ALU.mult))
                            seq(nc.vector.tensor_scalar(tmp_row, a, 0.0, -FMAX, ALU.is_equal, ALU.mult))
                            seq(nc.vector.tensor_tensor(w_row, w_row, tmp_row, ALU.add))
                            seq(nc.vector.tensor_reduce(nmax[:, 0:1], w_row, AX_X, ALU.max))
                            nc.vector.tensor_scalar(nmax[:, 1:2], nmax[:, 0:1], -1.0, None, ALU.mult)\
                                .then_inc(nmax_rdy, 1)
                            dve.wait_ge(exp_rdy, r + 1)
                            nc.vector.scalar_tensor_tensor(out=w_row, in0=a, scalar=0.0, in1=w_row,
                                                           op0=ALU.not_equal, op1=ALU.mult,
                                                           accum_out=den1[:, :]).then_inc(w_rdy, 1)
                            dve.wait_ge(w_rdy, r + ((layer - 1) * T + 1))
                            seq(nc.vector.tensor_copy(den[:, bass.ds(r, 1)], den1[:, :]))
                        else:
                            seq(nc.vector.tensor_scalar(tmp_row, a, 0.0, None, ALU.is_equal))
                            seq(nc.vector.tensor_tensor(w_row, a, tmp_row, ALU.add))
                            nc.vector.reciprocal(w_row, w_row).then_inc(rec_rdy, 1)
                            dve.wait_ge(sens_rdy, r * 2 + 2)
                            seq(nc.vector.scalar_tensor_tensor(out=w_row, in0=tmp_row, scalar=0.0, in1=w_row,
                                                               op0=ALU.is_equal, op1=ALU.mult))
                            nc.vector.scalar_tensor_tensor(out=w_row, in0=a, scalar=1.0, in1=w_row,
                                                           op0=ALU.is_lt, op1=ALU.mult).then_inc(w_rdy, 1)

                    def take(r, par):
                        t = r + base
                        dve.wait_ge(mm_done, t * 8 + 8)
                        nc.vector.tensor_copy(ys2[:, bass.ds(r * D, D)], bank[2 + par][:, 0:D]).then_inc(y_read, 1)

                    per_turn = {"plain": 0, "soft": 10, "sens": 6}[kind]
                    if kind == "sens":
                        seq(nc.vector.memset(cs[:, 0:1], -1.0))
                    with dve.Fori(0, T // 2) as i:
                        seq.enter(i, per_turn)
                        for par in range(2):
                            if kind != "plain":
                                weights(i * 2 + par, par)
                            take(i * 2 + par, par)
                        seq.leave(T // 2)
                    Count.dve = seq.total + seq.n
            Count.loaded += 8 * T

        def layer_end(layer):
            xtp0, xev0, var0 = Count.xtp, Count.xev, Count.var
            with nc.Block() as block:
                @block.vector
                def _(dve):
                    seq = Chain(dve, dve_seq)
                    seq.total = seq.base = Count.dve
                    if layer == 0:
                        seq(nc.vector.tensor_tensor(ys[:, :, :], ys[:, :, :], zs[:, :, :], ALU.add))
                        seq(nc.vector.tensor_tensor(ys[:, :, :], ys[:, :, :], bc(dinv[:, :]), ALU.mult))
                    if layer == 1:
                        seq(nc.vector.tensor_scalar(st_a[:, :], den[:, :], 0.0, None, ALU.is_le))
                        seq(nc.vector.tensor_tensor(den[:, :], den[:, :], st_a[:, :], ALU.add))
                        seq(nc.vector.reciprocal(st_a[:, :], den[:, :]))
                        seq(nc.vector.tensor_tensor(ys[:, :, :], ys[:, :, :], bc(st_a[:, :]), ALU.mult))
                    seq(nc.vector.tensor_tensor(xs[:, :, :], xs[:, :, :], ys[:, :, :], ALU.add))
                    seq(nc.vector.tensor_reduce(st_a[:, :], xs[:, :, :], AX_X, ALU.add))
                    seq(nc.vector.tensor_scalar(st_a[:, :], st_a[:, :], 1.0 / D, None, ALU.mult))
                    seq(nc.vector.tensor_tensor(xs[:, :, :], xs[:, :, :], bc(st_a[:, :]), ALU.subtract))
                    seq(nc.vector.tensor_tensor(ys[:, :, :], xs[:, :, :], xs[:, :, :], ALU.mult))
                    seq(nc.vector.tensor_reduce(st_a[:, :], ys[:, :, :], AX_X, ALU.add))
                    nc.vector.tensor_scalar(st_a[:, :], st_a[:, :], 1.0 / D, EPS, ALU.mult, ALU.add)\
                        .then_inc(var_rdy, 1)
                    dve.wait_ge(pow_rdy, var0 + 1)
                    nc.vector.tensor_tensor(xs[:, :, :], xs[:, :, :], bc(st_b[:, :]), ALU.mult).then_inc(xh_rdy, 1)
                    Count.dve = seq.total + seq.n
                    if layer < 2:
                        for g in range(NC):
                            dve.wait_ge(x_tp, xtp0 + g + 1)
                            nc.vector.tensor_copy(xT[:, g * CH:(g + 1) * CH], bank[g % 2][:, :]).then_inc(x_ev, 1)
                        for g in range(NC):
                            dve.wait_ge(x_tp, xtp0 + NC + g + 1)
                            if layer == 0:
                                nc.vector.tensor_copy(s_bc[:, g * CH:(g + 1) * CH], bank[2 + g % 2][:, :])\
                                    .then_inc(x_ev, 1)
                            else:
                                nc.vector.tensor_tensor(zs[:, 4 * g:4 * g + 4, :],
                                                        bank[2 + g % 2][:, :].rearrange("p (q d) -> p q d", d=D),
                                                        b2bc[:, :].unsqueeze(1).broadcast_to([P, 4, D]), ALU.add)\
                                    .then_inc(x_ev, 1)

                @block.gpsimd
                def _(pool):
                    pool.wait_ge(var_rdy, var0 + 1)
                    nc.gpsimd.tensor_tensor(st_b[:, :], st_a[:, :], neg_half[:, :], ALU.pow).then_inc(pow_rdy, 1)

                @block.tensor
                def _(pe):
                    pe.wait_ge(xh_rdy, layer + 2)
                    if layer < 2:
                        for g in range(NC):
                            if g >= 2:
                                pe.wait_ge(x_ev, xev0 + g - 1)
                            for q in range(4):
                                last = nc.tensor.transpose(bank[g % 2][:, q * P:(q + 1) * P], xs[:, 4 * g + q, :],
                                                           ident[:, :])
                            last.then_inc(x_tp, 1)
                        for g in range(NC):
                            pe.wait_ge(x_ev, xev0 + (NC if g < 2 else NC + g - 1))
                            if layer == 0:
                                last = nc.tensor.matmul(bank[2 + g % 2][:, :], hv_rep[:, :],
                                                        xT[:, g * CH:(g + 1) * CH], start=True, stop=True)
                            else:
                                for q in range(4):
                                    r = 4 * g + q
                                    last = nc.tensor.matmul(bank[2 + g % 2][:, q * P:(q + 1) * P],
                                                            xT[:, r * P:(r + 1) * P], w2[:, :], start=True, stop=True)
                            last.then_inc(x_tp, 1)
            Count.var += 1
            if layer < 2:
                Count.xtp += 2 * NC
                Count.xev += 2 * NC

        a_pass(0, "plain", zs)
        layer_end(0)
        a_pass(1, "soft", xs)
        layer_end(1)
        a_pass(2, "sens", zs)
        layer_end(2)
        a_pass(3, "plain", xs)

        at = [0]

        def cut(n, dt=F32, parts=P):
            v = arena[0:parts, at[0]:at[0] + n]
            at[0] += n
            return v

        axst, axT, hbuf, hsq, hT = (cut(CH) for _ in range(5))
        zsil, conv, u, dt, dtu = ([cut(CH) for _ in range(NH)] for _ in range(5))
        absv, expv, lnv, relv = ([cut(CH) for _ in range(NH)] for _ in range(4))
        bcr = cut(CH, parts=96)
        bc3 = sb("bc3", [96, CH], BF16)
        dtr = cut(CH, parts=R)
        b_sb = [cut(CH) for _ in range(2)]
        dA, dBu, prod = ([[cut(CH) for _ in range(2)] for _ in range(NH)] for _ in range(3))
        hst = [cut(CH) for _ in range(NH)]
        osb, osq = cut(CH), cut(CH)
        mst = sb("mst", [P, 4, 4])
        assert at[0] <= 22528

        names = ("ax_st ax_ps ax_sb h_ps hvar hrstd hn hT_ps hT_sb xz_ps xz_sb conv_rdy carried u_rdy dbc_ps "
                 "dtr_rdy bc_rdy dt_ps sp_rdy dt_rdy dtu_rdy b_ps b_rdy c_ps dA_rdy dBu_rdy scanned prod_rdy "
                 "summed yz_rdy o_ps ovar orstd o_rdy o_out osb_free").split()
        m = {n: sem("m_" + n) for n in names}
        pow0 = Count.var

        def v4(ap):
            return ap.rearrange("p (q d) -> p q d", d=D)

        with nc.Block() as block:
            @block.sync
            def _(sp):
                sp.sem_inc(m["osb_free"], 1)
                with sp.Fori(0, NC) as c:
                    sp.wait_ge(m["o_rdy"], c + 1)
                    sp.dma_start(out.rearrange("(c q p) d -> c p q d", q=4, p=P)[bass.ds(c, 1)]
                                 .rearrange("a p q d -> (a p) q d"), v4(osb)).then_inc(m["o_out"], 16)
                    sp.wait_ge(m["o_out"], c * 16 + 16)
                    sp.sem_inc(m["osb_free"], 1)
                sp.wait_ge(m["o_out"], 16 * NC)

            @block.gpsimd
            def _(pool):
                with pool.Fori(0, NC) as c:
                    pool.wait_ge(m["hvar"], c + 1)
                    nc.gpsimd.tensor_tensor(mst[:, 1, :], mst[:, 0, :], neg_half[:, 0:4], ALU.pow)\
                        .then_inc(m["hrstd"], 1)
                    for h in range(NH):
                        pool.wait_ge(m["dt_rdy"], c * NH + (h + 1))
                        nc.gpsimd.tensor_tensor(dtu[h], dt[h], u[h], ALU.mult).then_inc(m["dtu_rdy"], 1)
                    pool.wait_ge(m["dtu_rdy"], c * NH + NH)
                    for n in range(S):
                        pool.wait_ge(m["b_rdy"], c * S + (n + 1))
                        for h in range(NH):
                            if n >= 2:
                                pool.wait_ge(m["scanned"], c * (NH * S) + ((n - 2) * NH + h + 1))
                            nc.gpsimd.tensor_tensor(dBu[h][n % 2], dtu[h], b_sb[n % 2], ALU.mult)\
                                .then_inc(m["dBu_rdy"], 1)
                    pool.wait_ge(m["ovar"], c + 1)
                    nc.gpsimd.tensor_tensor(mst[:, 3, :], mst[:, 2, :], neg_half[:, 0:4], ALU.pow)\
                        .then_inc(m["orstd"], 1)

            @block.tensor
            def _(pe):
                with pe.Fori(0, NC) as c:
                    pe.wait_ge(m["ax_st"], c + 1)
                    for q in range(4):
                        last = nc.tensor.transpose(bank[5][:, q * P:(q + 1) * P], axst[:, q * P:(q + 1) * P], ident[:, :])
                    last.then_inc(m["ax_ps"], 1)
                    pe.wait_ge(m["ax_sb"], c + 1)
                    for q in range(4):
                        last = nc.tensor.matmul(bank[6][:, q * P:(q + 1) * P], axT[:, q * P:(q + 1) * P], gw[:, :],
                                                start=True, stop=True)
                    last.then_inc(m["h_ps"], 1)
                    pe.wait_ge(m["hn"], c + 1)
                    for q in range(4):
                        last = nc.tensor.transpose(bank[5][:, q * P:(q + 1) * P], hbuf[:, q * P:(q + 1) * P], ident[:, :])
                    last.then_inc(m["hT_ps"], 1)
                    pe.wait_ge(m["hT_sb"], c + 1)
                    for k, b in enumerate((6, 7, 5, 6)):
                        if k == 3:
                            pe.wait_ge(m["xz_sb"], c * 4 + 1)
                        nc.tensor.matmul(bank[b][:, :], win[:, k * P:(k + 1) * P], hT, start=True, stop=True)\
                            .then_inc(m["xz_ps"], 1)
                    pe.wait_ge(m["u_rdy"], c * NH + NH)
                    for h in range(NH):
                        last = nc.tensor.matmul(bank[7][0:96, :], wxp3[:, h, :, :].rearrange("p k n -> p (k n)"), u[h],
                                                start=(h == 0), stop=(h == NH - 1))
                    last.then_inc(m["dbc_ps"], 1)
                    for h in range(NH):
                        last = nc.tensor.matmul(bank[5][0:R, :], wxp[:, h, 0:R], u[h],
                                                start=(h == 0), stop=(h == NH - 1))
                    last.then_inc(m["dbc_ps"], 1)
                    pe.wait_ge(m["dtr_rdy"], c + 1)
                    for h, b in enumerate((6, 5)):
                        nc.tensor.matmul(bank[b][:, :], wdt[:, h * P:(h + 1) * P], dtr, start=True, stop=True)\
                            .then_inc(m["dt_ps"], 1)
                    pe.wait_ge(m["bc_rdy"], c + 1)

                    def sums(n):
                        for h in range(NH):
                            pe.wait_ge(m["prod_rdy"], c * (NH * S) + (n * NH + h + 1))
                            nc.tensor.matmul(bank[h][:, :], ident[:, :], prod[h][n % 2], start=(n == 0),
                                             stop=(n == S - 1)).then_inc(m["summed"], 1)

                    for n in range(S):
                        if n >= 1:
                            pe.wait_ge(m["b_rdy"], c * S + n)
                        nc.tensor.matmul(bank[2][:, :], sel[:, n, :], bc3[:, :], start=True, stop=True)\
                            .then_inc(m["b_ps"], 1)
                        if n >= 2:
                            pe.wait_ge(m["prod_rdy"], c * (NH * S) + (n - 1) * NH)
                        nc.tensor.matmul(bank[3 + n % 2][:, :], sel[:, S + n, :], bc3[:, :], start=True, stop=True)\
                            .then_inc(m["c_ps"], 1)
                        if n >= 1:
                            sums(n - 1)
                    sums(S - 1)
                    pe.wait_ge(m["yz_rdy"], c * NH + NH)
                    for q in range(4):
                        for h in range(NH):
                            last = nc.tensor.matmul(bank[2][:, q * P:(q + 1) * P], prod[h][0][:, q * P:(q + 1) * P],
                                                    wout[:, h, :], start=(h == 0), stop=(h == NH - 1))
                    last.then_inc(m["o_ps"], 1)

            @block.scalar
            def _(act):
                with act.Fori(0, NC) as c:
                    nc.scalar.copy(axst, ys2[:, bass.ds(c * CH, CH)]).then_inc(m["ax_st"], 1)
                    act.wait_ge(m["ax_ps"], c + 1)
                    nc.scalar.copy(axT, bank[5][:, :]).then_inc(m["ax_sb"], 1)
                    act.wait_ge(m["hT_ps"], c + 1)
                    nc.scalar.activation(hT, bank[5][:, :], ACT.Identity, bias=lnb[:, :], scale=lng[:, :])\
                        .then_inc(m["hT_sb"], 1)
                    for k, b in enumerate((6, 7, 5, 6)):
                        act.wait_ge(m["xz_ps"], c * 4 + (k + 1))
                        if k < 2:
                            nc.scalar.copy(xcp[:, k, K - 1:], bank[b][:, :]).then_inc(m["xz_sb"], 1)
                        else:
                            nc.scalar.activation(zsil[k - 2], bank[b][:, :], ACT.Silu).then_inc(m["xz_sb"], 1)
                    for h in range(NH):
                        act.wait_ge(m["conv_rdy"], c * NH + (h + 1))
                        nc.scalar.activation(u[h], conv[h], ACT.Silu).then_inc(m["u_rdy"], 1)
                    act.wait_ge(m["dbc_ps"], c * 2 + 2)
                    nc.scalar.copy(dtr, bank[5][0:R, :]).then_inc(m["dtr_rdy"], 1)
                    for h, b in enumerate((6, 5)):
                        act.wait_ge(m["dt_ps"], c * NH + (h + 1))
                        nc.scalar.activation(relv[h], bank[b][:, :], ACT.Relu, bias=bdt[:, h:h + 1]).then_inc(m["sp_rdy"], 1)
                        nc.scalar.activation(absv[h], bank[b][:, :], ACT.Abs, bias=bdt[:, h:h + 1]).then_inc(m["sp_rdy"], 1)
                        act.wait_ge(m["sp_rdy"], c * (4 * NH) + (4 * h + 2))
                        nc.scalar.activation(expv[h], absv[h], ACT.Exp, scale=-1.0).then_inc(m["sp_rdy"], 1)
                        act.wait_ge(m["sp_rdy"], c * (4 * NH) + (4 * h + 3))
                        nc.scalar.activation(lnv[h], expv[h], ACT.Ln, bias=1.0).then_inc(m["sp_rdy"], 1)
                    act.wait_ge(m["dt_rdy"], c * NH + NH)
                    for n in range(S):
                        for h in range(NH):
                            if n >= 2:
                                act.wait_ge(m["scanned"], c * (NH * S) + ((n - 2) * NH + h + 1))
                            nc.scalar.activation(dA[h][n % 2], dt[h], ACT.Exp, scale=Aneg[:, h, n:n + 1])\
                                .then_inc(m["dA_rdy"], 1)
                        act.wait_ge(m["b_ps"], c * S + (n + 1))
                        if n >= 2:
                            act.wait_ge(m["dBu_rdy"], c * (NH * S) + (n - 1) * NH)
                        nc.scalar.copy(b_sb[n % 2], bank[2][:, :]).then_inc(m["b_rdy"], 1)

            @block.vector
            def _(dve):
                seq = Chain(dve, dve_seq)
                seq.total = seq.base = Count.dve

                def normed(buf, sq, k, ready, back, count):
                    seq(nc.vector.tensor_reduce(mst[:, k, :], v4(buf), AX_X, ALU.add))
                    seq(nc.vector.tensor_scalar(mst[:, k, :], mst[:, k, :], 1.0 / D, None, ALU.mult))
                    seq(nc.vector.tensor_tensor(v4(buf), v4(buf), bc(mst[:, k, :], 4), ALU.subtract))
                    seq(nc.vector.tensor_tensor(sq, buf, buf, ALU.mult))
                    seq(nc.vector.tensor_reduce(mst[:, k, :], v4(sq), AX_X, ALU.add))
                    nc.vector.tensor_scalar(mst[:, k, :], mst[:, k, :], 1.0 / D, EPS, ALU.mult, ALU.add)\
                        .then_inc(ready, 1)
                    dve.wait_ge(back, count)
                    return nc.vector.tensor_tensor(v4(buf), v4(buf), bc(mst[:, k + 1, :], 4), ALU.mult)

                with dve.Fori(0, NC) as c:
                    seq.enter(c, 33)
                    dve.wait_ge(m["h_ps"], c + 1)
                    seq(nc.vector.tensor_tensor(v4(hbuf), v4(bank[6][:, :]),
                                                gbbc[:, :].unsqueeze(1).broadcast_to([P, 4, D]), ALU.add))
                    seq(nc.vector.tensor_scalar(hbuf, hbuf, 0.0, None, ALU.max))
                    normed(hbuf, hsq, 0, m["hvar"], m["hrstd"], c + 1).then_inc(m["hn"], 1)
                    for h in range(NH):
                        dve.wait_ge(m["xz_sb"], c * 4 + (h + 1))
                        seq(nc.vector.tensor_scalar(conv[h], xcp[:, h, 0:CH], cw[:, h, 0:1], cb[:, h:h + 1],
                                                    ALU.mult, ALU.add))
                        for k in range(1, K):
                            ins = nc.vector.scalar_tensor_tensor(out=conv[h], in0=xcp[:, h, k:k + CH],
                                                                 scalar=cw[:, h, k:k + 1], in1=conv[h],
                                                                 op0=ALU.mult, op1=ALU.add)
                            if k < K - 1:
                                seq(ins)
                            else:
                                ins.then_inc(m["conv_rdy"], 1)
                    dve.wait_ge(m["conv_rdy"], c * NH + NH)
                    seq(nc.vector.tensor_copy(xcp[:, :, 0:K - 1], xcp[:, :, CH:CH + K - 1]))
                    dve.wait_ge(m["dbc_ps"], c * 2 + 1)
                    seq(nc.vector.tensor_copy(bc3[:, :], bank[7][0:96, :]))
                    seq(nc.vector.tensor_tensor(bcr, bank[7][0:96, :], bc3[:, :], ALU.subtract))
                    seq(nc.vector.tensor_copy(bc3[32:64, :], bcr[32:64, :]))
                    seq(nc.vector.tensor_copy(bc3[64:96, :], bcr[64:96, :]))
                    seq(nc.vector.tensor_tensor(bcr[64:96, :], bcr[64:96, :], bc3[64:96, :], ALU.subtract))
                    nc.vector.tensor_copy(bc3[64:96, :], bcr[64:96, :]).then_inc(m["bc_rdy"], 1)
                    for h in range(NH):
                        dve.wait_ge(m["sp_rdy"], c * (4 * NH) + 4 * (h + 1))
                        seq(nc.vector.tensor_scalar(absv[h], expv[h], 1.0, -1.0, ALU.add, ALU.add))
                        seq(nc.vector.tensor_tensor(absv[h], expv[h], absv[h], ALU.subtract))
                        seq(nc.vector.tensor_tensor(relv[h], relv[h], lnv[h], ALU.add))
                        nc.vector.tensor_tensor(dt[h], relv[h], absv[h], ALU.add).then_inc(m["dt_rdy"], 1)
                    for n in range(S):
                        at_n = c * (NH * S) + n * NH
                        for h in range(NH):
                            dve.wait_ge(m["dA_rdy"], at_n + (h + 1))
                            dve.wait_ge(m["dBu_rdy"], at_n + (h + 1))
                            if n >= 1:
                                dve.wait_ge(m["prod_rdy"], at_n + (h + 1 - NH))
                            nc.vector.tensor_tensor_scan(hst[h], dA[h][n % 2], dBu[h][n % 2], state[:, h, n:n + 1],
                                                         ALU.mult, ALU.add).then_inc(m["scanned"], 1)
                        dve.wait_ge(m["c_ps"], c * S + (n + 1))
                        for h in range(NH):
                            dve.wait_ge(m["scanned"], at_n + (h + 1))
                            if n >= 2:
                                dve.wait_ge(m["summed"], at_n + (h + 1 - 2 * NH))
                            nc.vector.tensor_copy(state[:, h, n:n + 1], hst[h][:, CH - 1:CH])
                            nc.vector.tensor_tensor(prod[h][n % 2], hst[h], bank[3 + n % 2][:, :], ALU.mult)\
                                .then_inc(m["prod_rdy"], 1)
                    dve.wait_ge(m["prod_rdy"], c * (NH * S) + NH * S)
                    for h in range(NH):
                        dve.wait_ge(m["summed"], c * (NH * S) + ((S - 1) * NH + h + 1))
                        seq(nc.vector.scalar_tensor_tensor(out=hst[h], in0=u[h], scalar=dsk[:, h:h + 1],
                                                           in1=bank[h][:, :], op0=ALU.mult, op1=ALU.add))
                        nc.vector.tensor_tensor(prod[h][0], hst[h], zsil[h], ALU.mult).then_inc(m["yz_rdy"], 1)
                    dve.wait_ge(m["o_ps"], c + 1)
                    dve.wait_ge(m["osb_free"], c + 1)
                    seq(nc.vector.tensor_tensor(osb, bank[2][:, :], xs2[:, bass.ds(c * CH, CH)], ALU.add))
                    normed(osb, osq, 2, m["ovar"], m["orstd"], c + 1).then_inc(m["o_rdy"], 1)
                    seq.leave(NC)


_INS = ['x', 'adj', 'L0_gnn_W', 'L0_gnn_b', 'L1_gnn_H_v', 'L2_gnn_W', 'L2_gnn_B', 'L3_gnn_gcn_w', 'L3_gnn_gcn_b',
        'L3_gnn_ln_g', 'L3_gnn_ln_b', 'L3_gnn_w_in', 'L3_gnn_conv_w', 'L3_gnn_conv_b', 'L3_gnn_w_xp', 'L3_gnn_w_dt',
        'L3_gnn_b_dt', 'L3_gnn_A_log', 'L3_gnn_D_skip', 'L3_gnn_w_out']
_OUTS = [((N, D), 'float32')]


def kernel(**inputs):
    import numpy as _np
    import concourse.bacc as _bacc
    from concourse import mybir as _mybir
    from concourse.bass_utils import run_bass_kernel_spmd as _run

    nc = _bacc.Bacc("TRN2", target_bir_lowering=False, num_devices=1)
    arrays, args = {}, []
    for name in _INS:
        a = _np.ascontiguousarray(inputs[name])
        arrays[f"in_{name}_dram"] = a
        args.append(nc.dram_tensor(f"in_{name}_dram", a.shape, _mybir.dt.from_np(a.dtype), kind="ExternalInput").ap())
    for i, (shape, dtype) in enumerate(_OUTS):
        dt = _mybir.dt.from_np(_np.dtype(dtype))
        args.append(nc.dram_tensor(f"out_{i}_dram", shape, dt, kind="ExternalOutput").ap())
    build(nc, *args)
    r = _run(nc, [arrays], core_ids=[0])
    got = tuple(r.results[0][f"out_{i}_dram"] for i in range(len(_OUTS)))
    return got[0]
```

```python
from contextlib import ExitStack

import concourse.bass as bass
from concourse import mybir

ALU = mybir.AluOpType
ACT = mybir.ActivationFunctionType
AX_X = mybir.AxisListType.X
F32 = mybir.dt.float32
BF16 = mybir.dt.bfloat16
FP8 = mybir.dt.float8e4

P = 128
N = 4096
D = 128
T = N // P
CH = 512
NC = N // CH
DI = 2 * D
NH = DI // P
S = 16
R = 8
K = 4
EPS = 1e-5
FMAX = 3.4028234663852886e38
ZW = 3 * D + 4
PW = 1024
NP = N // PW
NPIECES = T * NP
BLK = PW // P
S_RANGE = 60.0
AT_SLOTS = 4


class Chain:

    def __init__(self, eng, sem):
        self.eng, self.sem, self.base, self.n, self.total = eng, sem, 0, 0, 0

    def __call__(self, ins):
        ins.then_inc(self.sem, 1)
        self.n += 1
        self.eng.wait_ge(self.sem, self.base + self.n)

    def enter(self, i, per_turn):
        self.total += self.n
        self.n, self.per_turn = 0, per_turn
        self.base = i * per_turn + self.total

    def leave(self, turns):
        assert self.n == self.per_turn, (self.n, self.per_turn)
        self.total += turns * self.n
        self.base, self.n = self.total, 0


def build(nc, x, adj, W0, b0, Hv, W2, B2, gcn_w, gcn_b, ln_g, ln_b, w_in, conv_w, conv_b, w_xp,
          w_dt, b_dt, A_log, D_skip, w_out, out):
    with ExitStack() as ctx:
        def sb(name, shape, dt=F32):
            return ctx.enter_context(nc.sbuf_tensor(name, shape, dt))

        def sem(name):
            return ctx.enter_context(nc.semaphore(name))

        bank = [ctx.enter_context(nc.psum_tensor(f"bank{i}", [P, CH], F32)) for i in range(8)]

        big = sb("big", [P, T * T * P], FP8)
        at8 = big[:, :].rearrange("p (r b i) -> p r b i", r=T, b=T)
        arena = big[:, :].bitcast(F32)
        xs = sb("xs", [P, T, D])
        z1 = sb("z1", [P, T, ZW], BF16)
        z2 = sb("z2", [P, T, ZW], BF16)
        z1f = z1[:, :, :].rearrange("p t w -> p (t w)").bitcast(F32)
        z2f = z2[:, :, :].rearrange("p t w -> p (t w)").bitcast(F32)
        zs2 = z1f[:, 0:N]
        zs = zs2.rearrange("p (t d) -> p t d", d=D)
        lin = z2f[:, 0:N]
        slots = [z1f[:, i * PW:(i + 1) * PW] for i in range(6)] + [z2f[:, N + i * PW:N + (i + 1) * PW] for i in range(2)]
        q01 = sb("q01", [P, 2, PW], BF16)
        qf = q01[:, :, :].rearrange("p a w -> p (a w)").bitcast(F32)
        x_scr = arena[:, 7 * N:8 * N]

        ident = sb("ident", [P, P])
        ident_bf = sb("ident_bf", [P, P], BF16)
        ones_bf = sb("ones_bf", [P, 2], BF16)
        w0T = sb("w0T", [P, P])
        w0n = w0T
        b0c = sb("b0c", [P, 1])
        hvc = sb("hvc", [P, 1])
        hv_bc = sb("hv_bc", [P, D])
        w2 = sb("w2", [P, P])
        b2bc = sb("b2bc", [P, P])
        neg_half = sb("neg_half", [P, T])
        half = sb("half", [P, 1])
        deg = sb("deg", [P, T])
        dinv = sb("dinv", [P, T])
        den = sb("den", [P, T])
        st_a = sb("st_a", [P, T])
        st_b = sb("st_b", [P, T])
        bn = sb("bn", [P, NC, 6])
        mv = sb("mv", [P, 2])
        mvs = sb("mvs", [P, 4, 2])
        cs = sb("cs", [P, 4])
        nmax = sb("nmax", [P, 2])
        den1 = sb("den1", [P, 4])
        miss = sb("miss", [P, NPIECES])
        srow = sb("srow", [P, T])
        srange = sb("srange", [P, 4])
        flag = sb("flag", [1, 2], mybir.dt.int32)

        gw = sb("gw", [P, P])
        gbbc = sb("gbbc", [P, P])
        lng = sb("lng", [P, 1])
        lnb = sb("lnb", [P, 1])
        win = sb("win", [P, 2 * DI])
        cw = sb("cw", [P, NH, K])
        cb = sb("cb", [P, NH])
        wxp = sb("wxp", [P, NH, R + 2 * S])
        wxp3 = sb("wxp3", [P, NH, 3, 2 * S])
        wdt = sb("wdt", [R, DI])
        bdt = sb("bdt", [P, NH])
        alog = sb("alog", [P, NH, S])
        Aneg = alog
        dsk = sb("dsk", [P, NH])
        wout = sb("wout", [P, NH, D])
        sel = sb("sel", [96, 2 * S], BF16)
        state = sb("state", [P, NH, S])

        a_row = [arena[:, i * N:(i + 1) * N] for i in range(2)]
        w_row = arena[:, 2 * N:3 * N]
        tmp_row = arena[:, 3 * N:4 * N]
        s_bc = arena[:, 4 * N:5 * N]
        xT = arena[:, 5 * N:6 * N]
        ys2 = arena[:, 6 * N:7 * N]
        ys = ys2.rearrange("p (t d) -> p t d", d=D)
        at_sb = arena[:, 7 * N:7 * N + AT_SLOTS * CH].rearrange("p (a w) -> p a w", w=CH)
        hv_rep = arena[:, 7 * N + AT_SLOTS * CH:7 * N + AT_SLOTS * CH + P]

        def bc(stat, n=T):
            return stat.unsqueeze(2).broadcast_to([P, n, D])

        s_in = sem("s_in")
        s_const = sem("s_const")
        s_fill = sem("s_fill")
        dve_seq = sem("dve_seq")
        fast_seq = sem("fast_seq")
        mam_seq = sem("mam_seq")

        w_tp = sem("w_tp")
        w_ev = sem("w_ev")
        p_tp = sem("p_tp")
        p_ev = sem("p_ev")
        lin_ps = sem("lin_ps")
        lin_sb = sem("lin_sb")
        cvar = sem("cvar")
        cstd = sem("cstd")
        xh_rdy = sem("xh_rdy")
        landed = [sem(f"landed{i}") for i in range(len(slots))]
        q_rdy = sem("q_rdy")
        counted = sem("counted")
        dif_rdy = sem("dif_rdy")
        dif_sum = sem("dif_sum")
        q_tp = sem("q_tp")
        at_rdy = sem("at_rdy")
        deg_rdy = sem("deg_rdy")
        miss0 = sem("miss0")
        mis_col = sem("mis_col")
        mis_tot = sem("mis_tot")

        f_dvar = sem("f_dvar")
        f_dinv = sem("f_dinv")
        f_tp = sem("f_tp")
        f_hi = sem("f_hi")
        f_res = sem("f_res")
        f_z = sem("f_z")
        f_mm = sem("f_mm")
        f_rd = sem("f_rd")
        f_var = sem("f_var")
        f_rstd = sem("f_rstd")
        f_rng = sem("f_rng")
        f_all = sem("f_all")
        f_w = sem("f_w")
        e_hi = sem("e_hi")
        e_res = sem("e_res")
        e_z = sem("e_z")
        g_z = sem("g_z")
        g_hi = sem("g_hi")
        g_mm = sem("g_mm")
        g_rd = sem("g_rd")
        g_var = sem("g_var")
        g_rstd = sem("g_rstd")
        l_mm = sem("l_mm")
        l_sb = sem("l_sb")

        def general_sems(name):
            names = ("x_tp",
                     "x_ev",
                     "var_rdy",
                     "pow_rdy",
                     "xn_rdy",
                     "deg_used",
                     "tp_done",
                     "at_ready",
                     "mm_done",
                     "y_read",
                     "nmax_rdy", "exp_rdy", "rec_rdy", "sens_rdy",
                     "w_rdy",
                     "seq")
            g = {n: sem(f"{name}_{n}") for n in names}
            g["a_loaded"] = [sem(f"{name}_a_loaded{i}") for i in range(2)]
            return g, Count()

        class Count:
            dve = xtp = xev = var = loaded = xn = 0

        LOADS = [
            (xs[:, :, :], x.rearrange("(t p) d -> p t d", p=P)),
            (w0n[:, :], W0), (b0c[:, :], b0.rearrange("(p a) -> p a", a=1)), (hvc[:, :], Hv),
            (w2[:, :], W2), (b2bc[:, :], B2.partition_broadcast(P)),
            (hv_bc[:, :], Hv.rearrange("p a -> (p a)").partition_broadcast(P)),
            (gw[:, :], gcn_w), (gbbc[:, :], gcn_b.partition_broadcast(P)),
            (lng[:, :], ln_g.rearrange("(p a) -> p a", a=1)), (lnb[:, :], ln_b.rearrange("(p a) -> p a", a=1)),
            (win[:, :], w_in),
            (cw[:, :, :], conv_w.rearrange("(h p) k -> p h k", p=P)),
            (cb[:, :], conv_b.rearrange("(h p) -> p h", p=P)),
            (wxp[:, :, :], w_xp.rearrange("(h p) k -> p h k", p=P)),
            (wdt[:, :], w_dt), (bdt[:, :], b_dt.rearrange("(h p) -> p h", p=P)),
            (alog[:, :, :], A_log.rearrange("(h p) k -> p h k", p=P)),
            (dsk[:, :], D_skip.rearrange("(h p) -> p h", p=P)),
            (wout[:, :, :], w_out.rearrange("(h p) k -> p h k", p=P)),
        ]
        ALL_IN = 16 * len(LOADS)
        adj_t = adj.rearrange("(t p) j -> t p j", p=P)

        def on_pool(p):
            return p % 3 == 1 and p < NPIECES - 4

        pool_pieces = [p for p in range(NPIECES) if on_pool(p)]
        dve_pieces = [p for p in range(NPIECES) if not on_pool(p)]

        with nc.Block() as block:
            @block.sync
            def _(sp):
                for dst, src in LOADS:
                    sp.dma_start(dst, src, allow_slow_non_contiguous=True).then_inc(s_in, 16)
                for p in range(NPIECES):
                    k = p % len(slots)
                    if p >= len(slots):
                        old = p - len(slots)
                        sp.wait_ge(q_rdy, old + 1)
                        if on_pool(old):
                            sp.wait_ge(dif_sum, pool_pieces.index(old) + 1)
                        else:
                            sp.wait_ge(counted, dve_pieces.index(old) + 1)
                    sp.dma_start(slots[k], adj_t[p // NP][:, (p % NP) * PW:(p % NP + 1) * PW])\
                        .then_inc(landed[k], 16)

            @block.gpsimd
            def _(pool):
                fills = 0
                for ap, value in ((ident[:, :], 0.0), (sel[:, :], 0.0), (neg_half[:, :], -0.5), (half[:, :], 0.5),
                                  (state[:, :, :], 0.0), (ident_bf[:, :], 0.0), (ones_bf[:, :], 1.0)):
                    nc.gpsimd.memset(ap, value).then_inc(s_fill, 1)
                    fills += 1
                pool.wait_ge(s_fill, fills)
                for eye in (ident, ident_bf):
                    nc.gpsimd.affine_select(out=eye[:, :], in_=eye[:, :], compare_op=ALU.not_equal, fill=1.0,
                                            base=0, pattern=[[-1, P]], channel_multiplier=1).then_inc(s_const, 1)
                for k in range(3):
                    nc.gpsimd.affine_select(out=sel[:, :], in_=sel[:, :], compare_op=ALU.not_equal,
                                            fill=1.0, base=-2 * S * k, pattern=[[-1, 2 * S]],
                                            channel_multiplier=1).then_inc(s_fill, 1)
                    fills += 1
                    pool.wait_ge(s_fill, fills)
                for j, p in enumerate(pool_pieces):
                    if p == 22:
                        pool.wait_ge(cvar, 1)
                        nc.gpsimd.tensor_tensor(cs[:, 1:2], cs[:, 0:1], half[:, :], ALU.pow).then_inc(cstd, 1)
                    pool.wait_ge(q_rdy, p + 1)
                    a = slots[p % len(slots)]
                    nc.gpsimd.tensor_tensor(a, a, q01[:, p % 2, :], ALU.subtract).then_inc(dif_rdy, 1)

            @block.tensor
            def _(pe):
                pe.wait_ge(s_in, ALL_IN)
                pe.wait_ge(s_const, 2)
                nc.tensor.transpose(bank[4][:, 0:P], w0n[:, :], ident[:, :]).then_inc(w_tp, 1)
                for g in range(NC):
                    if g >= 2:
                        pe.wait_ge(p_ev, g - 1)
                    for q in range(4):
                        last = nc.tensor.transpose(bank[g % 2][:, q * P:(q + 1) * P], xs[:, 4 * g + q, :], ident[:, :])
                    last.then_inc(p_tp, 1)
                pe.wait_ge(w_ev, 1)
                for c in range(NC):
                    pe.wait_ge(p_ev, c + 1)
                    if c >= 2:
                        pe.wait_ge(lin_sb, c - 1)
                    nc.tensor.matmul(bank[2 + c % 2][:, :], w0T[:, :], x_scr[:, c * CH:(c + 1) * CH],
                                     start=True, stop=True).then_inc(lin_ps, 1)
                pe.wait_ge(lin_sb, NC)

                def degrees(p):
                    pe.wait_ge(at_rdy, p + 1)
                    r = p // NP
                    for b in range(BLK):
                        jb = p % NP * BLK + b
                        last = nc.tensor.matmul(bank[5][:, r:r + 1], at8[:, r, jb, :], ones_bf[:, 0:1],
                                                start=(jb == 0), stop=(jb == T - 1))
                    if p == NPIECES - 1:
                        last.then_inc(deg_rdy, 1)

                for p in range(NPIECES):
                    pe.wait_ge(q_rdy, p + 1)
                    if p >= 4:
                        pe.wait_ge(at_rdy, p - 3)
                    for b in range(BLK):
                        last = nc.tensor.transpose(bank[p % 4][:, :].bitcast(BF16)[:, b * P:(b + 1) * P],
                                                   q01[:, p % 2, b * P:(b + 1) * P], ident_bf[:, :])
                    last.then_inc(q_tp, 1)
                    if p >= 3:
                        degrees(p - 3)
                for p in range(NPIECES - 3, NPIECES):
                    degrees(p)
                pe.wait_ge(mis_col, 1)
                nc.tensor.matmul(bank[7][0:1, 0:1], cs[:, 3:4], half[:, :], start=True, stop=True).then_inc(mis_tot, 1)

            @block.scalar
            def _(act):
                for g in range(NC):
                    act.wait_ge(p_tp, g + 1)
                    nc.scalar.copy(x_scr[:, g * CH:(g + 1) * CH], bank[g % 2][:, :]).then_inc(p_ev, 1)
                for c in range(NC):
                    act.wait_ge(lin_ps, c + 1)
                    nc.scalar.activation(lin[:, c * CH:(c + 1) * CH], bank[2 + c % 2][:, :], ACT.Identity,
                                         bias=b0c[:, :]).then_inc(lin_sb, 1)
                act.wait_ge(s_in, ALL_IN)
                for p in range(NPIECES):
                    act.wait_ge(q_tp, p + 1)
                    nc.scalar.copy(big[:, p * PW:(p + 1) * PW], bank[p % 4][:, :].bitcast(BF16), saturate=False)\
                        .then_inc(at_rdy, 1)
                    if p >= 2 and on_pool(p - 2):
                        a = slots[(p - 2) % len(slots)]
                        act.wait_ge(dif_rdy, pool_pieces.index(p - 2) + 1)
                        act.wait_ge(miss0, 1)
                        nc.scalar.activation(a, a, ACT.Abs, accum_out=miss[:, p - 2:p - 1]).then_inc(dif_sum, 1)

            @block.vector
            def _(dve):
                seq = Chain(dve, dve_seq)
                dve.wait_ge(w_tp, 1)
                nc.vector.tensor_copy(w0T[:, :], bank[4][:, 0:P]).then_inc(w_ev, 1)
                dve.wait_ge(s_in, ALL_IN)
                for k in range(3):
                    nc.vector.tensor_copy(wxp3[:, :, k, :], wxp[:, :, R:R + 2 * S])

                def binary(p):
                    a, k = slots[p % len(slots)], p % len(slots)
                    dve.wait_ge(landed[k], 16 * (p // len(slots) + 1))
                    if p >= 2:
                        dve.wait_ge(q_tp, p - 1)
                        if on_pool(p - 2):
                            dve.wait_ge(dif_rdy, pool_pieces.index(p - 2) + 1)
                        else:
                            dve.wait_ge(counted, dve_pieces.index(p - 2) + 1)
                    nc.vector.tensor_scalar(q01[:, p % 2, :], a, 1.0, None, ALU.is_equal).then_inc(q_rdy, 1)

                def compare(p):
                    if not on_pool(p):
                        a = slots[p % len(slots)]
                        dve.wait_ge(q_rdy, p + 1)
                        nc.vector.scalar_tensor_tensor(out=a, in0=a, scalar=1.0, in1=q01[:, p % 2, :],
                                                       op0=ALU.mult, op1=ALU.not_equal,
                                                       accum_out=miss[:, p:p + 1]).then_inc(counted, 1)

                nc.vector.memset(miss[:, :], 0.0).then_inc(miss0, 1)
                dve.wait_ge(miss0, 1)
                binary(0)
                for p in range(NPIECES):
                    if p + 1 < NPIECES:
                        binary(p + 1)
                    compare(p)
                    if p == 20:
                        for c in range(NC):
                            dve.wait_ge(lin_sb, c + 1)
                            seq(nc.vector.bn_stats(bn[:, c, :], lin[:, c * CH:(c + 1) * CH]))
                        seq(nc.vector.bn_aggr(mv[:, :], bn[:, :, :]))
                        nc.vector.tensor_scalar(cs[:, 0:1], mv[:, 1:2], N / (N - 1.0), None, ALU.mult).then_inc(cvar, 1)
                    if p == 28:
                        dve.wait_ge(cstd, 1)
                        seq(nc.vector.tensor_scalar(cs[:, 2:3], cs[:, 1:2], 1e-6, None, ALU.add))
                        seq(nc.vector.reciprocal(cs[:, 3:4], cs[:, 2:3]))
                        seq(nc.vector.tensor_scalar(lin, lin, mv[:, 0:1], cs[:, 3:4], ALU.subtract, ALU.mult))
                dve.wait_ge(counted, len(dve_pieces))
                dve.wait_ge(dif_sum, len(pool_pieces))
                nc.vector.tensor_reduce(cs[:, 3:4], miss[:, :], AX_X, ALU.add).then_inc(mis_col, 1)
                dve.wait_ge(mis_tot, 1)
                seq(nc.vector.tensor_scalar(flag[0:1, 0:1], bank[7][0:1, 0:1], 0.0, None, ALU.is_equal))
                seq(nc.vector.memset(flag[0:1, 1:2], 0))
                dve.wait_ge(deg_rdy, 1)
                seq(nc.vector.tensor_scalar(deg[:, :], bank[5][:, 0:T], 1.0, None, ALU.add))

        def v4(ap):
            return ap.rearrange("p (q d) -> p q d", d=D)

        fast_count = []

        def fast_layer0():
            with nc.Block() as block:
                tmp = [[z2f[:, N + (2 * i + k) * CH:N + (2 * i + k + 1) * CH] for k in range(2)] for i in range(2)]

                @block.gpsimd
                def _(pool):
                    pool.wait_ge(f_dvar, 1)
                    nc.gpsimd.tensor_tensor(st_b[:, :], st_a[:, :], neg_half[:, :], ALU.pow).then_inc(f_dinv, 1)
                    for k in range(NC):
                        pool.wait_ge(f_var, k + 1)
                        nc.gpsimd.tensor_tensor(st_b[:, 4 * k:4 * k + 4], st_a[:, 4 * k:4 * k + 4],
                                                neg_half[:, 0:4], ALU.pow).then_inc(f_rstd, 1)
                    pool.wait_ge(f_rng, 1)
                    nc.gpsimd.partition_all_reduce(srange[:, 2:4], srange[:, 0:2], P,
                                                   bass.bass_isa.ReduceOp.max).then_inc(f_all, 1)

                @block.tensor
                def _(pe):
                    for g in range(NC):
                        if g >= 2:
                            pe.wait_ge(f_res, 2 * (g - 2) + 1)
                        for q in range(4):
                            last = nc.tensor.transpose(bank[g % 2][:, q * P:(q + 1) * P],
                                                       lin[:, (4 * g + q) * P:(4 * g + q + 1) * P], ident[:, :])
                        last.then_inc(f_tp, 1)
                    for r in range(T):
                        b = bank[2 + r % 4]
                        if r >= 4:
                            pe.wait_ge(f_rd, r - 3)
                        for jb in range(T):
                            if r == 0 and jb % 4 == 0:
                                pe.wait_ge(f_z, jb // 4 + 1)
                            nc.tensor.matmul(b[:, 0:3 * D], at8[:, r, jb, :], z1[:, jb, 0:3 * D],
                                             start=(jb == 0), stop=False)
                        nc.tensor.matmul(b[:, 0:3 * D], ident_bf[:, :], z1[:, r, 0:3 * D], start=False, stop=True)\
                            .then_inc(f_mm, 1)

                @block.scalar
                def _(act):
                    for g in range(NC):
                        for part in range(2):
                            act.wait_ge(f_res, 2 * g + 1 + part)
                            nc.scalar.copy(z1[:, 4 * g:4 * g + 4, part * D:(part + 1) * D],
                                           v4(tmp[g % 2][part])).then_inc(f_hi, 1)

                @block.vector
                def _(dve):
                    seq = Chain(dve, fast_seq)
                    seq(nc.vector.tensor_scalar(st_a[:, :], deg[:, :], 1e-37, None, ALU.max))
                    nc.vector.tensor_copy(st_a[:, :], st_a[:, :]).then_inc(f_dvar, 1)
                    dve.wait_ge(f_dinv, 1)
                    seq(nc.vector.scalar_tensor_tensor(out=dinv[:, :], in0=deg[:, :], scalar=0.0, in1=st_b[:, :],
                                                       op0=ALU.is_gt, op1=ALU.mult))
                    for g in range(NC + 1):
                        if g < NC:
                            dve.wait_ge(f_tp, g + 1)
                            if g >= 2:
                                dve.wait_ge(f_z, g - 1)
                            nc.vector.tensor_tensor(v4(tmp[g % 2][0]), v4(bank[g % 2][:, :]),
                                                    bc(dinv[:, 4 * g:4 * g + 4], 4), ALU.mult).then_inc(f_res, 1)
                            dve.wait_ge(f_hi, 2 * g + 1)
                            nc.vector.tensor_tensor(v4(tmp[g % 2][1]), v4(tmp[g % 2][0]),
                                                    z1[:, 4 * g:4 * g + 4, 0:D], ALU.subtract).then_inc(f_res, 1)
                        if g >= 1:
                            k = g - 1
                            dve.wait_ge(f_hi, 2 * k + 2)
                            nc.vector.tensor_tensor(z1[:, 4 * k:4 * k + 4, 2 * D:3 * D], v4(tmp[k % 2][1]),
                                                    z1[:, 4 * k:4 * k + 4, D:2 * D], ALU.subtract).then_inc(f_z, 1)
                    v = [qf[:, i * D:(i + 1) * D] for i in range(2)]

                    def norm(k):
                        dve.wait_ge(f_rstd, k + 1)
                        for q in range(4):
                            r = 4 * k + q
                            nc.vector.tensor_scalar(xs[:, r, :], xs[:, r, :], mvs[:, q, 0:1], st_b[:, r:r + 1],
                                                    ALU.subtract, ALU.mult).then_inc(fast_seq, 1)
                            seq.n += 1
                        dve.wait_ge(fast_seq, seq.base + seq.n)
                        for q in range(4):
                            r = 4 * k + q
                            nc.vector.tensor_tensor_reduce(qf[:, 2 * D:3 * D], xs[:, r, :], hv_bc[:, :], 1.0, 0.0,
                                                           ALU.mult, ALU.add, srow[:, r:r + 1]).then_inc(fast_seq, 1)
                            seq.n += 1
                            dve.wait_ge(fast_seq, seq.base + seq.n)

                    for r in range(T):
                        dve.wait_ge(f_mm, r + 1)
                        seq(nc.vector.tensor_reduce(v[r % 2], bank[2 + r % 4][:, 0:3 * D]
                                                    .rearrange("p (k d) -> p d k", k=3), AX_X, ALU.add))
                        nc.vector.scalar_tensor_tensor(out=xs[:, r, :], in0=v[r % 2], scalar=dinv[:, r:r + 1],
                                                       in1=xs[:, r, :], op0=ALU.mult, op1=ALU.add).then_inc(f_rd, 1)
                        dve.wait_ge(f_rd, r + 1)
                        if r % 4 == 0 and r:
                            norm(r // 4 - 1)
                        seq(nc.vector.bn_stats(bn[:, r % 4, :], xs[:, r, :]))
                        seq(nc.vector.bn_aggr(mvs[:, r % 4, :], bn[:, r % 4, :]))
                        if r % 4 == 3:
                            nc.vector.tensor_scalar(st_a[:, r - 3:r + 1], mvs[:, :, 1], EPS, None, ALU.add)\
                                .then_inc(f_var, 1)
                    norm(NC - 1)
                    seq(nc.vector.tensor_reduce(srange[:, 0:1], srow[:, :], AX_X, ALU.max))
                    seq(nc.vector.tensor_reduce(srange[:, 1:2], srow[:, :], AX_X, ALU.min))
                    nc.vector.tensor_scalar(srange[:, 1:2], srange[:, 1:2], -1.0, None, ALU.mult).then_inc(f_rng, 1)
                    dve.wait_ge(f_all, 1)
                    seq(nc.vector.tensor_tensor(cs[0:1, 1:2], srange[0:1, 2:3], srange[0:1, 3:4], ALU.add))
                    seq(nc.vector.tensor_scalar(flag[0:1, 1:2], cs[0:1, 1:2], S_RANGE, None, ALU.is_le))
                    seq(nc.vector.tensor_scalar(srange[:, 0:1], srange[:, 2:3], -1.0, None, ALU.mult))
                    fast_count.append(seq.n)

        def fast_rest():
            with nc.Block() as block:
                tmp = [[z1f[:, (2 * i + k) * CH:(2 * i + k + 1) * CH] for k in range(2)] for i in range(2)]
                wt = st_a

                @block.gpsimd
                def _(pool):
                    for k in range(2 * NC):
                        pool.wait_ge(g_var, k + 1)
                        nc.gpsimd.tensor_tensor(den1[:, :], mvs[:, :, 1], neg_half[:, 0:4], ALU.pow).then_inc(g_rstd, 1)

                @block.tensor
                def _(pe):
                    for r in range(T):
                        b = bank[r % 4]
                        if r >= 4:
                            pe.wait_ge(g_rd, r - 3)
                        for jb in range(T):
                            if r == 0 and jb % 4 == 0:
                                pe.wait_ge(e_z, jb // 4 + 1)
                            last = nc.tensor.matmul(b[:, 0:ZW - 1], at8[:, r, jb, :], z2[:, jb, 0:ZW - 1],
                                                    start=(jb == 0), stop=(jb == T - 1))
                        last.then_inc(g_mm, 1)
                    for c in range(NC):
                        if c >= 4:
                            pe.wait_ge(l_sb, c - 3)
                        for jb in range(T):
                            if c == 0:
                                pe.wait_ge(g_z, jb + 1)
                            for part in range(3):
                                last = nc.tensor.matmul(bank[4 + c % 4][:, :], z1[:, jb, part * D:(part + 1) * D],
                                                        at8[:, 4 * c:4 * c + 4, jb, :],
                                                        start=(jb == 0 and part == 0),
                                                        stop=(jb == T - 1 and part == 2))
                        last.then_inc(l_mm, 1)

                @block.scalar
                def _(act):
                    nc.scalar.activation(wt[:, :], srow[:, :], ACT.Exp, bias=srange[:, 0:1]).then_inc(f_w, 1)
                    for g in range(NC):
                        for part in range(2):
                            act.wait_ge(e_res, 2 * g + 1 + part)
                            nc.scalar.copy(z2[:, 4 * g:4 * g + 4, part * D:(part + 1) * D],
                                           v4(tmp[g % 2][part])).then_inc(e_hi, 1)
                    for c in range(NC):
                        act.wait_ge(l_mm, c + 1)
                        nc.scalar.copy(lin[:, c * CH:(c + 1) * CH], bank[4 + c % 4][:, :]).then_inc(l_sb, 1)

                @block.vector
                def _(dve):
                    seq = Chain(dve, fast_seq)
                    seq.total = seq.base = fast_count[0]
                    dve.wait_ge(f_w, 1)
                    w0, w1 = 3 * D, 3 * D + 1
                    wr = qf[:, 0:T]
                    seq(nc.vector.tensor_copy(z2[:, :, w0], wt[:, :]))
                    seq(nc.vector.tensor_tensor(wr, wt[:, :], z2[:, :, w0], ALU.subtract))
                    seq(nc.vector.tensor_copy(z2[:, :, w1], wr))
                    seq(nc.vector.tensor_tensor(z2[:, :, w1 + 1], wr, z2[:, :, w1], ALU.subtract))
                    for g in range(NC + 1):
                        if g < NC:
                            if g >= 2:
                                dve.wait_ge(e_z, g - 1)
                            nc.vector.tensor_tensor(v4(tmp[g % 2][0]), xs[:, 4 * g:4 * g + 4, :],
                                                    bc(wt[:, 4 * g:4 * g + 4], 4), ALU.mult).then_inc(e_res, 1)
                            dve.wait_ge(e_hi, 2 * g + 1)
                            nc.vector.tensor_tensor(v4(tmp[g % 2][1]), v4(tmp[g % 2][0]),
                                                    z2[:, 4 * g:4 * g + 4, 0:D], ALU.subtract).then_inc(e_res, 1)
                        if g >= 1:
                            k = g - 1
                            dve.wait_ge(e_hi, 2 * k + 2)
                            nc.vector.tensor_tensor(z2[:, 4 * k:4 * k + 4, 2 * D:3 * D], v4(tmp[k % 2][1]),
                                                    z2[:, 4 * k:4 * k + 4, D:2 * D], ALU.subtract).then_inc(e_z, 1)
                    dve.wait_ge(e_z, NC)
                    v = qf[:, 0:D]
                    dd = cs
                    stats = [0]

                    def stat(q, r):
                        seq(nc.vector.bn_stats(bn[:, q, :], xs[:, r, :]))
                        seq(nc.vector.bn_aggr(mvs[:, q, :], bn[:, q, :]))

                    def spread():
                        nc.vector.tensor_scalar(mvs[:, :, 1], mvs[:, :, 1], EPS, None, ALU.add).then_inc(g_var, 1)
                        stats[0] += 1
                        dve.wait_ge(g_rstd, stats[0])

                    def norm(q, r):
                        seq(nc.vector.tensor_scalar(xs[:, r, :], xs[:, r, :], mvs[:, q, 0:1], den1[:, q:q + 1],
                                                    ALU.subtract, ALU.mult))

                    for k in range(NC):
                        for q in range(4):
                            r = 4 * k + q
                            dve.wait_ge(g_mm, r + 1)
                            seq(nc.vector.tensor_reduce(v, bank[r % 4][:, 0:3 * D]
                                                        .rearrange("p (k d) -> p d k", k=3), AX_X, ALU.add))
                            nc.vector.tensor_reduce(dd[:, 0:1], bank[r % 4][:, 3 * D:3 * D + 3], AX_X, ALU.add)\
                                .then_inc(g_rd, 1)
                            dve.wait_ge(g_rd, r + 1)
                            seq(nc.vector.tensor_scalar(dd[:, 1:2], dd[:, 0:1], 0.0, None, ALU.is_le))
                            seq(nc.vector.tensor_tensor(dd[:, 2:3], dd[:, 0:1], dd[:, 1:2], ALU.add))
                            seq(nc.vector.reciprocal(dd[:, 3:4], dd[:, 2:3]))
                            seq(nc.vector.scalar_tensor_tensor(out=xs[:, r, :], in0=v, scalar=dd[:, 3:4],
                                                               in1=xs[:, r, :], op0=ALU.mult, op1=ALU.add))
                            stat(q, r)
                        spread()
                        for q in range(4):
                            norm(q, 4 * k + q)
                        for q in range(4):
                            stat(q, 4 * k + q)
                        spread()
                        for q in range(4):
                            r = 4 * k + q
                            norm(q, r)
                            res = qf[:, D:2 * D]
                            seq(nc.vector.tensor_copy(z1[:, r, 0:D], xs[:, r, :]))
                            seq(nc.vector.tensor_tensor(res, xs[:, r, :], z1[:, r, 0:D], ALU.subtract))
                            seq(nc.vector.tensor_copy(z1[:, r, D:2 * D], res))
                            nc.vector.tensor_tensor(z1[:, r, 2 * D:3 * D], res, z1[:, r, D:2 * D], ALU.subtract)\
                                .then_inc(g_z, 1)
                            dve.wait_ge(g_z, r + 1)

        def general_start(G, count):
            with nc.Block() as block:
                @block.sync
                def _(sp):
                    for r in range(2):
                        sp.dma_start(a_row[r], adj_t[r]).then_inc(G["a_loaded"][r], 16)
                    with sp.Fori(1, T // 2) as i:
                        for par in range(2):
                            sp.wait_ge(G["deg_used"], i * 2 + (par - 1))
                            sp.dma_start(a_row[par], adj_t[bass.ds(i * 2 + par, 1)]
                                         .rearrange("a p j -> (a p) j")).then_inc(G["a_loaded"][par], 16)

                @block.gpsimd
                def _(pool):
                    pool.wait_ge(G["var_rdy"], 1)
                    nc.gpsimd.tensor_tensor(st_b[:, :], st_a[:, :], neg_half[:, :], ALU.pow).then_inc(G["pow_rdy"], 1)

                @block.tensor
                def _(pe):
                    for g in range(NC):
                        if g >= 2:
                            pe.wait_ge(G["x_ev"], g - 1)
                        for q in range(4):
                            last = nc.tensor.transpose(bank[g % 2][:, q * P:(q + 1) * P],
                                                       lin[:, (4 * g + q) * P:(4 * g + q + 1) * P], ident[:, :])
                        last.then_inc(G["x_tp"], 1)

                @block.vector
                def _(dve):
                    seq = Chain(dve, G["seq"])
                    for g in range(NC):
                        dve.wait_ge(G["x_tp"], g + 1)
                        nc.vector.tensor_copy(zs2[:, g * CH:(g + 1) * CH], bank[g % 2][:, :]).then_inc(G["x_ev"], 1)
                    with dve.Fori(0, T // 2) as i:
                        for par in range(2):
                            dve.wait_ge(G["a_loaded"][par], i * 16 + 16)
                            nc.vector.tensor_reduce(deg[:, bass.ds(i * 2 + par, 1)], a_row[par], AX_X, ALU.add)\
                                .then_inc(G["deg_used"], 1)
                    dve.wait_ge(G["deg_used"], T)
                    seq(nc.vector.tensor_scalar(deg[:, :], deg[:, :], 1.0, None, ALU.add))
                    nc.vector.tensor_scalar(st_a[:, :], deg[:, :], 1e-37, None, ALU.max).then_inc(G["var_rdy"], 1)
                    dve.wait_ge(G["pow_rdy"], 1)
                    seq(nc.vector.scalar_tensor_tensor(out=dinv[:, :], in0=deg[:, :], scalar=0.0, in1=st_b[:, :],
                                                       op0=ALU.is_gt, op1=ALU.mult))
                    seq(nc.vector.tensor_tensor(zs, zs, bc(dinv[:, :]), ALU.mult))
                    count.dve = seq.total + seq.n
            count.xtp, count.xev, count.var, count.loaded = NC, NC, 1, 8 * T

        def a_pass(G, count, turn, kind, rhs):
            base = turn * T
            w_base = base if kind == "sens" else 0
            loaded0 = count.loaded
            src = (lambda par: a_row[par]) if kind == "plain" else (lambda par: w_row)

            def tiles(eng, body):
                for r in range(2):
                    body(r, r, True)
                with eng.Fori(1, T // 2) as i:
                    for par in range(2):
                        body(i * 2 + par, par, False)

            with nc.Block() as block:
                @block.sync
                def _(sp):
                    def load(r, par, first):
                        if not first:
                            if kind == "plain":
                                sp.wait_ge(G["tp_done"], (r + (base - 1)) * 8)
                            else:
                                sp.wait_ge(G["w_rdy"], r + (w_base - 1))
                        if first:
                            sp.dma_start(a_row[par], adj_t[r]).then_inc(G["a_loaded"][par], 16)
                        else:
                            sp.dma_start(a_row[par], adj_t[bass.ds(r, 1)].rearrange("a p j -> (a p) j"))\
                                .then_inc(G["a_loaded"][par], 16)
                    tiles(sp, load)

                @block.tensor
                def _(pe):
                    def tile(r, par, first):
                        t = r + base

                        def products(g):
                            pe.wait_ge(G["at_ready"], t * 8 + (g + 1))
                            if g == 0 and not (first and base == 0):
                                pe.wait_ge(G["y_read"], t + (-1))
                            for q in range(4):
                                jb = 4 * g + q
                                last = nc.tensor.matmul(bank[2 + par][:, 0:D],
                                                        at_sb[:, g % AT_SLOTS, q * P:(q + 1) * P], rhs[:, jb, :],
                                                        start=(jb == 0), stop=(jb == T - 1))
                            last.then_inc(G["mm_done"], 1)

                        if kind == "plain":
                            pe.wait_ge(G["a_loaded"][par], (r - par) * 8 + (16 + loaded0))
                        else:
                            pe.wait_ge(G["w_rdy"], r + (w_base + 1))
                        for g in range(8):
                            if not (first and base == 0 and r == 0 and g < 2):
                                pe.wait_ge(G["at_ready"], t * 8 + (g - 1))
                            for q in range(4):
                                jb = 4 * g + q
                                last = nc.tensor.transpose(bank[g % 2][:, q * P:(q + 1) * P],
                                                           src(par)[:, jb * P:(jb + 1) * P], ident[:, :])
                            last.then_inc(G["tp_done"], 1)
                            if g >= 1:
                                products(g - 1)
                        products(7)
                    tiles(pe, tile)

                @block.scalar
                def _(act):
                    def tile(r, par, first):
                        t = r + base
                        if kind == "soft":
                            act.wait_ge(G["nmax_rdy"], r + 1)
                            nc.scalar.activation(w_row, w_row, ACT.Exp, bias=nmax[:, 1:2]).then_inc(G["exp_rdy"], 1)
                        if kind == "sens":
                            act.wait_ge(G["rec_rdy"], r + 1)
                            nc.scalar.activation(w_row, w_row, ACT.Square, bias=cs[:, 0:1]).then_inc(G["sens_rdy"], 1)
                            act.wait_ge(G["sens_rdy"], r * 2 + 1)
                            nc.scalar.activation(w_row, w_row, ACT.Exp, scale=-2.0).then_inc(G["sens_rdy"], 1)
                        for g in range(8):
                            act.wait_ge(G["tp_done"], t * 8 + (g + 1))
                            if not (first and base == 0 and r == 0 and g < AT_SLOTS):
                                act.wait_ge(G["mm_done"], t * 8 + (g + 1 - AT_SLOTS))
                            nc.scalar.copy(at_sb[:, g % AT_SLOTS, :], bank[g % 2][:, :]).then_inc(G["at_ready"], 1)
                    tiles(act, tile)

                @block.vector
                def _(dve):
                    seq = Chain(dve, G["seq"])
                    seq.total = seq.base = count.dve

                    def weights(r, par):
                        a = a_row[par]
                        dve.wait_ge(G["a_loaded"][par], (r - par) * 8 + (16 + loaded0))
                        if kind == "soft":
                            seq(nc.vector.tensor_tensor(w_row, a, s_bc, ALU.mult))
                            seq(nc.vector.tensor_scalar(tmp_row, a, 0.0, -FMAX, ALU.is_equal, ALU.mult))
                            seq(nc.vector.tensor_tensor(w_row, w_row, tmp_row, ALU.add))
                            seq(nc.vector.tensor_reduce(nmax[:, 0:1], w_row, AX_X, ALU.max))
                            nc.vector.tensor_scalar(nmax[:, 1:2], nmax[:, 0:1], -1.0, None, ALU.mult)\
                                .then_inc(G["nmax_rdy"], 1)
                            dve.wait_ge(G["exp_rdy"], r + 1)
                            nc.vector.scalar_tensor_tensor(out=w_row, in0=a, scalar=0.0, in1=w_row,
                                                           op0=ALU.not_equal, op1=ALU.mult,
                                                           accum_out=den1[:, 0:1]).then_inc(G["w_rdy"], 1)
                            dve.wait_ge(G["w_rdy"], r + (w_base + 1))
                            seq(nc.vector.tensor_copy(den[:, bass.ds(r, 1)], den1[:, 0:1]))
                        else:
                            seq(nc.vector.tensor_scalar(tmp_row, a, 0.0, None, ALU.is_equal))
                            seq(nc.vector.tensor_tensor(w_row, a, tmp_row, ALU.add))
                            nc.vector.reciprocal(w_row, w_row).then_inc(G["rec_rdy"], 1)
                            dve.wait_ge(G["sens_rdy"], r * 2 + 2)
                            seq(nc.vector.scalar_tensor_tensor(out=w_row, in0=tmp_row, scalar=0.0, in1=w_row,
                                                               op0=ALU.is_equal, op1=ALU.mult))
                            nc.vector.scalar_tensor_tensor(out=w_row, in0=a, scalar=1.0, in1=w_row,
                                                           op0=ALU.is_lt, op1=ALU.mult).then_inc(G["w_rdy"], 1)

                    def take(r, par):
                        t = r + base
                        dve.wait_ge(G["mm_done"], t * 8 + 8)
                        nc.vector.tensor_copy(ys2[:, bass.ds(r * D, D)], bank[2 + par][:, 0:D]).then_inc(G["y_read"], 1)

                    per_turn = {"plain": 0, "soft": 10, "sens": 6}[kind]
                    if kind == "sens":
                        seq(nc.vector.memset(cs[:, 0:1], -1.0))
                    with dve.Fori(0, T // 2) as i:
                        seq.enter(i, per_turn)
                        for par in range(2):
                            if kind != "plain":
                                weights(i * 2 + par, par)
                            take(i * 2 + par, par)
                        seq.leave(T // 2)
                    count.dve = seq.total + seq.n
            count.loaded += 8 * T

        def layer_end(G, count, layer):
            var0 = count.var
            with nc.Block() as block:
                @block.vector
                def _(dve):
                    seq = Chain(dve, G["seq"])
                    seq.total = seq.base = count.dve
                    if layer == 0:
                        seq(nc.vector.tensor_tensor(ys, ys, zs, ALU.add))
                        seq(nc.vector.tensor_tensor(ys, ys, bc(dinv[:, :]), ALU.mult))
                    if layer == 1:
                        seq(nc.vector.tensor_scalar(st_a[:, :], den[:, :], 0.0, None, ALU.is_le))
                        seq(nc.vector.tensor_tensor(den[:, :], den[:, :], st_a[:, :], ALU.add))
                        seq(nc.vector.reciprocal(st_a[:, :], den[:, :]))
                        seq(nc.vector.tensor_tensor(ys, ys, bc(st_a[:, :]), ALU.mult))
                    seq(nc.vector.tensor_tensor(xs[:, :, :], xs[:, :, :], ys, ALU.add))
                    seq(nc.vector.tensor_reduce(st_a[:, :], xs[:, :, :], AX_X, ALU.add))
                    seq(nc.vector.tensor_scalar(st_a[:, :], st_a[:, :], 1.0 / D, None, ALU.mult))
                    seq(nc.vector.tensor_tensor(xs[:, :, :], xs[:, :, :], bc(st_a[:, :]), ALU.subtract))
                    seq(nc.vector.tensor_tensor(ys, xs[:, :, :], xs[:, :, :], ALU.mult))
                    seq(nc.vector.tensor_reduce(st_a[:, :], ys, AX_X, ALU.add))
                    nc.vector.tensor_scalar(st_a[:, :], st_a[:, :], 1.0 / D, EPS, ALU.mult, ALU.add)\
                        .then_inc(G["var_rdy"], 1)
                    dve.wait_ge(G["pow_rdy"], var0 + 1)
                    seq(nc.vector.tensor_tensor(xs[:, :, :], xs[:, :, :], bc(st_b[:, :]), ALU.mult))
                    count.dve = seq.total + seq.n

                @block.gpsimd
                def _(pool):
                    pool.wait_ge(G["var_rdy"], var0 + 1)
                    nc.gpsimd.tensor_tensor(st_b[:, :], st_a[:, :], neg_half[:, :], ALU.pow).then_inc(G["pow_rdy"], 1)
            count.var += 1

        def transposed(G, count, what):
            src = ys if what == "product" else xs
            dst = lin if what == "product" else xT
            xtp0, xev0 = count.xtp, count.xev
            with nc.Block() as block:
                @block.vector
                def _(dve):
                    seq = Chain(dve, G["seq"])
                    seq.total = seq.base = count.dve
                    if what == "scores":
                        seq(nc.vector.tensor_copy(hv_rep, hvc[:, :].broadcast_to([P, P])))
                    count.dve = seq.total + seq.n
                    for g in range(NC):
                        dve.wait_ge(G["x_tp"], xtp0 + g + 1)
                        nc.vector.tensor_copy(dst[:, g * CH:(g + 1) * CH], bank[g % 2][:, :]).then_inc(G["x_ev"], 1)
                    for g in range(NC if what != "product" else 0):
                        dve.wait_ge(G["x_tp"], xtp0 + NC + g + 1)
                        if what == "scores":
                            ins = nc.vector.tensor_copy(s_bc[:, g * CH:(g + 1) * CH], bank[2 + g % 2][:, :])
                        else:
                            ins = nc.vector.tensor_tensor(zs[:, 4 * g:4 * g + 4, :], v4(bank[2 + g % 2][:, :]),
                                                          b2bc[:, :].unsqueeze(1).broadcast_to([P, 4, D]), ALU.add)
                        ins.then_inc(G["x_ev"], 1)

                @block.tensor
                def _(pe):
                    for g in range(NC):
                        if g >= 2:
                            pe.wait_ge(G["x_ev"], xev0 + g - 1)
                        for q in range(4):
                            last = nc.tensor.transpose(bank[g % 2][:, q * P:(q + 1) * P], src[:, 4 * g + q, :],
                                                       ident[:, :])
                        last.then_inc(G["x_tp"], 1)
                    for g in range(NC if what != "product" else 0):
                        pe.wait_ge(G["x_ev"], xev0 + (NC if g < 2 else NC + g - 1))
                        if what == "scores":
                            last = nc.tensor.matmul(bank[2 + g % 2][:, :], hv_rep, xT[:, g * CH:(g + 1) * CH],
                                                    start=True, stop=True)
                        else:
                            for q in range(4):
                                r = 4 * g + q
                                last = nc.tensor.matmul(bank[2 + g % 2][:, q * P:(q + 1) * P],
                                                        xT[:, r * P:(r + 1) * P], w2[:, :], start=True, stop=True)
                        last.then_inc(G["x_tp"], 1)
            both = NC if what == "product" else 2 * NC
            count.xtp += both
            count.xev += both

        def enter_branch():
            for engine in (nc.sync, nc.scalar, nc.vector, nc.gpsimd, nc.tensor):
                engine.nop()

        binary = nc.values_load(flag[0:1, 0:1], min_val=0, max_val=1)
        with nc.If(binary == 1):
            enter_branch()
            fast_layer0()
        with nc.Else():
            enter_branch()
            G, count = general_sems("g")
            general_start(G, count)
            a_pass(G, count, 0, "plain", zs)
            layer_end(G, count, 0)
        near = nc.values_load(flag[0:1, 1:2], min_val=0, max_val=1)
        with nc.If(near == 1):
            enter_branch()
            fast_rest()
        with nc.Else():
            enter_branch()
            G, count = general_sems("h")
            transposed(G, count, "scores")
            a_pass(G, count, 0, "soft", xs)
            layer_end(G, count, 1)
            transposed(G, count, "messages")
            a_pass(G, count, 1, "sens", zs)
            layer_end(G, count, 2)
            a_pass(G, count, 2, "plain", xs)
            transposed(G, count, "product")

        at = [0]

        def cut(n, dt=F32, parts=P):
            v = arena[0:parts, at[0]:at[0] + n]
            at[0] += n
            return v

        axT, hbuf, hsq, hT = (cut(CH) for _ in range(4))
        zsil, conv, u, dt, dtu = ([cut(CH) for _ in range(NH)] for _ in range(5))
        absv, expv, lnv, relv = ([cut(CH) for _ in range(NH)] for _ in range(4))
        bcr = cut(CH, parts=96)
        bc3 = cut(CH // 2, parts=96).bitcast(BF16)
        xcp = cut(NH * (CH + K - 1)).rearrange("p (h w) -> p h w", h=NH)
        dtr = cut(CH, parts=R)
        b_sb = [cut(CH) for _ in range(2)]
        dA, dBu, prod = ([[cut(CH) for _ in range(2)] for _ in range(NH)] for _ in range(3))
        hst = [cut(CH) for _ in range(NH)]
        osb, osq = cut(CH), cut(CH)
        mst = cut(16).rearrange("p (a b) -> p a b", b=4)

        names = ("A_rdy ax_sb h_ps hvar hrstd hn hT_ps hT_sb xz_ps xz_sb conv_rdy carried u_rdy dbc_ps "
                 "dtr_rdy bc_rdy dt_ps sp_rdy dt_rdy dtu_rdy b_ps b_rdy c_ps dA_rdy dBu_rdy scanned prod_rdy "
                 "summed yz_rdy o_ps ovar orstd o_rdy o_out osb_free").split()
        m = {n: sem("m_" + n) for n in names}
        with nc.Block() as block:
            @block.sync
            def _(sp):
                sp.sem_inc(m["osb_free"], 1)
                with sp.Fori(0, NC) as c:
                    sp.wait_ge(m["o_rdy"], c + 1)
                    sp.dma_start(out.rearrange("(c q p) d -> c p q d", q=4, p=P)[bass.ds(c, 1)]
                                 .rearrange("a p q d -> (a p) q d"), v4(osb)).then_inc(m["o_out"], 16)
                    sp.wait_ge(m["o_out"], c * 16 + 16)
                    sp.sem_inc(m["osb_free"], 1)
                sp.wait_ge(m["o_out"], 16 * NC)

            @block.gpsimd
            def _(pool):
                with pool.Fori(0, NC) as c:
                    pool.wait_ge(m["hvar"], c + 1)
                    nc.gpsimd.tensor_tensor(mst[:, 1, :], mst[:, 0, :], neg_half[:, 0:4], ALU.pow)\
                        .then_inc(m["hrstd"], 1)
                    for h in range(NH):
                        pool.wait_ge(m["dt_rdy"], c * NH + (h + 1))
                        nc.gpsimd.tensor_tensor(dtu[h], dt[h], u[h], ALU.mult).then_inc(m["dtu_rdy"], 1)
                    pool.wait_ge(m["dtu_rdy"], c * NH + NH)
                    for n in range(S):
                        pool.wait_ge(m["b_rdy"], c * S + (n + 1))
                        for h in range(NH):
                            if n >= 2:
                                pool.wait_ge(m["scanned"], c * (NH * S) + ((n - 2) * NH + h + 1))
                            nc.gpsimd.tensor_tensor(dBu[h][n % 2], dtu[h], b_sb[n % 2], ALU.mult)\
                                .then_inc(m["dBu_rdy"], 1)
                    pool.wait_ge(m["ovar"], c + 1)
                    nc.gpsimd.tensor_tensor(mst[:, 3, :], mst[:, 2, :], neg_half[:, 0:4], ALU.pow)\
                        .then_inc(m["orstd"], 1)

            @block.tensor
            def _(pe):
                with pe.Fori(0, NC) as c:
                    pe.wait_ge(m["ax_sb"], c + 1)
                    for q in range(4):
                        last = nc.tensor.matmul(bank[6][:, q * P:(q + 1) * P], axT[:, q * P:(q + 1) * P], gw[:, :],
                                                start=True, stop=True)
                    last.then_inc(m["h_ps"], 1)
                    pe.wait_ge(m["hn"], c + 1)
                    for q in range(4):
                        last = nc.tensor.transpose(bank[5][:, q * P:(q + 1) * P], hbuf[:, q * P:(q + 1) * P], ident[:, :])
                    last.then_inc(m["hT_ps"], 1)
                    pe.wait_ge(m["hT_sb"], c + 1)
                    for k, b in enumerate((6, 7, 5, 6)):
                        if k == 3:
                            pe.wait_ge(m["xz_sb"], c * 4 + 1)
                        nc.tensor.matmul(bank[b][:, :], win[:, k * P:(k + 1) * P], hT, start=True, stop=True)\
                            .then_inc(m["xz_ps"], 1)
                    pe.wait_ge(m["u_rdy"], c * NH + NH)
                    for h in range(NH):
                        last = nc.tensor.matmul(bank[7][0:96, :], wxp3[:, h, :, :].rearrange("p k n -> p (k n)"), u[h],
                                                start=(h == 0), stop=(h == NH - 1))
                    last.then_inc(m["dbc_ps"], 1)
                    for h in range(NH):
                        last = nc.tensor.matmul(bank[5][0:R, :], wxp[:, h, 0:R], u[h],
                                                start=(h == 0), stop=(h == NH - 1))
                    last.then_inc(m["dbc_ps"], 1)
                    pe.wait_ge(m["dtr_rdy"], c + 1)
                    for h, b in enumerate((6, 5)):
                        nc.tensor.matmul(bank[b][:, :], wdt[:, h * P:(h + 1) * P], dtr, start=True, stop=True)\
                            .then_inc(m["dt_ps"], 1)
                    pe.wait_ge(m["bc_rdy"], c + 1)

                    def sums(n):
                        for h in range(NH):
                            pe.wait_ge(m["prod_rdy"], c * (NH * S) + (n * NH + h + 1))
                            nc.tensor.matmul(bank[h][:, :], ident[:, :], prod[h][n % 2], start=(n == 0),
                                             stop=(n == S - 1)).then_inc(m["summed"], 1)

                    for n in range(S):
                        if n >= 1:
                            pe.wait_ge(m["b_rdy"], c * S + n)
                        nc.tensor.matmul(bank[2][:, :], sel[:, n:n + 1].broadcast_to([96, P]), bc3, start=True, stop=True)\
                            .then_inc(m["b_ps"], 1)
                        if n >= 2:
                            pe.wait_ge(m["prod_rdy"], c * (NH * S) + (n - 1) * NH)
                        nc.tensor.matmul(bank[3 + n % 2][:, :], sel[:, S + n:S + n + 1].broadcast_to([96, P]), bc3, start=True, stop=True)\
                            .then_inc(m["c_ps"], 1)
                        if n >= 1:
                            sums(n - 1)
                    sums(S - 1)
                    pe.wait_ge(m["yz_rdy"], c * NH + NH)
                    for q in range(4):
                        for h in range(NH):
                            last = nc.tensor.matmul(bank[2][:, q * P:(q + 1) * P], prod[h][0][:, q * P:(q + 1) * P],
                                                    wout[:, h, :], start=(h == 0), stop=(h == NH - 1))
                    last.then_inc(m["o_ps"], 1)

            @block.scalar
            def _(act):
                nc.scalar.activation(Aneg[:, :, :], alog[:, :, :], ACT.Exp).then_inc(m["A_rdy"], 1)
                act.wait_ge(m["A_rdy"], 1)
                nc.scalar.mul(Aneg[:, :, :], Aneg[:, :, :], -1.0).then_inc(m["A_rdy"], 1)
                act.wait_ge(m["A_rdy"], 2)
                with act.Fori(0, NC) as c:
                    nc.scalar.copy(axT, lin[:, bass.ds(c * CH, CH)]).then_inc(m["ax_sb"], 1)
                    act.wait_ge(m["hT_ps"], c + 1)
                    nc.scalar.activation(hT, bank[5][:, :], ACT.Identity, bias=lnb[:, :], scale=lng[:, :])\
                        .then_inc(m["hT_sb"], 1)
                    for k, b in enumerate((6, 7, 5, 6)):
                        act.wait_ge(m["xz_ps"], c * 4 + (k + 1))
                        if k < 2:
                            nc.scalar.copy(xcp[:, k, K - 1:], bank[b][:, :]).then_inc(m["xz_sb"], 1)
                        else:
                            nc.scalar.activation(zsil[k - 2], bank[b][:, :], ACT.Silu).then_inc(m["xz_sb"], 1)
                    for h in range(NH):
                        act.wait_ge(m["conv_rdy"], c * NH + (h + 1))
                        nc.scalar.activation(u[h], conv[h], ACT.Silu).then_inc(m["u_rdy"], 1)
                    act.wait_ge(m["dbc_ps"], c * 2 + 2)
                    nc.scalar.copy(dtr, bank[5][0:R, :]).then_inc(m["dtr_rdy"], 1)
                    for h, b in enumerate((6, 5)):
                        act.wait_ge(m["dt_ps"], c * NH + (h + 1))
                        nc.scalar.activation(relv[h], bank[b][:, :], ACT.Relu, bias=bdt[:, h:h + 1]).then_inc(m["sp_rdy"], 1)
                        nc.scalar.activation(absv[h], bank[b][:, :], ACT.Abs, bias=bdt[:, h:h + 1]).then_inc(m["sp_rdy"], 1)
                        act.wait_ge(m["sp_rdy"], c * (4 * NH) + (4 * h + 2))
                        nc.scalar.activation(expv[h], absv[h], ACT.Exp, scale=-1.0).then_inc(m["sp_rdy"], 1)
                        act.wait_ge(m["sp_rdy"], c * (4 * NH) + (4 * h + 3))
                        nc.scalar.activation(lnv[h], expv[h], ACT.Ln, bias=1.0).then_inc(m["sp_rdy"], 1)
                    act.wait_ge(m["dt_rdy"], c * NH + NH)
                    for n in range(S):
                        for h in range(NH):
                            if n >= 2:
                                act.wait_ge(m["scanned"], c * (NH * S) + ((n - 2) * NH + h + 1))
                            nc.scalar.activation(dA[h][n % 2], dt[h], ACT.Exp, scale=Aneg[:, h, n:n + 1])\
                                .then_inc(m["dA_rdy"], 1)
                        act.wait_ge(m["b_ps"], c * S + (n + 1))
                        if n >= 2:
                            act.wait_ge(m["dBu_rdy"], c * (NH * S) + (n - 1) * NH)
                        nc.scalar.copy(b_sb[n % 2], bank[2][:, :]).then_inc(m["b_rdy"], 1)

            @block.vector
            def _(dve):
                seq = Chain(dve, mam_seq)
                seq(nc.vector.memset(xcp[:, :, 0:K - 1], 0.0))

                def normed(buf, sq, k, ready, back, count):
                    seq(nc.vector.tensor_reduce(mst[:, k, :], v4(buf), AX_X, ALU.add))
                    seq(nc.vector.tensor_scalar(mst[:, k, :], mst[:, k, :], 1.0 / D, None, ALU.mult))
                    seq(nc.vector.tensor_tensor(v4(buf), v4(buf), bc(mst[:, k, :], 4), ALU.subtract))
                    seq(nc.vector.tensor_tensor(sq, buf, buf, ALU.mult))
                    seq(nc.vector.tensor_reduce(mst[:, k, :], v4(sq), AX_X, ALU.add))
                    nc.vector.tensor_scalar(mst[:, k, :], mst[:, k, :], 1.0 / D, EPS, ALU.mult, ALU.add)\
                        .then_inc(ready, 1)
                    dve.wait_ge(back, count)
                    return nc.vector.tensor_tensor(v4(buf), v4(buf), bc(mst[:, k + 1, :], 4), ALU.mult)

                with dve.Fori(0, NC) as c:
                    seq.enter(c, 33)
                    dve.wait_ge(m["h_ps"], c + 1)
                    seq(nc.vector.tensor_tensor(v4(hbuf), v4(bank[6][:, :]),
                                                gbbc[:, :].unsqueeze(1).broadcast_to([P, 4, D]), ALU.add))
                    seq(nc.vector.tensor_scalar(hbuf, hbuf, 0.0, None, ALU.max))
                    normed(hbuf, hsq, 0, m["hvar"], m["hrstd"], c + 1).then_inc(m["hn"], 1)
                    for h in range(NH):
                        dve.wait_ge(m["xz_sb"], c * 4 + (h + 1))
                        seq(nc.vector.tensor_scalar(conv[h], xcp[:, h, 0:CH], cw[:, h, 0:1], cb[:, h:h + 1],
                                                    ALU.mult, ALU.add))
                        for k in range(1, K):
                            ins = nc.vector.scalar_tensor_tensor(out=conv[h], in0=xcp[:, h, k:k + CH],
                                                                 scalar=cw[:, h, k:k + 1], in1=conv[h],
                                                                 op0=ALU.mult, op1=ALU.add)
                            if k < K - 1:
                                seq(ins)
                            else:
                                ins.then_inc(m["conv_rdy"], 1)
                    dve.wait_ge(m["conv_rdy"], c * NH + NH)
                    seq(nc.vector.tensor_copy(xcp[:, :, 0:K - 1], xcp[:, :, CH:CH + K - 1]))
                    dve.wait_ge(m["dbc_ps"], c * 2 + 1)
                    seq(nc.vector.tensor_copy(bc3, bank[7][0:96, :]))
                    seq(nc.vector.tensor_tensor(bcr, bank[7][0:96, :], bc3, ALU.subtract))
                    seq(nc.vector.tensor_copy(bc3[32:64, :], bcr[32:64, :]))
                    seq(nc.vector.tensor_copy(bc3[64:96, :], bcr[64:96, :]))
                    seq(nc.vector.tensor_tensor(bcr[64:96, :], bcr[64:96, :], bc3[64:96, :], ALU.subtract))
                    nc.vector.tensor_copy(bc3[64:96, :], bcr[64:96, :]).then_inc(m["bc_rdy"], 1)
                    for h in range(NH):
                        dve.wait_ge(m["sp_rdy"], c * (4 * NH) + 4 * (h + 1))
                        seq(nc.vector.tensor_scalar(absv[h], expv[h], 1.0, -1.0, ALU.add, ALU.add))
                        seq(nc.vector.tensor_tensor(absv[h], expv[h], absv[h], ALU.subtract))
                        seq(nc.vector.tensor_tensor(relv[h], relv[h], lnv[h], ALU.add))
                        nc.vector.tensor_tensor(dt[h], relv[h], absv[h], ALU.add).then_inc(m["dt_rdy"], 1)
                    for n in range(S):
                        at_n = c * (NH * S) + n * NH
                        for h in range(NH):
                            dve.wait_ge(m["dA_rdy"], at_n + (h + 1))
                            dve.wait_ge(m["dBu_rdy"], at_n + (h + 1))
                            if n >= 1:
                                dve.wait_ge(m["prod_rdy"], at_n + (h + 1 - NH))
                            nc.vector.tensor_tensor_scan(hst[h], dA[h][n % 2], dBu[h][n % 2], state[:, h, n:n + 1],
                                                         ALU.mult, ALU.add).then_inc(m["scanned"], 1)
                        dve.wait_ge(m["c_ps"], c * S + (n + 1))
                        for h in range(NH):
                            dve.wait_ge(m["scanned"], at_n + (h + 1))
                            if n >= 2:
                                dve.wait_ge(m["summed"], at_n + (h + 1 - 2 * NH))
                            nc.vector.tensor_copy(state[:, h, n:n + 1], hst[h][:, CH - 1:CH])
                            nc.vector.tensor_tensor(prod[h][n % 2], hst[h], bank[3 + n % 2][:, :], ALU.mult)\
                                .then_inc(m["prod_rdy"], 1)
                    dve.wait_ge(m["prod_rdy"], c * (NH * S) + NH * S)
                    for h in range(NH):
                        dve.wait_ge(m["summed"], c * (NH * S) + ((S - 1) * NH + h + 1))
                        seq(nc.vector.scalar_tensor_tensor(out=hst[h], in0=u[h], scalar=dsk[:, h:h + 1],
                                                           in1=bank[h][:, :], op0=ALU.mult, op1=ALU.add))
                        nc.vector.tensor_tensor(prod[h][0], hst[h], zsil[h], ALU.mult).then_inc(m["yz_rdy"], 1)
                    dve.wait_ge(m["o_ps"], c + 1)
                    dve.wait_ge(m["osb_free"], c + 1)
                    seq(nc.vector.tensor_tensor(osb, bank[2][:, :], xs[:, :, :].rearrange("p t d -> p (t d)")[:, bass.ds(c * CH, CH)], ALU.add))
                    normed(osb, osq, 2, m["ovar"], m["orstd"], c + 1).then_inc(m["o_rdy"], 1)
                    seq.leave(NC)


_INS = ['x', 'adj', 'L0_gnn_W', 'L0_gnn_b', 'L1_gnn_H_v', 'L2_gnn_W', 'L2_gnn_B', 'L3_gnn_gcn_w', 'L3_gnn_gcn_b',
        'L3_gnn_ln_g', 'L3_gnn_ln_b', 'L3_gnn_w_in', 'L3_gnn_conv_w', 'L3_gnn_conv_b', 'L3_gnn_w_xp', 'L3_gnn_w_dt',
        'L3_gnn_b_dt', 'L3_gnn_A_log', 'L3_gnn_D_skip', 'L3_gnn_w_out']
_OUTS = [((N, D), 'float32')]


def kernel(**inputs):
    import numpy as _np
    import concourse.bacc as _bacc
    from concourse import mybir as _mybir
    from concourse.bass_utils import run_bass_kernel_spmd as _run

    nc = _bacc.Bacc("TRN2", target_bir_lowering=False, num_devices=1)
    arrays, args = {}, []
    for name in _INS:
        a = _np.ascontiguousarray(inputs[name])
        arrays[f"in_{name}_dram"] = a
        args.append(nc.dram_tensor(f"in_{name}_dram", a.shape, _mybir.dt.from_np(a.dtype), kind="ExternalInput").ap())
    for i, (shape, dtype) in enumerate(_OUTS):
        dt = _mybir.dt.from_np(_np.dtype(dtype))
        args.append(nc.dram_tensor(f"out_{i}_dram", shape, dt, kind="ExternalOutput").ap())
    build(nc, *args)
    r = _run(nc, [arrays], core_ids=[0])
    got = tuple(r.results[0][f"out_{i}_dram"] for i in range(len(_OUTS)))
    return got[0]
```

```python
from contextlib import ExitStack

import concourse.bass as bass
from concourse import mybir

ALU = mybir.AluOpType
ACT = mybir.ActivationFunctionType
AX_X = mybir.AxisListType.X
F32 = mybir.dt.float32
BF16 = mybir.dt.bfloat16
FP8 = mybir.dt.float8e4

P = 128
N = 4096
D = 128
T = N // P
CH = 512
NC = N // CH
DI = 2 * D
NH = DI // P
S = 16
R = 8
K = 4
EPS = 1e-5
FMAX = 3.4028234663852886e38
ZW = 3 * D + 4
PW = 1024
NP = N // PW
NPIECES = T * NP
BLK = PW // P
S_RANGE = 60.0
AT_SLOTS = 4


class Chain:

    def __init__(self, eng, sem):
        self.eng, self.sem, self.base, self.n, self.total = eng, sem, 0, 0, 0

    def __call__(self, ins):
        ins.then_inc(self.sem, 1)
        self.n += 1
        self.eng.wait_ge(self.sem, self.base + self.n)

    def enter(self, i, per_turn):
        self.total += self.n
        self.n, self.per_turn = 0, per_turn
        self.base = i * per_turn + self.total

    def leave(self, turns):
        assert self.n == self.per_turn, (self.n, self.per_turn)
        self.total += turns * self.n
        self.base, self.n = self.total, 0


def build(nc, x, adj, W0, b0, Hv, W2, B2, gcn_w, gcn_b, ln_g, ln_b, w_in, conv_w, conv_b, w_xp,
          w_dt, b_dt, A_log, D_skip, w_out, out):
    with ExitStack() as ctx:
        def sb(name, shape, dt=F32):
            return ctx.enter_context(nc.sbuf_tensor(name, shape, dt))

        def sem(name):
            return ctx.enter_context(nc.semaphore(name))

        bank = [ctx.enter_context(nc.psum_tensor(f"bank{i}", [P, CH], F32)) for i in range(8)]

        big = sb("big", [P, T * T * P], FP8)
        at8 = big[:, :].rearrange("p (r b i) -> p r b i", r=T, b=T)
        arena = big[:, :].bitcast(F32)
        xs = sb("xs", [P, T, D])
        z1 = sb("z1", [P, T, ZW], BF16)
        z2 = sb("z2", [P, T, ZW], BF16)
        z1f = z1[:, :, :].rearrange("p t w -> p (t w)").bitcast(F32)
        z2f = z2[:, :, :].rearrange("p t w -> p (t w)").bitcast(F32)
        zs2 = z1f[:, 0:N]
        zs = zs2.rearrange("p (t d) -> p t d", d=D)
        lin = z2f[:, 0:N]
        slots = [z1f[:, i * PW:(i + 1) * PW] for i in range(6)] + [z2f[:, N + i * PW:N + (i + 1) * PW] for i in range(2)]
        q_mem = sb("q_mem", [P, PW + 8])
        qf = q_mem[:, :]
        q01 = q_mem[:, 0:PW].bitcast(BF16).rearrange("p (a w) -> p a w", a=2)
        x_scr = arena[:, 7 * N:8 * N]

        ident = sb("ident", [P, P])
        ident_bf = sb("ident_bf", [P, P], BF16)
        ones_bf = sb("ones_bf", [P, 2], BF16)
        w0T = sb("w0T", [P, P])
        w0n = w0T
        b0c = sb("b0c", [P, 1])
        hvc = sb("hvc", [P, 1])
        hv_bc = sb("hv_bc", [P, D])
        neg_half = sb("neg_half", [P, T])
        half = sb("half", [P, 1])
        deg = sb("deg", [P, T])
        dinv = sb("dinv", [P, T])
        den = sb("den", [P, T])
        st_a = sb("st_a", [P, T])
        st_b = sb("st_b", [P, T])
        bn = sb("bn", [P, NC, 6])
        mv = sb("mv", [P, 2])
        mvs = sb("mvs", [P, 4, 2])
        omv4 = sb("omv4", [P, 4, 2])
        mst = sb("mst", [P, 4, 4])
        ones_f = sb("ones_f", [1, P])
        cs = sb("cs", [P, 4])
        nmax = sb("nmax", [P, 2])
        den1 = sb("den1", [P, 4])
        miss = sb("miss", [P, NPIECES])
        srow = sb("srow", [P, T])
        srange = sb("srange", [P, 4])
        flag = sb("flag", [1, 2], mybir.dt.int32)

        gw = sb("gw", [P, P])
        gbbc = sb("gbbc", [P, P])
        lng = sb("lng", [P, 1])
        lnb = sb("lnb", [P, 1])
        win = sb("win", [P, 2 * DI])
        cw = sb("cw", [P, NH, K])
        cb = sb("cb", [P, NH])
        wxp = sb("wxp", [P, NH, R + 2 * S])
        wxp3 = sb("wxp3", [P, NH, 6 * S + R])
        wdt_mem = sb("wdt", [6 * S + R, DI])
        wdt = wdt_mem[6 * S:6 * S + R, :]
        bdt = sb("bdt", [P, NH])
        alog = sb("alog", [P, NH, S])
        Aneg = alog
        dsk = sb("dsk", [P, NH])
        wout = sb("wout", [P, NH, D])
        sel = sb("sel", [96, 2 * S], BF16)
        state = sb("state", [P, NH, S])

        a_row = [arena[:, i * N:(i + 1) * N] for i in range(2)]
        w_row = arena[:, 2 * N:3 * N]
        tmp_row = arena[:, 3 * N:4 * N]
        s_bc = arena[:, 4 * N:5 * N]
        xT = arena[:, 5 * N:6 * N]
        ys2 = arena[:, 6 * N:7 * N]
        ys = ys2.rearrange("p (t d) -> p t d", d=D)
        at_sb = arena[:, 7 * N:7 * N + AT_SLOTS * CH].rearrange("p (a w) -> p a w", w=CH)
        w2, b2bc = (arena[:, 7 * N + AT_SLOTS * CH + i * P:7 * N + AT_SLOTS * CH + (i + 1) * P] for i in (1, 2))
        ax_all = arena[:, 3 * N:4 * N]
        hv_rep = arena[:, 7 * N + AT_SLOTS * CH:7 * N + AT_SLOTS * CH + P]

        def bc(stat, n=T):
            return stat.unsqueeze(2).broadcast_to([P, n, D])

        s_first = sem("s_first")
        s_in = sem("s_in")
        s_const = sem("s_const")
        s_fill = sem("s_fill")
        dve_seq = sem("dve_seq")
        fast_seq = sem("fast_seq")
        mam_seq = sem("mam_seq")
        w2_in = sem("w2_in")

        w_tp = sem("w_tp")
        w_ev = sem("w_ev")
        p_tp = sem("p_tp")
        p_ev = sem("p_ev")
        lin_ps = sem("lin_ps")
        lin_sb = sem("lin_sb")
        cvar = sem("cvar")
        cstd = sem("cstd")
        xh_rdy = sem("xh_rdy")
        landed = [sem(f"landed{i}") for i in range(len(slots))]
        q_rdy = sem("q_rdy")
        counted = sem("counted")
        dif_rdy = sem("dif_rdy")
        dif_sum = sem("dif_sum")
        q_tp = sem("q_tp")
        at_rdy = sem("at_rdy")
        deg_rdy = sem("deg_rdy")
        miss0 = sem("miss0")
        mis_col = sem("mis_col")
        mis_tot = sem("mis_tot")

        f_dvar = sem("f_dvar")
        f_dinv = sem("f_dinv")
        f_tp = sem("f_tp")
        f_hi = sem("f_hi")
        f_res = sem("f_res")
        f_z = sem("f_z")
        f_mm = sem("f_mm")
        f_rd = sem("f_rd")
        f_var = sem("f_var")
        f_rstd = sem("f_rstd")
        f_rng = sem("f_rng")
        f_all = sem("f_all")
        f_w = sem("f_w")
        e_hi = sem("e_hi")
        e_res = sem("e_res")
        e_z = sem("e_z")
        g_z = sem("g_z")
        g_mm = sem("g_mm")
        g_rd = sem("g_rd")
        g_var = sem("g_var")
        g_rstd = sem("g_rstd")

        def general_sems(name):
            names = ("x_tp",
                     "x_ev",
                     "var_rdy",
                     "pow_rdy",
                     "xn_rdy",
                     "deg_used",
                     "tp_done",
                     "at_ready",
                     "mm_done",
                     "y_read",
                     "nmax_rdy", "exp_rdy", "rec_rdy", "sens_rdy",
                     "w_rdy",
                     "seq")
            g = {n: sem(f"{name}_{n}") for n in names}
            g["a_loaded"] = [sem(f"{name}_a_loaded{i}") for i in range(2)]
            return g, Count()

        class Count:
            dve = xtp = xev = var = loaded = xn = 0

        FIRST = [(w0n[:, :], W0), (b0c[:, :], b0.rearrange("(p a) -> p a", a=1)),
                 (xs[:, :, :], x.rearrange("(t p) d -> p t d", p=P))]
        LOADS = [
            (hvc[:, :], Hv),
            (hv_bc[:, :], Hv.rearrange("p a -> (p a)").partition_broadcast(P)),
            (gw[:, :], gcn_w), (gbbc[:, :], gcn_b.partition_broadcast(P)),
            (lng[:, :], ln_g.rearrange("(p a) -> p a", a=1)), (lnb[:, :], ln_b.rearrange("(p a) -> p a", a=1)),
            (win[:, :], w_in),
            (cw[:, :, :], conv_w.rearrange("(h p) k -> p h k", p=P)),
            (cb[:, :], conv_b.rearrange("(h p) -> p h", p=P)),
            (wxp[:, :, :], w_xp.rearrange("(h p) k -> p h k", p=P)),
            (wdt, w_dt), (bdt[:, :], b_dt.rearrange("(h p) -> p h", p=P)),
            (alog[:, :, :], A_log.rearrange("(h p) k -> p h k", p=P)),
            (dsk[:, :], D_skip.rearrange("(h p) -> p h", p=P)),
            (wout[:, :, :], w_out.rearrange("(h p) k -> p h k", p=P)),
        ]
        ALL_IN = 16 * len(LOADS)
        LIN_LATER = 4
        adj_t = adj.rearrange("(t p) j -> t p j", p=P)

        def on_pool(p):
            return p % 2 == 1 and p < NPIECES - 4

        pool_pieces = [p for p in range(NPIECES) if on_pool(p)]
        after_lin = next(p for p in pool_pieces if p > 22)
        dve_pieces = [p for p in range(NPIECES) if not on_pool(p)]

        with nc.Block() as block:
            @block.sync
            def _(sp):
                for dst, src in FIRST:
                    sp.dma_start(dst, src, allow_slow_non_contiguous=True).then_inc(s_first, 16)
                for p in range(NPIECES):
                    if p == len(slots):
                        for dst, src in LOADS:
                            sp.dma_start(dst, src, allow_slow_non_contiguous=True).then_inc(s_in, 16)
                    k = p % len(slots)
                    if p >= len(slots):
                        old = p - len(slots)
                        sp.wait_ge(q_rdy, old + 1)
                        if on_pool(old):
                            sp.wait_ge(dif_sum, pool_pieces.index(old) + 1)
                        else:
                            sp.wait_ge(counted, dve_pieces.index(old) + 1)
                    sp.dma_start(slots[k], adj_t[p // NP][:, (p % NP) * PW:(p % NP + 1) * PW])\
                        .then_inc(landed[k], 16)

            @block.gpsimd
            def _(pool):
                fills = 0
                for ap, value in ((ident[:, :], 0.0), (sel[:, :], 0.0), (neg_half[:, :], -0.5), (half[:, :], 0.5),
                                  (state[:, :, :], 0.0), (ident_bf[:, :], 0.0), (ones_bf[:, :], 1.0), (ones_f[:, :], 1.0)):
                    nc.gpsimd.memset(ap, value).then_inc(s_fill, 1)
                    fills += 1
                pool.wait_ge(s_fill, fills)
                for eye in (ident, ident_bf):
                    nc.gpsimd.affine_select(out=eye[:, :], in_=eye[:, :], compare_op=ALU.not_equal, fill=1.0,
                                            base=0, pattern=[[-1, P]], channel_multiplier=1).then_inc(s_const, 1)
                for k in range(3):
                    nc.gpsimd.affine_select(out=sel[:, :], in_=sel[:, :], compare_op=ALU.not_equal,
                                            fill=1.0, base=-2 * S * k, pattern=[[-1, 2 * S]],
                                            channel_multiplier=1).then_inc(s_fill, 1)
                    fills += 1
                    pool.wait_ge(s_fill, fills)
                for j, p in enumerate(pool_pieces):
                    if p == after_lin:
                        pool.wait_ge(cvar, 1)
                        nc.gpsimd.tensor_tensor(cs[:, 1:2], cs[:, 0:1], half[:, :], ALU.pow).then_inc(cstd, 1)
                    pool.wait_ge(q_rdy, p + 1)
                    a = slots[p % len(slots)]
                    nc.gpsimd.tensor_tensor(a, a, q01[:, p % 2, :], ALU.subtract).then_inc(dif_rdy, 1)

            @block.tensor
            def _(pe):
                pe.wait_ge(s_first, 16 * len(FIRST))
                pe.wait_ge(s_const, 2)
                nc.tensor.transpose(bank[4][:, 0:P], w0n[:, :], ident[:, :]).then_inc(w_tp, 1)
                pe.wait_ge(w_ev, 1)

                def x_turned(g):
                    if g:
                        pe.wait_ge(p_ev, g)
                    for q in range(4):
                        last = nc.tensor.transpose(bank[4][:, q * P:(q + 1) * P], xs[:, 4 * g + q, :], ident[:, :])
                    last.then_inc(p_tp, 1)

                def linear(c):
                    pe.wait_ge(p_ev, c + 1)
                    if c:
                        pe.wait_ge(lin_sb, c)
                    nc.tensor.matmul(bank[6][:, :], w0T[:, :], x_scr[:, c * CH:(c + 1) * CH],
                                     start=True, stop=True).then_inc(lin_ps, 1)

                def degrees(p):
                    pe.wait_ge(at_rdy, p + 1)
                    r = p // NP
                    for b in range(BLK):
                        jb = p % NP * BLK + b
                        last = nc.tensor.matmul(bank[5][:, r:r + 1], at8[:, r, jb, :], ones_bf[:, 0:1],
                                                start=(jb == 0), stop=(jb == T - 1))
                    if p == NPIECES - 1:
                        last.then_inc(deg_rdy, 1)

                for p in range(NPIECES):
                    pe.wait_ge(q_rdy, p + 1)
                    if p >= 4:
                        pe.wait_ge(at_rdy, p - 3)
                    for b in range(BLK):
                        last = nc.tensor.transpose(bank[p % 4][:, :].bitcast(BF16)[:, b * P:(b + 1) * P],
                                                   q01[:, p % 2, b * P:(b + 1) * P], ident_bf[:, :])
                    last.then_inc(q_tp, 1)
                    if p >= 3:
                        degrees(p - 3)
                    if p < NC:
                        x_turned(p)
                    if LIN_LATER <= p < LIN_LATER + NC:
                        linear(p - LIN_LATER)
                for p in range(NPIECES - 3, NPIECES):
                    degrees(p)
                pe.wait_ge(s_in, ALL_IN)
                pe.wait_ge(mis_col, 1)
                nc.tensor.matmul(bank[7][0:1, 0:1], cs[:, 3:4], half[:, :], start=True, stop=True).then_inc(mis_tot, 1)

            @block.scalar
            def _(act):
                for p in range(NPIECES):
                    act.wait_ge(q_tp, p + 1)
                    nc.scalar.copy(big[:, p * PW:(p + 1) * PW], bank[p % 4][:, :].bitcast(BF16), saturate=False)\
                        .then_inc(at_rdy, 1)
                    if p < NC:
                        act.wait_ge(p_tp, p + 1)
                        nc.scalar.copy(x_scr[:, p * CH:(p + 1) * CH], bank[4][:, :]).then_inc(p_ev, 1)
                    if LIN_LATER <= p < LIN_LATER + NC:
                        c = p - LIN_LATER
                        act.wait_ge(lin_ps, c + 1)
                        nc.scalar.activation(lin[:, c * CH:(c + 1) * CH], bank[6][:, :], ACT.Identity,
                                             bias=b0c[:, :]).then_inc(lin_sb, 1)
                    if p >= 2 and on_pool(p - 2):
                        a = slots[(p - 2) % len(slots)]
                        act.wait_ge(dif_rdy, pool_pieces.index(p - 2) + 1)
                        act.wait_ge(miss0, 1)
                        nc.scalar.activation(a, a, ACT.Abs, accum_out=miss[:, p - 2:p - 1]).then_inc(dif_sum, 1)

            @block.vector
            def _(dve):
                seq = Chain(dve, dve_seq)
                dve.wait_ge(w_tp, 1)
                nc.vector.tensor_copy(w0T[:, :], bank[4][:, 0:P]).then_inc(w_ev, 1)

                def binary(p):
                    a, k = slots[p % len(slots)], p % len(slots)
                    dve.wait_ge(landed[k], 16 * (p // len(slots) + 1))
                    if p >= 2:
                        dve.wait_ge(q_tp, p - 1)
                        if on_pool(p - 2):
                            dve.wait_ge(dif_rdy, pool_pieces.index(p - 2) + 1)
                        else:
                            dve.wait_ge(counted, dve_pieces.index(p - 2) + 1)
                    nc.vector.tensor_scalar(q01[:, p % 2, :], a, 1.0, None, ALU.is_equal).then_inc(q_rdy, 1)

                def compare(p):
                    if not on_pool(p):
                        a = slots[p % len(slots)]
                        dve.wait_ge(q_rdy, p + 1)
                        nc.vector.scalar_tensor_tensor(out=a, in0=a, scalar=1.0, in1=q01[:, p % 2, :],
                                                       op0=ALU.mult, op1=ALU.not_equal,
                                                       accum_out=miss[:, p:p + 1]).then_inc(counted, 1)

                nc.vector.memset(miss[:, :], 0.0).then_inc(miss0, 1)
                dve.wait_ge(miss0, 1)
                binary(0)
                for p in range(NPIECES):
                    if p + 1 < NPIECES:
                        binary(p + 1)
                    compare(p)
                    if p == 16:
                        dve.wait_ge(s_in, ALL_IN)
                        for k in range(3):
                            nc.vector.tensor_copy(wxp3[:, :, k * 2 * S:(k + 1) * 2 * S], wxp[:, :, R:R + 2 * S])
                        nc.vector.tensor_copy(wxp3[:, :, 6 * S:], wxp[:, :, 0:R])
                    if p == 20:
                        for c in range(NC):
                            dve.wait_ge(lin_sb, c + 1)
                            seq(nc.vector.bn_stats(bn[:, c, :], lin[:, c * CH:(c + 1) * CH]))
                        seq(nc.vector.bn_aggr(mv[:, :], bn[:, :, :]))
                        nc.vector.tensor_scalar(cs[:, 0:1], mv[:, 1:2], N / (N - 1.0), None, ALU.mult).then_inc(cvar, 1)
                    if p == 28:
                        dve.wait_ge(cstd, 1)
                        seq(nc.vector.tensor_scalar(cs[:, 2:3], cs[:, 1:2], 1e-6, None, ALU.add))
                        seq(nc.vector.reciprocal(cs[:, 3:4], cs[:, 2:3]))
                        seq(nc.vector.tensor_scalar(lin, lin, mv[:, 0:1], cs[:, 3:4], ALU.subtract, ALU.mult))
                dve.wait_ge(counted, len(dve_pieces))
                dve.wait_ge(dif_sum, len(pool_pieces))
                nc.vector.tensor_reduce(cs[:, 3:4], miss[:, :], AX_X, ALU.add).then_inc(mis_col, 1)
                dve.wait_ge(mis_tot, 1)
                seq(nc.vector.tensor_scalar(flag[0:1, 0:1], bank[7][0:1, 0:1], 0.0, None, ALU.is_equal))
                seq(nc.vector.memset(flag[0:1, 1:2], 0))
                dve.wait_ge(deg_rdy, 1)
                seq(nc.vector.tensor_scalar(deg[:, :], bank[5][:, 0:T], 1.0, None, ALU.add))

        def v4(ap):
            return ap.rearrange("p (q d) -> p q d", d=D)

        fast_count = []

        def fast_layer0():
            with nc.Block() as block:
                tmp = [[z2f[:, N + (2 * i + k) * CH:N + (2 * i + k + 1) * CH] for k in range(2)] for i in range(2)]

                @block.gpsimd
                def _(pool):
                    pool.wait_ge(f_dvar, 1)
                    for k in range(NC):
                        nc.gpsimd.tensor_tensor(st_b[:, 4 * k:4 * k + 4], st_a[:, 4 * k:4 * k + 4],
                                                neg_half[:, 0:4], ALU.pow).then_inc(f_dinv, 1)
                    for k in range(NC):
                        pool.wait_ge(f_var, k + 1)
                        nc.gpsimd.tensor_tensor(st_b[:, 4 * k:4 * k + 4], st_a[:, 4 * k:4 * k + 4],
                                                neg_half[:, 0:4], ALU.pow).then_inc(f_rstd, 1)
                    pool.wait_ge(f_rng, 1)
                    nc.gpsimd.partition_all_reduce(srange[:, 2:4], srange[:, 0:2], P,
                                                   bass.bass_isa.ReduceOp.max).then_inc(f_all, 1)

                @block.tensor
                def _(pe):
                    def lin_back(g):
                        if g >= 2:
                            pe.wait_ge(f_res, 2 * (g - 2) + 1)
                        for q in range(4):
                            last = nc.tensor.transpose(bank[g % 2][:, q * P:(q + 1) * P],
                                                       lin[:, (4 * g + q) * P:(4 * g + q + 1) * P], ident[:, :])
                        last.then_inc(f_tp, 1)

                    def neighbours(r, jbs):
                        for jb in jbs:
                            nc.tensor.matmul(bank[2 + r % 6][:, 0:3 * D], at8[:, r, jb, :], z1[:, jb, 0:3 * D],
                                             start=(jb == 0), stop=False)

                    def self_loop(r):
                        nc.tensor.matmul(bank[2 + r % 6][:, 0:3 * D], ident_bf[:, :], z1[:, r, 0:3 * D],
                                         start=False, stop=True).then_inc(f_mm, 1)

                    lin_back(0)
                    lin_back(1)
                    for g in range(NC):
                        if g + 2 < NC:
                            lin_back(g + 2)
                        pe.wait_ge(f_z, g + 1)
                        for r in range(4):
                            neighbours(r, range(4 * g, 4 * g + 4))
                    for r in range(4):
                        self_loop(r)
                    for r in range(4, T):
                        if r >= 6:
                            pe.wait_ge(f_rd, r - 5)
                        neighbours(r, range(T))
                        self_loop(r)

                @block.scalar
                def _(act):
                    for g in range(NC):
                        for part in range(2):
                            act.wait_ge(f_res, 2 * g + 1 + part)
                            nc.scalar.copy(z1[:, 4 * g:4 * g + 4, part * D:(part + 1) * D],
                                           v4(tmp[g % 2][part])).then_inc(f_hi, 1)

                @block.vector
                def _(dve):
                    seq = Chain(dve, fast_seq)
                    seq(nc.vector.tensor_scalar(st_a[:, :], deg[:, :], 1e-37, None, ALU.max))
                    nc.vector.tensor_copy(st_a[:, :], st_a[:, :]).then_inc(f_dvar, 1)
                    for g in range(NC + 1):
                        if g < NC:
                            dve.wait_ge(f_dinv, g + 1)
                            four = slice(4 * g, 4 * g + 4)
                            seq(nc.vector.scalar_tensor_tensor(out=dinv[:, four], in0=deg[:, four], scalar=0.0,
                                                               in1=st_b[:, four], op0=ALU.is_gt, op1=ALU.mult))
                            dve.wait_ge(f_tp, g + 1)
                            if g >= 2:
                                dve.wait_ge(f_z, g - 1)
                            nc.vector.tensor_tensor(v4(tmp[g % 2][0]), v4(bank[g % 2][:, :]),
                                                    bc(dinv[:, 4 * g:4 * g + 4], 4), ALU.mult).then_inc(f_res, 1)
                            dve.wait_ge(f_hi, 2 * g + 1)
                            nc.vector.tensor_tensor(v4(tmp[g % 2][1]), v4(tmp[g % 2][0]),
                                                    z1[:, 4 * g:4 * g + 4, 0:D], ALU.subtract).then_inc(f_res, 1)
                        if g >= 1:
                            k = g - 1
                            dve.wait_ge(f_hi, 2 * k + 2)
                            nc.vector.tensor_tensor(z1[:, 4 * k:4 * k + 4, 2 * D:3 * D], v4(tmp[k % 2][1]),
                                                    z1[:, 4 * k:4 * k + 4, D:2 * D], ALU.subtract).then_inc(f_z, 1)
                    v = [qf[:, i * D:(i + 1) * D] for i in range(2)]

                    def norm(k):
                        dve.wait_ge(f_rstd, k + 1)
                        for q in range(4):
                            r = 4 * k + q
                            nc.vector.tensor_scalar(xs[:, r, :], xs[:, r, :], mvs[:, q, 0:1], st_b[:, r:r + 1],
                                                    ALU.subtract, ALU.mult).then_inc(fast_seq, 1)
                            seq.n += 1
                        dve.wait_ge(fast_seq, seq.base + seq.n)
                        for q in range(4):
                            r = 4 * k + q
                            nc.vector.tensor_tensor_reduce(qf[:, 2 * D:3 * D], xs[:, r, :], hv_bc[:, :], 1.0, 0.0,
                                                           ALU.mult, ALU.add, srow[:, r:r + 1]).then_inc(fast_seq, 1)
                            seq.n += 1
                            dve.wait_ge(fast_seq, seq.base + seq.n)

                    for r in range(T):
                        dve.wait_ge(f_mm, r + 1)
                        seq(nc.vector.tensor_reduce(v[r % 2], bank[2 + r % 6][:, 0:3 * D]
                                                    .rearrange("p (k d) -> p d k", k=3), AX_X, ALU.add))
                        nc.vector.scalar_tensor_tensor(out=xs[:, r, :], in0=v[r % 2], scalar=dinv[:, r:r + 1],
                                                       in1=xs[:, r, :], op0=ALU.mult, op1=ALU.add).then_inc(f_rd, 1)
                        dve.wait_ge(f_rd, r + 1)
                        if r % 4 == 0 and r:
                            norm(r // 4 - 1)
                        seq(nc.vector.bn_stats(bn[:, r % 4, :], xs[:, r, :]))
                        seq(nc.vector.bn_aggr(mvs[:, r % 4, :], bn[:, r % 4, :]))
                        if r % 4 == 3:
                            nc.vector.tensor_scalar(st_a[:, r - 3:r + 1], mvs[:, :, 1], EPS, None, ALU.add)\
                                .then_inc(f_var, 1)
                    norm(NC - 1)
                    seq(nc.vector.tensor_reduce(srange[:, 0:1], srow[:, :], AX_X, ALU.max))
                    seq(nc.vector.tensor_reduce(srange[:, 1:2], srow[:, :], AX_X, ALU.min))
                    nc.vector.tensor_scalar(srange[:, 1:2], srange[:, 1:2], -1.0, None, ALU.mult).then_inc(f_rng, 1)
                    dve.wait_ge(f_all, 1)
                    seq(nc.vector.tensor_tensor(cs[0:1, 1:2], srange[0:1, 2:3], srange[0:1, 3:4], ALU.add))
                    seq(nc.vector.tensor_scalar(flag[0:1, 1:2], cs[0:1, 1:2], S_RANGE, None, ALU.is_le))
                    seq(nc.vector.tensor_scalar(srange[:, 0:1], srange[:, 2:3], -1.0, None, ALU.mult))
                    fast_count.append(seq.n)

        def l3_bank(k):
            return bank[k % 2]

        def pe_l3(k, lo, hi):
            for i in range(lo, hi):
                jb, part = i // 3, i % 3
                last = nc.tensor.matmul(l3_bank(k)[:, :], z1[:, jb, part * D:(part + 1) * D],
                                        at8[:, 4 * k:4 * k + 4, jb, :], start=(i == 0), stop=(i == 3 * T - 1))
            return last

        L3_EARLY = T - 4

        def fast_rest():
            with nc.Block() as block:
                tmp = [[z1f[:, (2 * i + k) * CH:(2 * i + k + 1) * CH] for k in range(2)] for i in range(2)]
                wt = st_a

                @block.gpsimd
                def _(pool):
                    for k in range(2 * NC):
                        pool.wait_ge(g_var, k + 1)
                        nc.gpsimd.tensor_tensor(den1[:, :], mvs[:, :, 1], neg_half[:, 0:4], ALU.pow).then_inc(g_rstd, 1)

                @block.tensor
                def _(pe):
                    def neighbours(r, jbs):
                        for jb in jbs:
                            last = nc.tensor.matmul(bank[r % 8][:, 0:ZW - 1], at8[:, r, jb, :], z2[:, jb, 0:ZW - 1],
                                                    start=(jb == 0), stop=(jb == T - 1))
                        if jb == T - 1:
                            last.then_inc(g_mm, 1)

                    for g in range(NC):
                        pe.wait_ge(e_z, g + 1)
                        for r in range(4):
                            neighbours(r, range(4 * g, 4 * g + 4))
                    for r in range(4, T):
                        if r >= 8:
                            pe.wait_ge(g_rd, r - 7)
                        neighbours(r, range(T))
                    pe.wait_ge(g_z, L3_EARLY)
                    pe.wait_ge(g_rd, T - 7)
                    pe_l3(0, 0, 3 * L3_EARLY)

                @block.scalar
                def _(act):
                    nc.scalar.activation(wt[:, :], srow[:, :], ACT.Exp, bias=srange[:, 0:1]).then_inc(f_w, 1)
                    for g in range(NC):
                        for part in range(2):
                            act.wait_ge(e_res, 2 * g + 1 + part)
                            nc.scalar.copy(z2[:, 4 * g:4 * g + 4, part * D:(part + 1) * D],
                                           v4(tmp[g % 2][part])).then_inc(e_hi, 1)

                @block.vector
                def _(dve):
                    seq = Chain(dve, fast_seq)
                    seq.total = seq.base = fast_count[0]
                    dve.wait_ge(f_w, 1)
                    w0, w1 = 3 * D, 3 * D + 1
                    wr = qf[:, 0:T]
                    seq(nc.vector.tensor_copy(z2[:, :, w0], wt[:, :]))
                    seq(nc.vector.tensor_tensor(wr, wt[:, :], z2[:, :, w0], ALU.subtract))
                    seq(nc.vector.tensor_copy(z2[:, :, w1], wr))
                    seq(nc.vector.tensor_tensor(z2[:, :, w1 + 1], wr, z2[:, :, w1], ALU.subtract))
                    for g in range(NC + 1):
                        if g < NC:
                            if g >= 2:
                                dve.wait_ge(e_z, g - 1)
                            nc.vector.tensor_tensor(v4(tmp[g % 2][0]), xs[:, 4 * g:4 * g + 4, :],
                                                    bc(wt[:, 4 * g:4 * g + 4], 4), ALU.mult).then_inc(e_res, 1)
                            dve.wait_ge(e_hi, 2 * g + 1)
                            nc.vector.tensor_tensor(v4(tmp[g % 2][1]), v4(tmp[g % 2][0]),
                                                    z2[:, 4 * g:4 * g + 4, 0:D], ALU.subtract).then_inc(e_res, 1)
                        if g >= 1:
                            k = g - 1
                            dve.wait_ge(e_hi, 2 * k + 2)
                            nc.vector.tensor_tensor(z2[:, 4 * k:4 * k + 4, 2 * D:3 * D], v4(tmp[k % 2][1]),
                                                    z2[:, 4 * k:4 * k + 4, D:2 * D], ALU.subtract).then_inc(e_z, 1)
                    dve.wait_ge(e_z, NC)
                    v = qf[:, 0:D]
                    dd = cs
                    stats = [0]

                    def stat(q, r):
                        seq(nc.vector.bn_stats(bn[:, q, :], xs[:, r, :]))
                        seq(nc.vector.bn_aggr(mvs[:, q, :], bn[:, q, :]))

                    def spread():
                        nc.vector.tensor_scalar(mvs[:, :, 1], mvs[:, :, 1], EPS, None, ALU.add).then_inc(g_var, 1)
                        stats[0] += 1
                        dve.wait_ge(g_rstd, stats[0])

                    def norm(q, r):
                        seq(nc.vector.tensor_scalar(xs[:, r, :], xs[:, r, :], mvs[:, q, 0:1], den1[:, q:q + 1],
                                                    ALU.subtract, ALU.mult))

                    for k in range(NC):
                        for q in range(4):
                            r = 4 * k + q
                            dve.wait_ge(g_mm, r + 1)
                            seq(nc.vector.tensor_reduce(v, bank[r % 8][:, 0:3 * D]
                                                        .rearrange("p (k d) -> p d k", k=3), AX_X, ALU.add))
                            nc.vector.tensor_reduce(dd[:, 0:1], bank[r % 8][:, 3 * D:3 * D + 3], AX_X, ALU.add)\
                                .then_inc(g_rd, 1)
                            dve.wait_ge(g_rd, r + 1)
                            seq(nc.vector.tensor_scalar(dd[:, 1:2], dd[:, 0:1], 0.0, None, ALU.is_le))
                            seq(nc.vector.tensor_tensor(dd[:, 2:3], dd[:, 0:1], dd[:, 1:2], ALU.add))
                            seq(nc.vector.reciprocal(dd[:, 3:4], dd[:, 2:3]))
                            seq(nc.vector.scalar_tensor_tensor(out=xs[:, r, :], in0=v, scalar=dd[:, 3:4],
                                                               in1=xs[:, r, :], op0=ALU.mult, op1=ALU.add))
                            stat(q, r)
                        spread()
                        for q in range(4):
                            norm(q, 4 * k + q)
                        for q in range(4):
                            stat(q, 4 * k + q)
                        spread()
                        for q in range(4):
                            r = 4 * k + q
                            norm(q, r)
                            res = qf[:, D:2 * D]
                            seq(nc.vector.tensor_copy(z1[:, r, 0:D], xs[:, r, :]))
                            seq(nc.vector.tensor_tensor(res, xs[:, r, :], z1[:, r, 0:D], ALU.subtract))
                            seq(nc.vector.tensor_copy(z1[:, r, D:2 * D], res))
                            nc.vector.tensor_tensor(z1[:, r, 2 * D:3 * D], res, z1[:, r, D:2 * D], ALU.subtract)\
                                .then_inc(g_z, 1)
                            dve.wait_ge(g_z, r + 1)

        def general_start(G, count):
            with nc.Block() as block:
                @block.sync
                def _(sp):
                    for r in range(2):
                        sp.dma_start(a_row[r], adj_t[r]).then_inc(G["a_loaded"][r], 16)
                    with sp.Fori(1, T // 2) as i:
                        for par in range(2):
                            sp.wait_ge(G["deg_used"], i * 2 + (par - 1))
                            sp.dma_start(a_row[par], adj_t[bass.ds(i * 2 + par, 1)]
                                         .rearrange("a p j -> (a p) j")).then_inc(G["a_loaded"][par], 16)

                @block.gpsimd
                def _(pool):
                    pool.wait_ge(G["var_rdy"], 1)
                    nc.gpsimd.tensor_tensor(st_b[:, :], st_a[:, :], neg_half[:, :], ALU.pow).then_inc(G["pow_rdy"], 1)

                @block.tensor
                def _(pe):
                    for g in range(NC):
                        if g >= 2:
                            pe.wait_ge(G["x_ev"], g - 1)
                        for q in range(4):
                            last = nc.tensor.transpose(bank[g % 2][:, q * P:(q + 1) * P],
                                                       lin[:, (4 * g + q) * P:(4 * g + q + 1) * P], ident[:, :])
                        last.then_inc(G["x_tp"], 1)

                @block.vector
                def _(dve):
                    seq = Chain(dve, G["seq"])
                    for g in range(NC):
                        dve.wait_ge(G["x_tp"], g + 1)
                        nc.vector.tensor_copy(zs2[:, g * CH:(g + 1) * CH], bank[g % 2][:, :]).then_inc(G["x_ev"], 1)
                    with dve.Fori(0, T // 2) as i:
                        for par in range(2):
                            dve.wait_ge(G["a_loaded"][par], i * 16 + 16)
                            nc.vector.tensor_reduce(deg[:, bass.ds(i * 2 + par, 1)], a_row[par], AX_X, ALU.add)\
                                .then_inc(G["deg_used"], 1)
                    dve.wait_ge(G["deg_used"], T)
                    seq(nc.vector.tensor_scalar(deg[:, :], deg[:, :], 1.0, None, ALU.add))
                    nc.vector.tensor_scalar(st_a[:, :], deg[:, :], 1e-37, None, ALU.max).then_inc(G["var_rdy"], 1)
                    dve.wait_ge(G["pow_rdy"], 1)
                    seq(nc.vector.scalar_tensor_tensor(out=dinv[:, :], in0=deg[:, :], scalar=0.0, in1=st_b[:, :],
                                                       op0=ALU.is_gt, op1=ALU.mult))
                    seq(nc.vector.tensor_tensor(zs, zs, bc(dinv[:, :]), ALU.mult))
                    count.dve = seq.total + seq.n
            count.xtp, count.xev, count.var, count.loaded = NC, NC, 1, 8 * T

        def a_pass(G, count, turn, kind, rhs):
            base = turn * T
            w_base = base if kind == "sens" else 0
            loaded0 = count.loaded
            src = (lambda par: a_row[par]) if kind == "plain" else (lambda par: w_row)

            def tiles(eng, body):
                for r in range(2):
                    body(r, r, True)
                with eng.Fori(1, T // 2) as i:
                    for par in range(2):
                        body(i * 2 + par, par, False)

            with nc.Block() as block:
                @block.sync
                def _(sp):
                    def load(r, par, first):
                        if not first:
                            if kind == "plain":
                                sp.wait_ge(G["tp_done"], (r + (base - 1)) * 8)
                            else:
                                sp.wait_ge(G["w_rdy"], r + (w_base - 1))
                        if first:
                            sp.dma_start(a_row[par], adj_t[r]).then_inc(G["a_loaded"][par], 16)
                        else:
                            sp.dma_start(a_row[par], adj_t[bass.ds(r, 1)].rearrange("a p j -> (a p) j"))\
                                .then_inc(G["a_loaded"][par], 16)
                    tiles(sp, load)

                @block.tensor
                def _(pe):
                    def tile(r, par, first):
                        t = r + base

                        def products(g):
                            pe.wait_ge(G["at_ready"], t * 8 + (g + 1))
                            if g == 0 and not (first and base == 0):
                                pe.wait_ge(G["y_read"], t + (-1))
                            for q in range(4):
                                jb = 4 * g + q
                                last = nc.tensor.matmul(bank[2 + par][:, 0:D],
                                                        at_sb[:, g % AT_SLOTS, q * P:(q + 1) * P], rhs[:, jb, :],
                                                        start=(jb == 0), stop=(jb == T - 1))
                            last.then_inc(G["mm_done"], 1)

                        if kind == "plain":
                            pe.wait_ge(G["a_loaded"][par], (r - par) * 8 + (16 + loaded0))
                        else:
                            pe.wait_ge(G["w_rdy"], r + (w_base + 1))
                        for g in range(8):
                            if not (first and base == 0 and r == 0 and g < 2):
                                pe.wait_ge(G["at_ready"], t * 8 + (g - 1))
                            for q in range(4):
                                jb = 4 * g + q
                                last = nc.tensor.transpose(bank[g % 2][:, q * P:(q + 1) * P],
                                                           src(par)[:, jb * P:(jb + 1) * P], ident[:, :])
                            last.then_inc(G["tp_done"], 1)
                            if g >= 1:
                                products(g - 1)
                        products(7)
                    tiles(pe, tile)

                @block.scalar
                def _(act):
                    def tile(r, par, first):
                        t = r + base
                        if kind == "soft":
                            act.wait_ge(G["nmax_rdy"], r + 1)
                            nc.scalar.activation(w_row, w_row, ACT.Exp, bias=nmax[:, 1:2]).then_inc(G["exp_rdy"], 1)
                        if kind == "sens":
                            act.wait_ge(G["rec_rdy"], r + 1)
                            nc.scalar.activation(w_row, w_row, ACT.Square, bias=cs[:, 0:1]).then_inc(G["sens_rdy"], 1)
                            act.wait_ge(G["sens_rdy"], r * 2 + 1)
                            nc.scalar.activation(w_row, w_row, ACT.Exp, scale=-2.0).then_inc(G["sens_rdy"], 1)
                        for g in range(8):
                            act.wait_ge(G["tp_done"], t * 8 + (g + 1))
                            if not (first and base == 0 and r == 0 and g < AT_SLOTS):
                                act.wait_ge(G["mm_done"], t * 8 + (g + 1 - AT_SLOTS))
                            nc.scalar.copy(at_sb[:, g % AT_SLOTS, :], bank[g % 2][:, :]).then_inc(G["at_ready"], 1)
                    tiles(act, tile)

                @block.vector
                def _(dve):
                    seq = Chain(dve, G["seq"])
                    seq.total = seq.base = count.dve

                    def weights(r, par):
                        a = a_row[par]
                        dve.wait_ge(G["a_loaded"][par], (r - par) * 8 + (16 + loaded0))
                        if kind == "soft":
                            seq(nc.vector.tensor_tensor(w_row, a, s_bc, ALU.mult))
                            seq(nc.vector.tensor_scalar(tmp_row, a, 0.0, -FMAX, ALU.is_equal, ALU.mult))
                            seq(nc.vector.tensor_tensor(w_row, w_row, tmp_row, ALU.add))
                            seq(nc.vector.tensor_reduce(nmax[:, 0:1], w_row, AX_X, ALU.max))
                            nc.vector.tensor_scalar(nmax[:, 1:2], nmax[:, 0:1], -1.0, None, ALU.mult)\
                                .then_inc(G["nmax_rdy"], 1)
                            dve.wait_ge(G["exp_rdy"], r + 1)
                            nc.vector.scalar_tensor_tensor(out=w_row, in0=a, scalar=0.0, in1=w_row,
                                                           op0=ALU.not_equal, op1=ALU.mult,
                                                           accum_out=den1[:, 0:1]).then_inc(G["w_rdy"], 1)
                            dve.wait_ge(G["w_rdy"], r + (w_base + 1))
                            seq(nc.vector.tensor_copy(den[:, bass.ds(r, 1)], den1[:, 0:1]))
                        else:
                            seq(nc.vector.tensor_scalar(tmp_row, a, 0.0, None, ALU.is_equal))
                            seq(nc.vector.tensor_tensor(w_row, a, tmp_row, ALU.add))
                            nc.vector.reciprocal(w_row, w_row).then_inc(G["rec_rdy"], 1)
                            dve.wait_ge(G["sens_rdy"], r * 2 + 2)
                            seq(nc.vector.scalar_tensor_tensor(out=w_row, in0=tmp_row, scalar=0.0, in1=w_row,
                                                               op0=ALU.is_equal, op1=ALU.mult))
                            nc.vector.scalar_tensor_tensor(out=w_row, in0=a, scalar=1.0, in1=w_row,
                                                           op0=ALU.is_lt, op1=ALU.mult).then_inc(G["w_rdy"], 1)

                    def take(r, par):
                        t = r + base
                        dve.wait_ge(G["mm_done"], t * 8 + 8)
                        nc.vector.tensor_copy(ys2[:, bass.ds(r * D, D)], bank[2 + par][:, 0:D]).then_inc(G["y_read"], 1)

                    per_turn = {"plain": 0, "soft": 10, "sens": 6}[kind]
                    if kind == "sens":
                        seq(nc.vector.memset(cs[:, 0:1], -1.0))
                    with dve.Fori(0, T // 2) as i:
                        seq.enter(i, per_turn)
                        for par in range(2):
                            if kind != "plain":
                                weights(i * 2 + par, par)
                            take(i * 2 + par, par)
                        seq.leave(T // 2)
                    count.dve = seq.total + seq.n
            count.loaded += 8 * T

        def layer_end(G, count, layer):
            var0 = count.var
            with nc.Block() as block:
                @block.vector
                def _(dve):
                    seq = Chain(dve, G["seq"])
                    seq.total = seq.base = count.dve
                    if layer == 0:
                        seq(nc.vector.tensor_tensor(ys, ys, zs, ALU.add))
                        seq(nc.vector.tensor_tensor(ys, ys, bc(dinv[:, :]), ALU.mult))
                    if layer == 1:
                        seq(nc.vector.tensor_scalar(st_a[:, :], den[:, :], 0.0, None, ALU.is_le))
                        seq(nc.vector.tensor_tensor(den[:, :], den[:, :], st_a[:, :], ALU.add))
                        seq(nc.vector.reciprocal(st_a[:, :], den[:, :]))
                        seq(nc.vector.tensor_tensor(ys, ys, bc(st_a[:, :]), ALU.mult))
                    seq(nc.vector.tensor_tensor(xs[:, :, :], xs[:, :, :], ys, ALU.add))
                    seq(nc.vector.tensor_reduce(st_a[:, :], xs[:, :, :], AX_X, ALU.add))
                    seq(nc.vector.tensor_scalar(st_a[:, :], st_a[:, :], 1.0 / D, None, ALU.mult))
                    seq(nc.vector.tensor_tensor(xs[:, :, :], xs[:, :, :], bc(st_a[:, :]), ALU.subtract))
                    seq(nc.vector.tensor_tensor(ys, xs[:, :, :], xs[:, :, :], ALU.mult))
                    seq(nc.vector.tensor_reduce(st_a[:, :], ys, AX_X, ALU.add))
                    nc.vector.tensor_scalar(st_a[:, :], st_a[:, :], 1.0 / D, EPS, ALU.mult, ALU.add)\
                        .then_inc(G["var_rdy"], 1)
                    dve.wait_ge(G["pow_rdy"], var0 + 1)
                    seq(nc.vector.tensor_tensor(xs[:, :, :], xs[:, :, :], bc(st_b[:, :]), ALU.mult))
                    count.dve = seq.total + seq.n

                @block.gpsimd
                def _(pool):
                    pool.wait_ge(G["var_rdy"], var0 + 1)
                    nc.gpsimd.tensor_tensor(st_b[:, :], st_a[:, :], neg_half[:, :], ALU.pow).then_inc(G["pow_rdy"], 1)
            count.var += 1

        def transposed(G, count, what):
            src = ys if what == "product" else xs
            dst = ax_all if what == "product" else xT
            xtp0, xev0 = count.xtp, count.xev
            with nc.Block() as block:
                @block.sync
                def _(sp):
                    if what == "messages":
                        sp.dma_start(w2, W2).then_inc(w2_in, 16)
                        sp.dma_start(b2bc, B2.partition_broadcast(P)).then_inc(w2_in, 16)

                @block.vector
                def _(dve):
                    if what == "messages":
                        dve.wait_ge(w2_in, 32)
                    seq = Chain(dve, G["seq"])
                    seq.total = seq.base = count.dve
                    if what == "scores":
                        seq(nc.vector.tensor_copy(hv_rep, hvc[:, :].broadcast_to([P, P])))
                    count.dve = seq.total + seq.n
                    for g in range(NC):
                        dve.wait_ge(G["x_tp"], xtp0 + g + 1)
                        nc.vector.tensor_copy(dst[:, g * CH:(g + 1) * CH], bank[g % 2][:, :]).then_inc(G["x_ev"], 1)
                    for g in range(NC if what != "product" else 0):
                        dve.wait_ge(G["x_tp"], xtp0 + NC + g + 1)
                        if what == "scores":
                            ins = nc.vector.tensor_copy(s_bc[:, g * CH:(g + 1) * CH], bank[2 + g % 2][:, :])
                        else:
                            ins = nc.vector.tensor_tensor(zs[:, 4 * g:4 * g + 4, :], v4(bank[2 + g % 2][:, :]),
                                                          b2bc.unsqueeze(1).broadcast_to([P, 4, D]), ALU.add)
                        ins.then_inc(G["x_ev"], 1)

                @block.tensor
                def _(pe):
                    if what == "messages":
                        pe.wait_ge(w2_in, 32)
                    for g in range(NC):
                        if g >= 2:
                            pe.wait_ge(G["x_ev"], xev0 + g - 1)
                        for q in range(4):
                            last = nc.tensor.transpose(bank[g % 2][:, q * P:(q + 1) * P], src[:, 4 * g + q, :],
                                                       ident[:, :])
                        last.then_inc(G["x_tp"], 1)
                    for g in range(NC if what != "product" else 0):
                        pe.wait_ge(G["x_ev"], xev0 + (NC if g < 2 else NC + g - 1))
                        if what == "scores":
                            last = nc.tensor.matmul(bank[2 + g % 2][:, :], hv_rep, xT[:, g * CH:(g + 1) * CH],
                                                    start=True, stop=True)
                        else:
                            for q in range(4):
                                r = 4 * g + q
                                last = nc.tensor.matmul(bank[2 + g % 2][:, q * P:(q + 1) * P],
                                                        xT[:, r * P:(r + 1) * P], w2, start=True, stop=True)
                        last.then_inc(G["x_tp"], 1)
            both = NC if what == "product" else 2 * NC
            count.xtp += both
            count.xev += both

        names = ("ax_ps ax_sb h_ps h_rdy hvar hrstd hn hT_ps hT_sb xz_ps xz_sb conv_rdy carried u_rdy dbc_ps "
                 "dtr_rdy bc_rdy dt_ps sp_abs sp_exp sp_ln dt_rdy dtu_rdy b_ps b_rdy c_ps cs_rdy dA_rdy dBu_rdy scanned kept "
                 "prod_v prod_p summed yz_rdy o_ps o_read ovar orstd o_rdy o_out osb_free A_rdy").split()
        m = {n: sem("m_" + n) for n in names}

        def region(k):
            return [arena[:, k * N + i * CH:k * N + (i + 1) * CH] for i in range(8)]

        at = [0]

        def cut(n, dt=F32, parts=P):
            v = z2f[0:parts, at[0]:at[0] + n]
            at[0] += n
            return v

        hbuf, hT, e0, e1, ln1 = (cut(CH) for _ in range(5))
        wk = [[cut(CH) for _ in range(3)] for _ in range(NH)]
        xcp = [cut(CH + K - 1), qf[:, CH:2 * CH + K - 1]]
        assert at[0] <= T * ZW // 2
        osb = qf[:, 0:CH]
        tmp = osb
        hmv = mvs
        xs2 = xs[:, :, :].rearrange("p t d -> p (t d)")

        def mamba(m, fused):

            def pool_n(c):
                return POOL_C if fused and c >= 1 else ()

            def before(c, n, on_pool):
                if not fused:
                    return 0 if on_pool else c * (NH * S) + n * NH
                total = 0
                for k in range(c + 1):
                    for j in range(S if k < c else n):
                        total += NH * ((j in pool_n(k)) == on_pool)
                return total

            def at_(c, per, k):
                return c * per + k

            def own(c):
                v = region(c if fused else 0)
                return dict(u=v[0:2], dt=v[2:4], zs=v[4:6], ax=v[7], ln=[v[6], ln1], dtr=v[6][6 * S:6 * S + R, :],
                            dtu=[v[6], z1s[c % 2 if fused else 0]], bc3=v[7][0:96, 0:CH // 2].bitcast(BF16))

            z1s = [z1f[:, i * CH:(i + 1) * CH] for i in range(12)]
            dA, b_sb, c_sb, yz = [z1s[2:4], z1s[4:6]], z1s[6:8], z1s[8:10], z1s[10:12]
            ev = [e0, e1]

            def place(c, n):
                if not fused:
                    return n % 3
                if c == 0:
                    return (0, 1, 2, 5)[n % 4]
                if c == 1:
                    return (3, 0, 1, 2)[n % 4]
                return (4, 3, 0, 1, 2)[((c - 2) * S + n) % 5]

            def slot(c, h, n):
                return (wk[h] + [(hbuf, hT)[h], ev[h], yz[h]])[place(c, n)]

            def before_in(c, n, where):
                k, j = c, n - 1
                while j >= 0 or (fused and k > 0):
                    if j < 0:
                        k, j = k - 1, S - 1
                    if where(k, j) == where(c, n):
                        return k, j
                    j -= 1
                return None

            def summing(c, turn):
                n = turn - 1
                return [k for k in (n, n - 2) if 0 <= k < S and (k in pool_n(c)) == (k < n)]

            def summed(c, n):
                if not fused:
                    return at_(c, NH * S, n * NH)
                order = [k for turn in range(S + 1) for k in summing(c, turn)]
                return c * NH * S + order.index(n) * NH


            def pe_prep(pe, c, step):
                o = own(c)
                if step == 1:
                    pe.wait_ge(m["ax_sb"], c + 1)
                    if fused and c:
                        pe.wait_ge(m["hT_sb"], c)
                    for q in range(4):
                        nc.tensor.matmul(bank[6][:, q * P:(q + 1) * P], o["ax"][:, q * P:(q + 1) * P], gw[:, :],
                                         start=True, stop=False)
                        last = nc.tensor.matmul(bank[6][:, q * P:(q + 1) * P], ones_f[0:1, :], gbbc[0:1, :],
                                                start=False, stop=True)
                    last.then_inc(m["h_ps"], 1)
                elif step == 2:
                    pe.wait_ge(m["hn"], c + 1)
                    for q in range(4):
                        last = nc.tensor.transpose(bank[6][:, q * P:(q + 1) * P], hbuf[:, q * P:(q + 1) * P],
                                                   ident[:, :])
                    last.then_inc(m["hT_ps"], 1)
                elif step in (3, 4):
                    if step == 3:
                        pe.wait_ge(m["hT_sb"], c + 1)
                        if fused and c:
                            pe.wait_ge(m["sp_abs"], c * 2 * NH)
                    for i, b in enumerate((5, 7)):
                        k = 2 * (step - 3) + i
                        if step == 4:
                            pe.wait_ge(m["xz_sb"], at_(c, 4, i + 1))
                        nc.tensor.matmul(bank[b][:, :], win[:, k * P:(k + 1) * P], hT, start=True, stop=True)\
                            .then_inc(m["xz_ps"], 1)
                elif step == 5:
                    pe.wait_ge(m["u_rdy"], at_(c, NH, NH))
                    for h in range(NH):
                        last = nc.tensor.matmul(bank[5][0:6 * S + R, :], wxp3[:, h, :], o["u"][h],
                                                start=(h == 0), stop=(h == NH - 1))
                    last.then_inc(m["dbc_ps"], 1)
                else:
                    pe.wait_ge(m["dtr_rdy"], c + 1)
                    pe.wait_ge(m["bc_rdy"], c + 1)
                    for h, b in enumerate((5, 7)):
                        nc.tensor.matmul(bank[b][:, :], wdt[:, h * P:(h + 1) * P], o["dtr"], start=True, stop=True)\
                            .then_inc(m["dt_ps"], 1)

            def b_bank(c, n):
                return (2, 6)[n % 2] if fused and c >= 1 else 2

            def c_bank(c, n):
                return (7, 3, 4)[((c - 2) * S + n) % 3] if fused and c >= 2 else 3 + n % 2

            def pe_b(pe, c, n):
                if n == 0:
                    pe.wait_ge(m["bc_rdy"], c + 1)
                if last := before_in(c, n, b_bank):
                    pe.wait_ge(m["b_rdy"], at_(last[0], S, last[1] + 1))
                nc.tensor.matmul(bank[b_bank(c, n)][:, :], sel[:, n:n + 1].broadcast_to([96, P]), own(c)["bc3"],
                                 start=True, stop=True).then_inc(m["b_ps"], 1)

            def pe_c(pe, c, n):
                if last := before_in(c, n, c_bank):
                    k, j = last
                    if j in pool_n(k):
                        pe.wait_ge(m["cs_rdy"], before(k, j, True) // NH + 1)
                    else:
                        pe.wait_ge(m["prod_v"], before(k, j, False) + NH)
                nc.tensor.matmul(bank[c_bank(c, n)][:, :], sel[:, S + n:S + n + 1].broadcast_to([96, P]),
                                 own(c)["bc3"], start=True, stop=True).then_inc(m["c_ps"], 1)

            def pe_sum(pe, c, n):
                if n == 0 and fused and c:
                    pe.wait_ge(m["yz_rdy"], c * NH)
                for h in range(NH):
                    if n in pool_n(c):
                        pe.wait_ge(m["prod_p"], before(c, n, True) + (h + 1))
                    else:
                        pe.wait_ge(m["prod_v"], before(c, n, False) + (h + 1))
                    nc.tensor.matmul(bank[h][:, :], ident[:, :], slot(c, h, n), start=(n == 0),
                                     stop=(n == S - 1)).then_inc(m["summed"], 1)

            def pe_out(pe, c):
                pe.wait_ge(m["yz_rdy"], at_(c, NH, NH))
                for q in range(4):
                    for h in range(NH):
                        last = nc.tensor.matmul(bank[5][:, q * P:(q + 1) * P], yz[h][:, q * P:(q + 1) * P],
                                                wout[:, h, :], start=(h == 0), stop=(h == NH - 1))
                last.then_inc(m["o_ps"], 1)

            def act_prep(act, c, step):
                o = own(c)
                if step == 0:
                    act.wait_ge(m["ax_ps"], c + 1)
                    nc.scalar.copy(o["ax"], l3_bank(c)[:, :]).then_inc(m["ax_sb"], 1)
                elif step == 1:
                    act.wait_ge(m["h_ps"], c + 1)
                    nc.scalar.activation(hbuf, bank[6][:, :], ACT.Relu).then_inc(m["h_rdy"], 1)
                elif step == 2:
                    act.wait_ge(m["hT_ps"], c + 1)
                    nc.scalar.activation(hT, bank[6][:, :], ACT.Identity, bias=lnb[:, :], scale=lng[:, :])\
                        .then_inc(m["hT_sb"], 1)
                elif step == 3:
                    act.wait_ge(m["carried"], at_(c, NH, NH))
                    for k, b in enumerate((5, 7)):
                        act.wait_ge(m["xz_ps"], at_(c, 4, k + 1))
                        nc.scalar.copy(xcp[k][:, K - 1:], bank[b][:, :]).then_inc(m["xz_sb"], 1)
                elif step == 4:
                    for k, b in enumerate((5, 7)):
                        act.wait_ge(m["xz_ps"], at_(c, 4, k + 3))
                        nc.scalar.activation(o["zs"][k], bank[b][:, :], ACT.Silu).then_inc(m["xz_sb"], 1)
                elif step == 5:
                    for h in range(NH):
                        act.wait_ge(m["conv_rdy"], at_(c, NH, h + 1))
                        nc.scalar.activation(o["u"][h], o["u"][h], ACT.Silu).then_inc(m["u_rdy"], 1)
                elif step == 6:
                    act.wait_ge(m["dbc_ps"], c + 1)
                    nc.scalar.copy(o["dtr"], bank[5][6 * S:6 * S + R, :]).then_inc(m["dtr_rdy"], 1)
                elif step == 7:
                    if fused and c:
                        act.wait_ge(m["dt_rdy"], c * NH)
                    for h, b in enumerate((5, 7)):
                        act.wait_ge(m["dt_ps"], at_(c, NH, h + 1))
                        nc.scalar.activation(o["dt"][h], bank[b][:, :], ACT.Relu, bias=bdt[:, h:h + 1])\
                            .then_inc(m["sp_abs"], 1)
                        nc.scalar.activation(ev[h], bank[b][:, :], ACT.Abs, bias=bdt[:, h:h + 1])\
                            .then_inc(m["sp_abs"], 1)
                elif step == 8:
                    for h in range(NH):
                        act.wait_ge(m["sp_abs"], at_(c, 2 * NH, 2 * h + 2))
                        nc.scalar.activation(ev[h], ev[h], ACT.Exp, scale=-1.0).then_inc(m["sp_exp"], 1)
                else:
                    for h in range(NH):
                        act.wait_ge(m["sp_exp"], at_(c, NH, h + 1))
                        nc.scalar.activation(o["ln"][h], ev[h], ACT.Ln, bias=1.0).then_inc(m["sp_ln"], 1)

            def act_main(act, c, n):
                o = own(c)
                if n == 0:
                    act.wait_ge(m["dt_rdy"], at_(c, NH, NH))
                    if fused and c == 0:
                        act.wait_ge(m["ax_ps"], NC)
                act.wait_ge(m["b_ps"], at_(c, S, n + 1))
                if n >= 2:
                    act.wait_ge(m["dBu_rdy"], at_(c, NH * S, (n - 1) * NH))
                elif fused and c:
                    act.wait_ge(m["dBu_rdy"], c * NH * S + (n - 1) * NH)
                nc.scalar.copy(b_sb[n % 2], bank[b_bank(c, n)][:, :]).then_inc(m["b_rdy"], 1)
                if n - 1 in pool_n(c):
                    act.wait_ge(m["c_ps"], at_(c, S, n))
                    j = before(c, n - 1, True) // NH
                    if j >= 2:
                        act.wait_ge(m["prod_p"], (j - 1) * NH)
                    nc.scalar.copy(c_sb[j % 2], bank[c_bank(c, n - 1)][:, :]).then_inc(m["cs_rdy"], 1)
                for h in range(NH):
                    if n >= 2:
                        act.wait_ge(m["scanned"], at_(c, NH * S, (n - 2) * NH + h + 1))
                    elif fused and c:
                        act.wait_ge(m["scanned"], c * NH * S + (n - 2) * NH + h + 1)
                    nc.scalar.activation(dA[h][n % 2], o["dt"][h], ACT.Exp, scale=Aneg[:, h, n:n + 1])\
                        .then_inc(m["dA_rdy"], 1)

            def pool_prep(pool, c, step):
                o = own(c)
                if step == 1:
                    pool.wait_ge(m["hvar"], c + 1)
                    nc.gpsimd.tensor_tensor(mst[:, 1, :], mst[:, 0, :], neg_half[:, 0:4], ALU.pow)\
                        .then_inc(m["hrstd"], 1)
                else:
                    h = step - 2
                    if fused and c == 0:
                        pool.wait_ge(m["ax_ps"], NC)
                    pool.wait_ge(m["dt_rdy"], at_(c, NH, h + 1))
                    if fused and c >= 2 and h:
                        pool.wait_ge(m["dBu_rdy"], (c - 1) * NH * S)
                    nc.gpsimd.tensor_tensor(o["dtu"][h], o["dt"][h], o["u"][h], ALU.mult).then_inc(m["dtu_rdy"], 1)

            def pool_c(pool, c, n):
                j = before(c, n, True) // NH
                pool.wait_ge(m["cs_rdy"], j + 1)
                for h in range(NH):
                    pool.wait_ge(m["kept"], at_(c, NH * S, n * NH + h + 1))
                    w = slot(c, h, n)
                    nc.gpsimd.tensor_tensor(w, w, c_sb[j % 2], ALU.mult).then_inc(m["prod_p"], 1)

            def pool_main(pool, c, n):
                if n == 0:
                    pool.wait_ge(m["dtu_rdy"], at_(c, NH, NH))
                o = own(c)
                pool.wait_ge(m["b_rdy"], at_(c, S, n + 1))
                for h in range(NH):
                    if last := before_in(c, n, place):
                        pool.wait_ge(m["summed"], summed(*last) + (h + 1))
                    nc.gpsimd.tensor_tensor(slot(c, h, n), o["dtu"][h], b_sb[n % 2], ALU.mult)\
                        .then_inc(m["dBu_rdy"], 1)
                if n >= 2 and n - 2 in pool_n(c):
                    pool_c(pool, c, n - 2)

            def pool_out(pool, c):
                pool.wait_ge(m["ovar"], c + 1)
                nc.gpsimd.tensor_tensor(mst[:, 3, :], mst[:, 2, :], neg_half[:, 0:4], ALU.pow).then_inc(m["orstd"], 1)

            def stats(seq, buf, mv4, k, ready):
                if fused:
                    for q in range(4):
                        seq(nc.vector.bn_stats(bn[:, q, :], buf[:, q * D:(q + 1) * D]))
                        seq(nc.vector.bn_aggr(mv4[:, q, :], bn[:, q, :]))
                    nc.vector.tensor_scalar(mst[:, k, :], mv4[:, :, 1], EPS, None, ALU.add).then_inc(ready, 1)
                    return
                seq(nc.vector.tensor_reduce(mst[:, k, :], v4(buf), AX_X, ALU.add))
                seq(nc.vector.tensor_scalar(mst[:, k, :], mst[:, k, :], 1.0 / D, None, ALU.mult))
                seq(nc.vector.tensor_tensor(v4(buf), v4(buf), bc(mst[:, k, :], 4), ALU.subtract))
                seq(nc.vector.tensor_tensor(hT, buf, buf, ALU.mult))
                seq(nc.vector.tensor_reduce(mst[:, k, :], v4(hT), AX_X, ALU.add))
                nc.vector.tensor_scalar(mst[:, k, :], mst[:, k, :], 1.0 / D, EPS, ALU.mult, ALU.add)\
                    .then_inc(ready, 1)

            def normed(seq, buf, mv4, k, done):
                if not fused:
                    nc.vector.tensor_tensor(v4(buf), v4(buf), bc(mst[:, k + 1, :], 4), ALU.mult).then_inc(done, 1)
                    return
                for q in range(4):
                    ins = nc.vector.tensor_scalar(buf[:, q * D:(q + 1) * D], buf[:, q * D:(q + 1) * D],
                                                  mv4[:, q, 0:1], mst[:, k + 1, q:q + 1], ALU.subtract, ALU.mult)
                    if q < 3:
                        ins.then_inc(mam_seq, 1)
                        seq.n += 1
                    else:
                        ins.then_inc(done, 1)

            def dve_prep(dve, seq, c, step):
                o = own(c)
                if step == 1:
                    dve.wait_ge(m["h_rdy"], c + 1)
                    stats(seq, hbuf, hmv, 0, m["hvar"])
                elif step == 2:
                    dve.wait_ge(m["hrstd"], c + 1)
                    normed(seq, hbuf, hmv, 0, m["hn"])
                elif step in (3, 4):
                    h = step - 3
                    dve.wait_ge(m["xz_sb"], at_(c, 4, h + 1))
                    cv = o["u"][h]
                    seq(nc.vector.tensor_scalar(cv, xcp[h][:, 0:CH], cw[:, h, 0:1], cb[:, h:h + 1], ALU.mult, ALU.add))
                    for k in range(1, K):
                        ins = nc.vector.scalar_tensor_tensor(out=cv, in0=xcp[h][:, k:k + CH], scalar=cw[:, h, k:k + 1],
                                                             in1=cv, op0=ALU.mult, op1=ALU.add)
                        if k < K - 1:
                            seq(ins)
                        else:
                            ins.then_inc(m["conv_rdy"], 1)
                    if h == NH - 1:
                        dve.wait_ge(m["conv_rdy"], at_(c, NH, NH))
                        for x in xcp:
                            nc.vector.tensor_copy(x[:, 0:K - 1], x[:, CH:CH + K - 1]).then_inc(m["carried"], 1)
                elif step == 5:
                    b3, rest = o["bc3"], tmp[0:96, :]
                    dve.wait_ge(m["dbc_ps"], c + 1)
                    seq(nc.vector.tensor_copy(b3, bank[5][0:96, :]))
                    seq(nc.vector.tensor_tensor(rest, bank[5][0:96, :], b3, ALU.subtract))
                    seq(nc.vector.tensor_copy(b3[32:64, :], rest[32:64, :]))
                    seq(nc.vector.tensor_copy(b3[64:96, :], rest[64:96, :]))
                    seq(nc.vector.tensor_tensor(rest[64:96, :], rest[64:96, :], b3[64:96, :], ALU.subtract))
                    nc.vector.tensor_copy(b3[64:96, :], rest[64:96, :]).then_inc(m["bc_rdy"], 1)
                else:
                    h = step - 6
                    dt = o["dt"][h]
                    if h == 0:
                        dve.wait_ge(m["bc_rdy"], c + 1)
                    else:
                        dve.wait_ge(m["dt_rdy"], at_(c, NH, h))
                    dve.wait_ge(m["sp_ln"], at_(c, NH, h + 1))
                    seq(nc.vector.tensor_scalar(tmp, ev[h], 1.0, -1.0, ALU.add, ALU.add))
                    nc.vector.tensor_tensor(dt, dt, o["ln"][h], ALU.add).then_inc(mam_seq, 1)
                    seq.n += 1
                    seq(nc.vector.tensor_tensor(tmp, ev[h], tmp, ALU.subtract))
                    nc.vector.tensor_tensor(dt, dt, tmp, ALU.add).then_inc(m["dt_rdy"], 1)

            def dve_main(dve, c, n):
                for h in range(NH):
                    dve.wait_ge(m["dA_rdy"], at_(c, NH * S, n * NH + h + 1))
                    dve.wait_ge(m["dBu_rdy"], at_(c, NH * S, n * NH + h + 1))
                    w = slot(c, h, n)
                    nc.vector.tensor_tensor_scan(w, dA[h][n % 2], w, state[:, h, n:n + 1], ALU.mult, ALU.add)\
                        .then_inc(m["scanned"], 1)
                for h in range(NH):
                    dve.wait_ge(m["scanned"], at_(c, NH * S, n * NH + h + 1))
                    w = slot(c, h, n)
                    nc.vector.tensor_copy(state[:, h, n:n + 1], w[:, CH - 1:CH]).then_inc(m["kept"], 1)
                if n not in pool_n(c):
                    dve.wait_ge(m["c_ps"], at_(c, S, n + 1))
                    for h in range(NH):
                        w = slot(c, h, n)
                        dve.wait_ge(m["kept"], at_(c, NH * S, n * NH + h + 1))
                        nc.vector.tensor_tensor(w, w, bank[c_bank(c, n)][:, :], ALU.mult).then_inc(m["prod_v"], 1)

            def dve_gate(dve, seq, c):
                o = own(c)
                for h in range(NH):
                    dve.wait_ge(m["summed"], at_(c, NH * S, (S - 1) * NH + h + 1))
                    seq(nc.vector.scalar_tensor_tensor(out=yz[h], in0=o["u"][h], scalar=dsk[:, h:h + 1],
                                                       in1=bank[h][:, :], op0=ALU.mult, op1=ALU.add))
                    nc.vector.tensor_tensor(yz[h], yz[h], o["zs"][h], ALU.mult).then_inc(m["yz_rdy"], 1)

            def dve_out(dve, seq, c, step):
                if step == 1:
                    dve.wait_ge(m["o_ps"], c + 1)
                    dve.wait_ge(m["osb_free"], c + 1)
                    sl = slice(c * CH, (c + 1) * CH) if fused else bass.ds(c * CH, CH)
                    nc.vector.tensor_tensor(osb, bank[5][:, :], xs2[:, sl], ALU.add).then_inc(m["o_read"], 1)
                    dve.wait_ge(m["o_read"], c + 1)
                    stats(seq, osb, omv4, 2, m["ovar"])
                else:
                    dve.wait_ge(m["orstd"], c + 1)
                    normed(seq, osb, omv4, 2, m["o_rdy"])

            out_c = out.rearrange("(c q p) d -> c p q d", q=4, p=P)

            with nc.Block() as block:
                @block.sync
                def _(sp):
                    sp.sem_inc(m["osb_free"], 1)

                    def store(c):
                        sp.wait_ge(m["o_rdy"], c + 1)
                        dst = out_c[c] if fused else out_c[bass.ds(c, 1)].rearrange("a p q d -> (a p) q d")
                        sp.dma_start(dst, v4(osb)).then_inc(m["o_out"], 16)
                        sp.wait_ge(m["o_out"], at_(c, 16, 16))
                        sp.sem_inc(m["osb_free"], 1)
                    if fused:
                        for c in range(NC):
                            store(c)
                    else:
                        with sp.Fori(0, NC) as c:
                            store(c)
                    sp.wait_ge(m["o_out"], 16 * NC)

                @block.tensor
                def _(pe):
                    if not fused:
                        with pe.Fori(0, NC) as c:
                            for step in range(1, 7):
                                pe_prep(pe, c, step)
                            pe_b(pe, c, 0)
                            pe_c(pe, c, 0)
                            for n in range(S):
                                if n + 1 < S:
                                    pe_b(pe, c, n + 1)
                                if n >= 1:
                                    pe_sum(pe, c, n - 1)
                                if n + 1 < S:
                                    pe_c(pe, c, n + 1)
                            pe_sum(pe, c, S - 1)
                            pe_out(pe, c)
                        return
                    for t in range(TURNS):
                        per = 3 * T // PER
                        k, lo = t // PER, t % PER * per
                        if lo == 0 and k >= 2:
                            pe.wait_ge(m["ax_sb"], k - 1)
                        if k == 0:
                            lo = max(lo, 3 * L3_EARLY)
                        if lo < (t % PER + 1) * per:
                            last = pe_l3(k, lo, (t % PER + 1) * per)
                        if t % PER == PER - 1:
                            last.then_inc(m["ax_ps"], 1)
                        for k, step in tasks("PE", t - TURNS):
                            pe_prep(pe, k, step)
                    pe_b(pe, 0, 0)
                    pe_b(pe, 0, 1)
                    pe_c(pe, 0, 0)
                    for t in range(NC * S):
                        c, n = t // S, t % S
                        if t + 2 < NC * S:
                            pe_b(pe, (t + 2) // S, (t + 2) % S)
                        if t + 1 < NC * S:
                            pe_c(pe, (t + 1) // S, (t + 1) % S)
                        if n == 0 and c:
                            for k in summing(c - 1, S):
                                pe_sum(pe, c - 1, k)
                        for k in summing(c, n):
                            pe_sum(pe, c, k)
                        if n == 2 and c:
                            pe_out(pe, c - 1)
                        for k, step in tasks("PE", t):
                            pe_prep(pe, k, step)
                    for k in summing(NC - 1, S):
                        pe_sum(pe, NC - 1, k)
                    pe_out(pe, NC - 1)

                @block.scalar
                def _(act):
                    nc.scalar.activation(Aneg[:, :, :], alog[:, :, :], ACT.Exp).then_inc(m["A_rdy"], 1)
                    act.wait_ge(m["A_rdy"], 1)
                    nc.scalar.mul(Aneg[:, :, :], Aneg[:, :, :], -1.0).then_inc(m["A_rdy"], 1)
                    act.wait_ge(m["A_rdy"], 2)
                    if not fused:
                        with act.Fori(0, NC) as c:
                            act.wait_ge(m["osb_free"], c + 1)
                            nc.scalar.copy(own(c)["ax"], ax_all[:, bass.ds(c * CH, CH)]).then_inc(m["ax_sb"], 1)
                            for step in range(1, 10):
                                act_prep(act, c, step)
                            for n in range(S):
                                act_main(act, c, n)
                        return
                    for t in range(-TURNS, NC * S):
                        if t >= 0:
                            act_main(act, t // S, t % S)
                        for k, step in tasks("ACT", t):
                            act_prep(act, k, step)

                @block.gpsimd
                def _(pool):
                    if not fused:
                        with pool.Fori(0, NC) as c:
                            for step in range(1, 4):
                                pool_prep(pool, c, step)
                            for n in range(S):
                                pool_main(pool, c, n)
                            pool_out(pool, c)
                        return
                    for t in range(-TURNS, NC * S):
                        c, n = t // S, t % S
                        if t >= 0:
                            pool_main(pool, c, n)
                            if n == 5 and c:
                                pool_out(pool, c - 1)
                            if n in DTU_AT and c + 1 < NC:
                                pool_prep(pool, c + 1, DTU_AT[n])
                        for k, step in tasks("POOL", t):
                            pool_prep(pool, k, step)
                        if t == -1:
                            pool_prep(pool, 0, 2)
                            pool_prep(pool, 0, 3)
                    pool_out(pool, NC - 1)

                @block.vector
                def _(dve):
                    seq = Chain(dve, mam_seq)
                    for x in xcp:
                        nc.vector.memset(x[:, 0:K - 1], 0.0).then_inc(m["carried"], 1)
                    dve.wait_ge(m["carried"], NH)
                    if not fused:
                        with dve.Fori(0, NC) as c:
                            seq.enter(c, 29)
                            dve.wait_ge(m["osb_free"], c + 1)
                            for step in range(1, 8):
                                dve_prep(dve, seq, c, step)
                            for n in range(S):
                                dve_main(dve, c, n)
                            dve_gate(dve, seq, c)
                            for step in (1, 2):
                                dve_out(dve, seq, c, step)
                            seq.leave(NC)
                        return
                    for t in range(-TURNS, NC * S):
                        c, n = t // S, t % S
                        if t >= 0:
                            dve_main(dve, c, n)
                            if c and n == 0:
                                dve_gate(dve, seq, c - 1)
                            elif c and n in (3, 6):
                                dve_out(dve, seq, c - 1, n // 3)
                        for k, step in tasks("DVE", t):
                            dve_prep(dve, seq, k, step)
                    dve_gate(dve, seq, NC - 1)
                    for step in (1, 2):
                        dve_out(dve, seq, NC - 1, step)

        PER = 6
        TURNS = PER * NC
        STEPS = {"PE": [(1, 1, 1), (2, 3, 5), (3, 4, 7), (4, 5, 8), (5, 7, 12), (6, 8, 14)],
                 "ACT": [(0, 0, 0), (1, 1, 1), (2, 3, 6), (3, 4, 8), (4, 5, 9), (5, 6, 11), (6, 7, 13), (7, 8, 15),
                         (8, 8, 16), (9, 8, 17)],
                 "POOL": [(1, 1, 3)],
                 "DVE": [(1, 1, 2), (2, 2, 4), (3, 4, 9), (4, 5, 10), (5, 7, 13), (6, 9, 18), (7, 9, 19)]}
        AHEAD = {"PE": 1, "ACT": 2, "POOL": 1, "DVE": 0}
        POOL_C = (8,)
        DTU_AT = {8: 2, 12: 3}

        def tasks(engine, t):
            found = []
            for k in range(NC):
                end = (k + 1) * PER - 1 - TURNS
                left = [rank for steps in STEPS.values() for _, after, rank in steps if end + after >= 0]
                for step, after, rank in STEPS[engine]:
                    turn = end + after
                    if turn >= 0:
                        turn = rank - min(left) + AHEAD[engine]
                    if turn == t:
                        found.append((k, step))
            return found

        def enter_branch():
            for engine in (nc.sync, nc.scalar, nc.vector, nc.gpsimd, nc.tensor):
                engine.nop()

        binary = nc.values_load(flag[0:1, 0:1], min_val=0, max_val=1)
        with nc.If(binary == 1):
            enter_branch()
            fast_layer0()
        with nc.Else():
            enter_branch()
            G, count = general_sems("g")
            general_start(G, count)
            a_pass(G, count, 0, "plain", zs)
            layer_end(G, count, 0)
        near = nc.values_load(flag[0:1, 1:2], min_val=0, max_val=1)
        with nc.If(near == 1):
            enter_branch()
            fast_rest()
            mamba(m, True)
        with nc.Else():
            enter_branch()
            G, count = general_sems("h")
            transposed(G, count, "scores")
            a_pass(G, count, 0, "soft", xs)
            layer_end(G, count, 1)
            transposed(G, count, "messages")
            a_pass(G, count, 1, "sens", zs)
            layer_end(G, count, 2)
            a_pass(G, count, 2, "plain", xs)
            transposed(G, count, "product")
            mamba(m, False)

_INS = ['x', 'adj', 'L0_gnn_W', 'L0_gnn_b', 'L1_gnn_H_v', 'L2_gnn_W', 'L2_gnn_B', 'L3_gnn_gcn_w', 'L3_gnn_gcn_b',
        'L3_gnn_ln_g', 'L3_gnn_ln_b', 'L3_gnn_w_in', 'L3_gnn_conv_w', 'L3_gnn_conv_b', 'L3_gnn_w_xp', 'L3_gnn_w_dt',
        'L3_gnn_b_dt', 'L3_gnn_A_log', 'L3_gnn_D_skip', 'L3_gnn_w_out']
_OUTS = [((N, D), 'float32')]


def kernel(**inputs):
    import numpy as _np
    import concourse.bacc as _bacc
    from concourse import mybir as _mybir
    from concourse.bass_utils import run_bass_kernel_spmd as _run

    nc = _bacc.Bacc("TRN2", target_bir_lowering=False, num_devices=1)
    arrays, args = {}, []
    for name in _INS:
        a = _np.ascontiguousarray(inputs[name])
        arrays[f"in_{name}_dram"] = a
        args.append(nc.dram_tensor(f"in_{name}_dram", a.shape, _mybir.dt.from_np(a.dtype), kind="ExternalInput").ap())
    for i, (shape, dtype) in enumerate(_OUTS):
        dt = _mybir.dt.from_np(_np.dtype(dtype))
        args.append(nc.dram_tensor(f"out_{i}_dram", shape, dt, kind="ExternalOutput").ap())
    build(nc, *args)
    r = _run(nc, [arrays], core_ids=[0])
    got = tuple(r.results[0][f"out_{i}_dram"] for i in range(len(_OUTS)))
    return got[0]
```
